# Optimizing a Trainium2 kernel written in Bass

```python
import numpy as np
import jax
import jax.numpy as jnp

def _softmax(x, axis=-1):
    return jax.nn.softmax(x, axis=axis)

def _gelu(x):
    return jax.nn.gelu(x, approximate=True)

def _silu(x):
    return jax.nn.silu(x)

def _sigmoid(x):
    return jax.nn.sigmoid(x)

def _layernorm(x, axis=-1, eps=1e-05):
    m = jnp.mean(x, axis=axis, keepdims=True)
    v = jnp.var(x, axis=axis, keepdims=True)
    return (x - m) / jnp.sqrt(v + eps)

def _scatter_add(tgt, idx, src, axis=0):
    return tgt.at[idx].add(src)

def _segment_sum(src, seg, n):
    return jax.ops.segment_sum(src, seg, n)
kernel_name = 'mk_adaln_attn_ffn_d2_seqx_r4_e9ee0b'

def setup_inputs(seed: int=0):
    np.random.seed(seed)
    _w = jnp.asarray

    def _rec_inputs():
        import jax
        import jax.numpy as jnp
        _rk = jax.random.key(seed)
        x = -0.0003929 + 0.9999 * jax.random.normal(jax.random.fold_in(_rk, 1), (32, 64, 256), jnp.float32)
        _lenS = 64 - jax.random.randint(jax.random.fold_in(_rk, 7), (32,), 0, max(1, 64 // 4) + 1, jnp.int32)
        _lenS2 = 64 - jax.random.randint(jax.random.fold_in(_rk, 8), (32,), 0, max(1, 64 // 4) + 1, jnp.int32)
        itok_B_0_7 = jax.random.randint(jax.random.fold_in(_rk, 11), (32,), 0, 8, jnp.int32)
        itok_B_0_2 = jax.random.randint(jax.random.fold_in(_rk, 12), (32,), 0, 3, jnp.int32)
        itok_B_0_8 = jax.random.randint(jax.random.fold_in(_rk, 13), (32,), 0, 9, jnp.int32)
        return (x, itok_B_0_7, itok_B_0_2, itok_B_0_8)
    x, itok_B_0_7, itok_B_0_2, itok_B_0_8 = _rec_inputs()

    def _L0_cond_setup():
        import jax, jax.numpy as jnp
        import numpy as np
        S, O, H = (8, 256, 256)
        B, N = (32, 128)
        key = jax.random.key(seed)
        k1, k2, k3, k4 = jax.random.split(key, 4)
        x = jax.random.normal(k1, (B, N, H), dtype=jnp.float32)
        subject_id = jax.random.randint(k2, (B,), 0, S)
        wbound = jnp.sqrt(2.0 / 6.0) * jnp.sqrt(3.0 / H)
        weight = jax.random.uniform(k3, (S, O, H), minval=-wbound, maxval=wbound, dtype=jnp.float32)
        bbound = 1.0 / jnp.sqrt(H)
        bias = jax.random.uniform(k4, (S, O), minval=-bbound, maxval=bbound, dtype=jnp.float32)
        return {'x': x, 'subject_id': subject_id, 'weight': weight, 'bias': bias}
    _L0_cond_all = _L0_cond_setup()
    _L0_cond_in = {k: v for k, v in _L0_cond_all.items() if k in ('weight', 'bias')}
    del _L0_cond_all

    def _L0_attn_setup():
        import jax, jax.numpy as jnp
        import numpy as np
        B, S, HID = (4, 256, 256)
        H, D = (16, 64)
        NEG_INF = -10000000000.0

        def rope_alternate(inputs, position, min_timescale=1.0, max_timescale=10000.0):
            d = inputs.shape[-1]
            half = d // 2
            fraction = 2.0 * jnp.arange(half, dtype=jnp.float32) / d
            timescale = min_timescale * (max_timescale / min_timescale) ** fraction
            sinusoid = position[:, :, None, None] / timescale
            sin, cos = (jnp.sin(sinusoid), jnp.cos(sinusoid))
            first, second = jnp.split(inputs, 2, axis=-1)
            return jnp.concatenate([(first * cos - second * sin).astype(inputs.dtype), (second * cos + first * sin).astype(inputs.dtype)], axis=-1)
        key = jax.random.key(seed)
        k1, k2, k3 = jax.random.split(key, 3)
        x = jax.random.normal(k1, (B, S, HID), dtype=jnp.float32)
        wqkv = jax.random.normal(k2, (HID, 3 * H * D), dtype=jnp.float32) * (1.0 / np.sqrt(HID))
        wo = jax.random.normal(k3, (H * D, HID), dtype=jnp.float32) * (1.0 / np.sqrt(H * D))
        return {'x': x, 'wqkv': wqkv, 'wo': wo}
    _L0_attn_all = _L0_attn_setup()
    _L0_attn_in = {k: v for k, v in _L0_attn_all.items() if k in ('wqkv', 'wo')}
    del _L0_attn_all

    def _L0_cond2_setup():
        import jax, jax.numpy as jnp
        import numpy as np
        D_MODEL = 256
        D_FF = 1024
        N_EXPERTS = 5
        BATCH = 8
        SEQ = 512

        def _gated_ffn(x, wi0, wi1, wo):
            g = jax.nn.gelu(x @ wi0, approximate=True)
            l = x @ wi1
            return g * l @ wo
        key = jax.random.key(seed)
        ks = jax.random.split(key, 12)
        s = 0.02
        inp = {'hidden_states': jax.random.normal(ks[0], (BATCH, SEQ, D_MODEL), jnp.float32), 'type_label': jax.random.randint(ks[1], (BATCH,), 0, N_EXPERTS, jnp.int32), 'Wi0': jax.random.normal(ks[2], (N_EXPERTS, D_MODEL, D_FF), jnp.float32) * s, 'Wi1': jax.random.normal(ks[3], (N_EXPERTS, D_MODEL, D_FF), jnp.float32) * s, 'Wo': jax.random.normal(ks[4], (N_EXPERTS, D_FF, D_MODEL), jnp.float32) * s, 'sWi0': jax.random.normal(ks[5], (D_MODEL, D_FF), jnp.float32) * s, 'sWi1': jax.random.normal(ks[6], (D_MODEL, D_FF), jnp.float32) * s, 'sWo': jax.random.normal(ks[7], (D_FF, D_MODEL), jnp.float32) * s, 'g0': jax.random.normal(ks[8], (2 * D_MODEL, D_MODEL), jnp.float32) * s, 'g1': jax.random.normal(ks[9], (D_MODEL, 2), jnp.float32) * s}
        return inp
    _L0_cond2_all = _L0_cond2_setup()
    _L0_cond2_in = {k: v for k, v in _L0_cond2_all.items() if k in ('Wi0', 'Wi1', 'Wo', 'sWi0', 'sWi1', 'sWo', 'g0', 'g1')}
    del _L0_cond2_all

    def _L0_ffn_setup():
        import jax, jax.numpy as jnp
        import numpy as np
        SWIGLU_ALPHA = 1.702
        SWIGLU_LIMIT = 7.0
        TOP_K = 4
        key = jax.random.key(seed)
        k = jax.random.split(key, 5)
        B, S, D, E, I = (2, 256, 256, 8, 512)
        return {'hidden_states': jax.random.normal(k[0], (B, S, D), dtype=jnp.float32), 'router_weight': jax.random.normal(k[1], (E, D), dtype=jnp.float32) * 0.02, 'router_bias': jnp.zeros((E,), dtype=jnp.float32), 'gate_up_proj': jax.random.normal(k[2], (E, 2 * I, D), dtype=jnp.float32) * 0.02, 'gate_up_proj_bias': jnp.zeros((E, 2 * I), dtype=jnp.float32), 'down_proj': jax.random.normal(k[3], (E, D, I), dtype=jnp.float32) * 0.02, 'down_proj_bias': jnp.zeros((E, D), dtype=jnp.float32)}
    _L0_ffn_all = _L0_ffn_setup()
    _L0_ffn_in = {k: v for k, v in _L0_ffn_all.items() if k in ('router_weight', 'router_bias', 'gate_up_proj', 'gate_up_proj_bias', 'down_proj', 'down_proj_bias')}
    del _L0_ffn_all

    def _L1_cond_setup():
        import jax, jax.numpy as jnp
        import numpy as np
        B, S, D, F = (32, 128, 256, 1024)
        R_COMMON, R_DOMAIN, E = (16, 16, 8)
        ALPHA = 2.0

        def _expert_lora(x, expert_ids, Wa, Wb):
            Ab = Wa[expert_ids]
            Bb = Wb[expert_ids]
            low = jnp.einsum('bsd,brd->bsr', x, Ab)
            return ALPHA * jnp.einsum('bsr,bor->bso', low, Bb)
        key = jax.random.key(seed)
        ks = jax.random.split(key, 12)
        sd = lambda k, shape: jax.random.normal(k, shape, dtype=jnp.float32) * (1.0 / np.sqrt(shape[-1]))
        return {'hidden_states': jax.random.normal(ks[0], (B, S, D), dtype=jnp.float32), 'expert_ids': jax.random.randint(ks[1], (B,), 0, E, dtype=jnp.int32), 'wi': sd(ks[2], (F, D)), 'wo': sd(ks[3], (D, F)), 'common_wi_a': sd(ks[4], (R_COMMON, D)), 'common_wi_b': sd(ks[5], (F, R_COMMON)), 'common_wo_a': sd(ks[6], (R_COMMON, F)), 'common_wo_b': sd(ks[7], (D, R_COMMON)), 'experts_wi_a': sd(ks[8], (E, R_DOMAIN, D)), 'experts_wi_b': sd(ks[9], (F, R_DOMAIN)) * jnp.ones((E, 1, 1)) * 0.0 + sd(ks[9], (E, F, R_DOMAIN)), 'experts_wo_a': sd(ks[10], (E, R_DOMAIN, F)), 'experts_wo_b': sd(ks[11], (E, D, R_DOMAIN))}
    _L1_cond_all = _L1_cond_setup()
    _L1_cond_in = {k: v for k, v in _L1_cond_all.items() if k in ('wi', 'wo', 'common_wi_a', 'common_wi_b', 'common_wo_a', 'common_wo_b', 'experts_wi_a', 'experts_wi_b', 'experts_wo_a', 'experts_wo_b')}
    del _L1_cond_all

    def _L1_attn_setup():
        import jax, jax.numpy as jnp
        import numpy as np
        import math
        B, T, C = (2, 512, 256)
        NH = 16
        HD = C // NH

        def _rope_factor(T, d, dtype):
            theta = 1.0 / 10000.0 ** (2.0 * jnp.arange(0, d // 2, dtype=jnp.float32) / d)
            seq = jnp.arange(1, T + 1, dtype=jnp.float32)
            ang = jnp.einsum('n,d->nd', seq, theta)
            ang = jnp.concatenate([ang, ang], axis=-1)
            return (jnp.cos(ang) + jnp.sin(ang)).astype(dtype)
        key = jax.random.key(seed)
        ks = jax.random.split(key, 5)
        s = 0.02
        return {'x': jax.random.normal(ks[0], (B, T, C), dtype=jnp.float32), 'W_attn': jax.random.normal(ks[1], (3 * C, C), dtype=jnp.float32) * s, 'b_attn': jax.random.normal(ks[2], (3 * C,), dtype=jnp.float32) * s, 'W_proj': jax.random.normal(ks[3], (C, C), dtype=jnp.float32) * s, 'b_proj': jax.random.normal(ks[4], (C,), dtype=jnp.float32) * s}
    _L1_attn_all = _L1_attn_setup()
    _L1_attn_in = {k: v for k, v in _L1_attn_all.items() if k in ('W_attn', 'b_attn', 'W_proj', 'b_proj')}
    del _L1_attn_all

    def _L1_cond2_setup():
        import jax, jax.numpy as jnp
        import numpy as np
        LN_EPS = 1e-05
        key = jax.random.key(seed)
        ks = jax.random.split(key, 8)
        B, S, H, A, L = (32, 512, 256, 64, 10)
        return {'hidden_states': jax.random.normal(ks[0], (B, S, H), dtype=jnp.float32), 'language_ids': jax.random.randint(ks[1], (B,), 0, L, dtype=jnp.int64), 'W1': jax.random.normal(ks[2], (L, H, A), dtype=jnp.float32) * (1.0 / np.sqrt(H)), 'b1': jnp.zeros((L, A), dtype=jnp.float32), 'W2': jax.random.normal(ks[3], (L, A, H), dtype=jnp.float32) * (1.0 / np.sqrt(A)), 'b2': jnp.zeros((L, H), dtype=jnp.float32), 'gamma': jnp.ones((L, H), dtype=jnp.float32), 'beta': jnp.zeros((L, H), dtype=jnp.float32)}
    _L1_cond2_all = _L1_cond2_setup()
    _L1_cond2_in = {k: v for k, v in _L1_cond2_all.items() if k in ('W1', 'b1', 'W2', 'b2', 'gamma', 'beta')}
    del _L1_cond2_all

    def _L1_ffn_setup():
        import jax, jax.numpy as jnp
        import numpy as np
        key = jax.random.key(seed)
        k1, k2, k3, k4, k5 = jax.random.split(key, 5)
        d_in, d_out, r = (256, 256, 32)
        x = jax.random.normal(k1, (8, 2048, d_in), dtype=jnp.float32)
        W = jax.random.normal(k2, (d_out, d_in), dtype=jnp.float32) * (1.0 / np.sqrt(d_in))
        b = jax.random.normal(k3, (d_out,), dtype=jnp.float32) * 0.01
        V_r = jax.random.normal(k4, (d_in, r), dtype=jnp.float32) * (1.0 / np.sqrt(d_in))
        C = jax.random.normal(k5, (d_out, r), dtype=jnp.float32) * (1.0 / np.sqrt(r))
        return {'x': x, 'W': W, 'b': b, 'V_r': V_r, 'C': C}
    _L1_ffn_all = _L1_ffn_setup()
    _L1_ffn_in = {k: v for k, v in _L1_ffn_all.items() if k in ('W', 'b', 'V_r', 'C')}
    del _L1_ffn_all
    return {'x': x, 'itok_B_0_7': itok_B_0_7, 'itok_B_0_2': itok_B_0_2, 'itok_B_0_8': itok_B_0_8, 'L0_cond_weight': _L0_cond_in['weight'], 'L0_cond_bias': _L0_cond_in['bias'], 'L0_attn_wqkv': _L0_attn_in['wqkv'], 'L0_attn_wo': _L0_attn_in['wo'], 'L0_cond2_Wi0': _L0_cond2_in['Wi0'], 'L0_cond2_Wi1': _L0_cond2_in['Wi1'], 'L0_cond2_Wo': _L0_cond2_in['Wo'], 'L0_cond2_sWi0': _L0_cond2_in['sWi0'], 'L0_cond2_sWi1': _L0_cond2_in['sWi1'], 'L0_cond2_sWo': _L0_cond2_in['sWo'], 'L0_cond2_g0': _L0_cond2_in['g0'], 'L0_cond2_g1': _L0_cond2_in['g1'], 'L0_ffn_router_weight': _L0_ffn_in['router_weight'], 'L0_ffn_router_bias': _L0_ffn_in['router_bias'], 'L0_ffn_gate_up_proj': _L0_ffn_in['gate_up_proj'], 'L0_ffn_gate_up_proj_bias': _L0_ffn_in['gate_up_proj_bias'], 'L0_ffn_down_proj': _L0_ffn_in['down_proj'], 'L0_ffn_down_proj_bias': _L0_ffn_in['down_proj_bias'], 'L1_cond_wi': _L1_cond_in['wi'], 'L1_cond_wo': _L1_cond_in['wo'], 'L1_cond_common_wi_a': _L1_cond_in['common_wi_a'], 'L1_cond_common_wi_b': _L1_cond_in['common_wi_b'], 'L1_cond_common_wo_a': _L1_cond_in['common_wo_a'], 'L1_cond_common_wo_b': _L1_cond_in['common_wo_b'], 'L1_cond_experts_wi_a': _L1_cond_in['experts_wi_a'], 'L1_cond_experts_wi_b': _L1_cond_in['experts_wi_b'], 'L1_cond_experts_wo_a': _L1_cond_in['experts_wo_a'], 'L1_cond_experts_wo_b': _L1_cond_in['experts_wo_b'], 'L1_attn_W_attn': _L1_attn_in['W_attn'], 'L1_attn_b_attn': _L1_attn_in['b_attn'], 'L1_attn_W_proj': _L1_attn_in['W_proj'], 'L1_attn_b_proj': _L1_attn_in['b_proj'], 'L1_cond2_W1': _L1_cond2_in['W1'], 'L1_cond2_b1': _L1_cond2_in['b1'], 'L1_cond2_W2': _L1_cond2_in['W2'], 'L1_cond2_b2': _L1_cond2_in['b2'], 'L1_cond2_gamma': _L1_cond2_in['gamma'], 'L1_cond2_beta': _L1_cond2_in['beta'], 'L1_ffn_W': _L1_ffn_in['W'], 'L1_ffn_b': _L1_ffn_in['b'], 'L1_ffn_V_r': _L1_ffn_in['V_r'], 'L1_ffn_C': _L1_ffn_in['C']}

def reference(x, itok_B_0_7, itok_B_0_2, itok_B_0_8, L0_cond_weight, L0_cond_bias, L0_attn_wqkv, L0_attn_wo, L0_cond2_Wi0, L0_cond2_Wi1, L0_cond2_Wo, L0_cond2_sWi0, L0_cond2_sWi1, L0_cond2_sWo, L0_cond2_g0, L0_cond2_g1, L0_ffn_router_weight, L0_ffn_router_bias, L0_ffn_gate_up_proj, L0_ffn_gate_up_proj_bias, L0_ffn_down_proj, L0_ffn_down_proj_bias, L1_cond_wi, L1_cond_wo, L1_cond_common_wi_a, L1_cond_common_wi_b, L1_cond_common_wo_a, L1_cond_common_wo_b, L1_cond_experts_wi_a, L1_cond_experts_wi_b, L1_cond_experts_wo_a, L1_cond_experts_wo_b, L1_attn_W_attn, L1_attn_b_attn, L1_attn_W_proj, L1_attn_b_proj, L1_cond2_W1, L1_cond2_b1, L1_cond2_W2, L1_cond2_b2, L1_cond2_gamma, L1_cond2_beta, L1_ffn_W, L1_ffn_b, L1_ffn_V_r, L1_ffn_C):
    import jax
    import jax.numpy as jnp

    def _L0_cond_ref(x, subject_id, weight, bias):
        import jax, jax.numpy as jnp
        import numpy as np
        S, O, H = (8, 256, 256)
        B, N = (32, 128)
        W = weight[subject_id]
        b = bias[subject_id]
        y = jnp.einsum('bnh,boh->bno', x, W) + b[:, None, :]
        return y

    def _L0_attn_ref(x, wqkv, wo):
        import jax, jax.numpy as jnp
        import numpy as np
        B, S, HID = (4, 256, 256)
        H, D = (16, 64)
        NEG_INF = -10000000000.0

        def rope_alternate(inputs, position, min_timescale=1.0, max_timescale=10000.0):
            d = inputs.shape[-1]
            half = d // 2
            fraction = 2.0 * jnp.arange(half, dtype=jnp.float32) / d
            timescale = min_timescale * (max_timescale / min_timescale) ** fraction
            sinusoid = position[:, :, None, None] / timescale
            sin, cos = (jnp.sin(sinusoid), jnp.cos(sinusoid))
            first, second = jnp.split(inputs, 2, axis=-1)
            return jnp.concatenate([(first * cos - second * sin).astype(inputs.dtype), (second * cos + first * sin).astype(inputs.dtype)], axis=-1)
        b, s, _ = x.shape
        qkv = jnp.einsum('bsh,hf->bsf', x, wqkv).reshape(b, s, 3, H, D)
        q, k, v = (qkv[:, :, 0], qkv[:, :, 1], qkv[:, :, 2])
        pos = jnp.broadcast_to(jnp.arange(s, dtype=jnp.float32)[None, :], (b, s))
        q = rope_alternate(q, pos)
        k = rope_alternate(k, pos)
        q = q / jnp.sqrt(jnp.float32(D)).astype(q.dtype)
        logits = jnp.einsum('bqhd,bkhd->bhqk', q, k)
        causal = jnp.where(jnp.tril(jnp.ones((s, s), dtype=bool))[None, None], 0.0, NEG_INF).astype(logits.dtype)
        probs = jax.nn.softmax(logits + causal, axis=-1)
        ctx = jnp.einsum('bhqk,bkhd->bqhd', probs, v).reshape(b, s, H * D)
        return jnp.einsum('bsf,fh->bsh', ctx, wo)

    def _L0_cond2_ref(hidden_states, type_label, Wi0, Wi1, Wo, sWi0, sWi1, sWo, g0, g1):
        import jax, jax.numpy as jnp
        import numpy as np
        D_MODEL = 256
        D_FF = 1024
        N_EXPERTS = 5
        BATCH = 8
        SEQ = 512

        def _gated_ffn(x, wi0, wi1, wo):
            g = jax.nn.gelu(x @ wi0, approximate=True)
            l = x @ wi1
            return g * l @ wo
        share_out = _gated_ffn(hidden_states, sWi0, sWi1, sWo)
        wi0 = Wi0[type_label]
        wi1 = Wi1[type_label]
        wo = Wo[type_label]
        hg = jax.nn.gelu(jnp.einsum('bsd,bdf->bsf', hidden_states, wi0), approximate=True)
        hl = jnp.einsum('bsd,bdf->bsf', hidden_states, wi1)
        expert_out = jnp.einsum('bsf,bfd->bsd', hg * hl, wo)
        gate_in = jnp.concatenate([expert_out[:, 0], share_out[:, 0]], axis=-1)
        weights = jax.nn.softmax(jax.nn.relu(gate_in @ g0) @ g1, axis=-1)
        w0 = weights[:, 0][:, None, None]
        w1 = weights[:, 1][:, None, None]
        return expert_out * w0 + share_out * w1

    def _L0_ffn_ref(hidden_states, router_weight, router_bias, gate_up_proj, gate_up_proj_bias, down_proj, down_proj_bias):
        import jax, jax.numpy as jnp
        import numpy as np
        SWIGLU_ALPHA = 1.702
        SWIGLU_LIMIT = 7.0
        TOP_K = 4
        B, S, D = hidden_states.shape
        E = router_weight.shape[0]
        x = hidden_states.reshape(-1, D)
        N = x.shape[0]
        logits = x @ router_weight.T + router_bias
        topk_logits, topk_idx = jax.lax.top_k(logits, TOP_K)
        topk_w = jax.nn.softmax(topk_logits.astype(jnp.float32), axis=-1)
        combine = jnp.zeros((N, E), dtype=jnp.float32)
        combine = combine.at[jnp.arange(N)[:, None], topk_idx].set(topk_w)
        gate_up = jnp.einsum('nd,ejd->nej', x, gate_up_proj) + gate_up_proj_bias
        gate, up = jnp.split(gate_up, 2, axis=-1)
        gate = jnp.minimum(gate, SWIGLU_LIMIT)
        up = jnp.clip(up, -SWIGLU_LIMIT, SWIGLU_LIMIT)
        act = (up + 1.0) * gate * jax.nn.sigmoid(SWIGLU_ALPHA * gate)
        out = jnp.einsum('nei,edi->ned', act, down_proj) + down_proj_bias
        y = jnp.einsum('ned,ne->nd', out, combine.astype(out.dtype))
        return y.reshape(B, S, D)

    def _L1_cond_ref(hidden_states, expert_ids, wi, wo, common_wi_a, common_wi_b, common_wo_a, common_wo_b, experts_wi_a, experts_wi_b, experts_wo_a, experts_wo_b):
        import jax, jax.numpy as jnp
        import numpy as np
        B, S, D, F = (32, 128, 256, 1024)
        R_COMMON, R_DOMAIN, E = (16, 16, 8)
        ALPHA = 2.0

        def _expert_lora(x, expert_ids, Wa, Wb):
            Ab = Wa[expert_ids]
            Bb = Wb[expert_ids]
            low = jnp.einsum('bsd,brd->bsr', x, Ab)
            return ALPHA * jnp.einsum('bsr,bor->bso', low, Bb)
        x = hidden_states
        hidden_i = jnp.einsum('bsd,fd->bsf', x, wi)
        hidden_i += ALPHA * jnp.einsum('bsr,fr->bsf', jnp.einsum('bsd,rd->bsr', x, common_wi_a), common_wi_b)
        hidden_i += _expert_lora(x, expert_ids, experts_wi_a, experts_wi_b)
        hidden_i = jax.nn.relu(hidden_i)
        hidden_o = jnp.einsum('bsf,df->bsd', hidden_i, wo)
        hidden_o += ALPHA * jnp.einsum('bsr,dr->bsd', jnp.einsum('bsf,rf->bsr', hidden_i, common_wo_a), common_wo_b)
        hidden_o += _expert_lora(hidden_i, expert_ids, experts_wo_a, experts_wo_b)
        return hidden_o

    def _L1_attn_ref(x, W_attn, b_attn, W_proj, b_proj):
        import jax, jax.numpy as jnp
        import numpy as np
        import math
        B, T, C = (2, 512, 256)
        NH = 16
        HD = C // NH

        def _rope_factor(T, d, dtype):
            theta = 1.0 / 10000.0 ** (2.0 * jnp.arange(0, d // 2, dtype=jnp.float32) / d)
            seq = jnp.arange(1, T + 1, dtype=jnp.float32)
            ang = jnp.einsum('n,d->nd', seq, theta)
            ang = jnp.concatenate([ang, ang], axis=-1)
            return (jnp.cos(ang) + jnp.sin(ang)).astype(dtype)
        Bs, Ts, Cs = x.shape
        qkv = x @ W_attn.T + b_attn
        q, k, v = jnp.split(qkv, 3, axis=-1)

        def to_heads(t):
            return t.reshape(Bs, Ts, NH, HD).transpose(0, 2, 1, 3)
        q, k, v = (to_heads(q), to_heads(k), to_heads(v))
        f = _rope_factor(Ts, HD, x.dtype)
        q = q * f
        k = k * f
        att = jnp.einsum('bhqd,bhkd->bhqk', q, k) * (1.0 / math.sqrt(HD))
        causal = jnp.tril(jnp.ones((Ts, Ts), dtype=bool))
        att = jnp.where(causal, att, jnp.finfo(att.dtype).min)
        att = jax.nn.softmax(att, axis=-1)
        y = jnp.einsum('bhqk,bhkd->bhqd', att, v)
        y = y.transpose(0, 2, 1, 3).reshape(Bs, Ts, Cs)
        y = y @ W_proj.T + b_proj
        return y

    def _L1_cond2_ref(hidden_states, language_ids, W1, b1, W2, b2, gamma, beta):
        import jax, jax.numpy as jnp
        import numpy as np
        LN_EPS = 1e-05
        w1 = W1[language_ids]
        w2 = W2[language_ids]
        h = jnp.einsum('bsh,bha->bsa', hidden_states, w1) + b1[language_ids][:, None, :]
        h = jax.nn.relu(h)
        adapted = jnp.einsum('bsa,bah->bsh', h, w2) + b2[language_ids][:, None, :]
        x = hidden_states + adapted
        mean = jnp.mean(x, axis=-1, keepdims=True)
        var = jnp.mean(jnp.square(x - mean), axis=-1, keepdims=True)
        normed = (x - mean) * jax.lax.rsqrt(var + LN_EPS)
        return normed * gamma[language_ids][:, None, :] + beta[language_ids][:, None, :]

    def _L1_ffn_ref(x, W, b, V_r, C):
        import jax, jax.numpy as jnp
        import numpy as np
        base = jnp.einsum('bsd,od->bso', x, W) + b
        correction = jnp.einsum('bsr,or->bso', jnp.einsum('bsd,dr->bsr', x, V_r), C)
        return base + correction
    x = x + _L0_attn_ref(_L0_cond_ref(x, itok_B_0_7, L0_cond_weight, L0_cond_bias), L0_attn_wqkv, L0_attn_wo)
    x = x + _L0_ffn_ref(_L0_cond2_ref(x, itok_B_0_2, L0_cond2_Wi0, L0_cond2_Wi1, L0_cond2_Wo, L0_cond2_sWi0, L0_cond2_sWi1, L0_cond2_sWo, L0_cond2_g0, L0_cond2_g1), L0_ffn_router_weight, L0_ffn_router_bias, L0_ffn_gate_up_proj, L0_ffn_gate_up_proj_bias, L0_ffn_down_proj, L0_ffn_down_proj_bias)
    x = x + _L1_attn_ref(_L1_cond_ref(x, itok_B_0_7, L1_cond_wi, L1_cond_wo, L1_cond_common_wi_a, L1_cond_common_wi_b, L1_cond_common_wo_a, L1_cond_common_wo_b, L1_cond_experts_wi_a, L1_cond_experts_wi_b, L1_cond_experts_wo_a, L1_cond_experts_wo_b), L1_attn_W_attn, L1_attn_b_attn, L1_attn_W_proj, L1_attn_b_proj)
    x = x + _L1_ffn_ref(_L1_cond2_ref(x, itok_B_0_8, L1_cond2_W1, L1_cond2_b1, L1_cond2_W2, L1_cond2_b2, L1_cond2_gamma, L1_cond2_beta), L1_ffn_W, L1_ffn_b, L1_ffn_V_r, L1_ffn_C)
    return x

_drawn_inputs = setup_inputs


def setup_inputs(seed=0):
    import zlib

    import numpy as np

    out = dict(_drawn_inputs(seed))
    spreads = {'L0_ffn_router_bias': (0.0, 0.1),
     'L0_ffn_gate_up_proj_bias': (0.0, 0.574),
     'L0_ffn_down_proj_bias': (0.0, 0.1),
     'L1_cond2_b1': (0.0, 2.0),
     'L1_cond2_b2': (0.0, 2.0),
     'L1_cond2_gamma': (1.0, 0.6),
     'L1_cond2_beta': (0.0, 0.8)}
    factors = {'L0_cond2_Wi0': 7.043,
     'L0_cond2_Wi1': 6.677,
     'L0_cond2_Wo': 7.028,
     'L0_cond2_sWi0': 7.059,
     'L0_cond2_sWi1': 7.057,
     'L0_cond2_sWo': 6.772,
     'L0_cond2_g0': 8.0,
     'L0_cond2_g1': 8.0,
     'L0_ffn_router_weight': 6.856,
     'L0_ffn_gate_up_proj': 8.0,
     'L0_ffn_down_proj': 3.911,
     'L1_attn_b_attn': 17.202,
     'L1_attn_b_proj': 198.92,
     'L1_ffn_b': 200.0,
     'L1_cond2_W1': 5.514,
     'L1_cond2_W2': 4.554,
     'L1_ffn_W': 3.697,
     'L1_ffn_V_r': 3.686,
     'L1_ffn_C': 3.66}
    for name, (base, spread) in spreads.items():
        noise = np.random.default_rng([zlib.crc32(name.encode()), seed]).standard_normal(out[name].shape)
        drawn = base * np.exp(spread * noise) if base else spread * noise
        out[name] = jnp.asarray(drawn.astype(out[name].dtype))
    for name, factor in factors.items():
        out[name] = (out[name] * factor).astype(out[name].dtype)
    return out
```

```python
from contextlib import ExitStack

import numpy as np

import concourse.bass as bass
from concourse import mybir

F32 = mybir.dt.float32
I32 = mybir.dt.int32
ALU = mybir.AluOpType
ACT = mybir.ActivationFunctionType
AX = mybir.AxisListType

P = 128
B, S, D = 32, 64, 256
N = B * S
KT = D // P
PAIRS = N // P
TB = 512
NTB = N // TB
HEADS = 16
HD0 = 64
HD1 = D // HEADS
QF = HEADS * HD0
FF = 1024
FT = FF // P
E0 = 8
E2 = 5
SLOTS = 4
BLOCKS = (B + E2 * (SLOTS - 1)) // SLOTS
EM, IM = 8, 512
TOP_K = 4
JT = IM // P
LIMIT, SWIGLU_ALPHA = 7.0, 1.702
EL, RL = 8, 16
LANG, A2 = 10, 64
LT = LANG * A2 // P
EPS = 1e-5


def bcast(ap, axis, n):
    ap = ap.unsqueeze(axis)
    shape = list(ap.shape)
    shape[axis] = n
    return ap.to_broadcast(shape)


def wait(eng, sem, value):
    if isinstance(value, int) and value <= 0:
        return
    eng.wait_ge(sem, value)


def live(p):
    return not isinstance(p, int) or 0 <= p < PAIRS


LEAD, TAIL = 3, 3


def pipeline(eng, step):
    for i in range(-2, LEAD):
        step(i, i % 2)
    trips = (PAIRS - 2 - LEAD) // 2
    with eng.Fori(0, trips) as t:
        for u in range(2):
            step(t * 2 + (LEAD + u), (LEAD + u) % 2)
    for i in range(LEAD + 2 * trips, PAIRS + TAIL):
        step(i, i % 2)


def build_program(nc, io, out):
    ctx = ExitStack()
    with ctx:
        def sb(name, shape, dt=F32, c=ctx):
            return c.enter_context(nc.sbuf_tensor(name, shape, dt))

        def sem(name):
            return ctx.enter_context(nc.semaphore(name))

        banks = [ctx.enter_context(nc.psum_tensor(f"bank{k}", [P, 512], F32)) for k in range(8)]
        xT = sb("xT", [P, KT, N + SLOTS * S])
        ident = sb("ident", [P, P])
        mask = sb("mask", [P, S])
        cols = sb("cols", [P, 16])
        samp = sb("samp", [P, 3, B])
        samp_i = sb("samp_i", [P, 3, B], I32)
        oh_sub = sb("oh_sub", [E0, B])
        oh_lora = sb("oh_lora", [P, B])
        oh_lang = sb("oh_lang", [P, LT, B])
        oh_lang10 = sb("oh_lang10", [LANG, B])
        slot_sample = sb("slot_sample", [1, BLOCKS * SLOTS], I32)
        block_expert = sb("block_expert", [1, BLOCKS], I32)

        attention0(nc, io, banks, sb, sem, xT, ident, mask, cols, samp, samp_i, oh_sub, oh_lora,
                   oh_lang, oh_lang10, slot_sample, block_expert)
        with ExitStack() as c:
            hT = sb("hT", [P, KT, N], F32, c)
            gated_ffn(nc, io, banks, sb, sem, xT, hT, slot_sample, block_expert)
            mixture(nc, io, banks, sb, sem, xT, hT, ident)
        with ExitStack() as c:
            zT = sb("zT", [P, KT, N], F32, c)
            lora_ffn(nc, io, banks, sb, sem, xT, zT, oh_lora)
            attention1(nc, io, banks, sb, sem, xT, zT, ident, mask)
        adapter_ffn(nc, io, banks, sb, sem, xT, oh_lang, oh_lang10, out)


def attention0(nc, io, banks, sb0, sem, xT, ident, mask, cols, samp, samp_i, oh_sub, oh_lora, oh_lang,
               oh_lang10, slot_sample, block_expert):
    with ExitStack() as c:
        def sb(name, shape, dt=F32):
            return sb0(name, shape, dt, c)

        wqkv = sb("wqkv", [P, KT, 3 * QF])
        wo = sb("wo", [P, QF // P, D])
        rope = sb("rope", [P, 4, HD0])
        btab = sb("btab", [E0, D])
        biasT = sb("biasT", [P, KT, B])
        wsub = [sb(f"wsub{k}", [P, 2, KT, D]) for k in range(2)]
        xs = [sb(f"xs{k}", [P, KT, P]) for k in range(2)]
        ysb = sb("ysb", [P, D])
        yT = [sb(f"yT{k}", [P, KT, P]) for k in range(2)]
        rc = [sb(f"rc{k}", [P, 512]) for k in range(2)]
        rs = [sb(f"rs{k}", [P, 512]) for k in range(2)]
        qk = [sb(f"qk{k}", [P, 2 * QF]) for k in range(2)]
        v = [sb(f"v{k}", [P, QF]) for k in range(2)]
        qT = sb("qT", [P, HEADS // 2, P])
        kpad = sb("kpad", [P, HEADS // 2, 2, P])
        sc = sb("sc", [P, HEADS, S])
        ex = sb("ex", [P, HEADS, S])
        mx = sb("mx", [P, HEADS])
        sm = sb("sm", [P, HEADS])
        ri = sb("ri", [P, HEADS])
        pr = sb("pr", [P, HEADS, P])
        prT = sb("prT", [P, HEADS, P])
        ctxT = sb("ctxT", [P, QF // P, P])
        rt = {n: sb("rt_" + n, [1, *s]) for n, s in dict(
            es=(E2, B), j8=(E2, B // SLOTS), ee=(E2, E2), ll=(B, B), q=(BLOCKS * SLOTS,),
            sm=(BLOCKS * SLOTS, B), em=(BLOCKS * SLOTS,),
            kk=(BLOCKS,)).items()}
        oh = sb("r_oh", [1, E2, B])
        cnt = sb("r_cnt", [1, E2])
        cmp8 = sb("r_cmp8", [1, E2, B // SLOTS])
        nblk = sb("r_nblk", [1, E2])
        lowb = sb("r_lowb", [1, E2, E2])
        base = sb("r_base", [1, E2])
        base4 = sb("r_base4", [1, E2])
        same = sb("r_same", [1, B, B])
        rank = sb("r_rank", [1, B])
        ohb = sb("r_ohb", [1, B, E2])
        pos = sb("r_pos", [1, B])
        hit = sb("r_hit", [1, BLOCKS * SLOTS, B])
        sid = sb("r_sid", [1, BLOCKS * SLOTS])
        ble = sb("r_ble", [1, BLOCKS, E2])
        bex = sb("r_bex", [1, BLOCKS])

        a_small, a_x, a_wqkv, a_wo, a_route = (sem(n) for n in (
            "a_small_in", "a_x_in", "a_wqkv_in", "a_wo_in", "a_route_in"))
        a_w = [sem(f"a_wsub{k}_in") for k in range(2)]
        a_zero, a_tab, a_bias_ready, a_bias, a_routed = (sem(n) for n in (
            "a_zeroed", "a_tables", "a_bias_ready", "a_bias_copied", "a_routed"))
        a_xs, a_cond, a_y, a_yt_ready, a_yt = (sem(n) for n in (
            "a_xs_staged", "a_cond_ready", "a_y_copied", "a_yt_ready", "a_yt_copied"))
        a_qk_ready, a_rope, a_add, a_v_ready, a_v = (sem(n) for n in (
            "a_qk_ready", "a_rope_done", "a_rope_added", "a_v_ready", "a_v_copied"))
        a_tq_ready, a_tq, a_s_ready, a_s, a_mx, a_sub, a_exp, a_sum, a_rec, a_p = (sem(n) for n in (
            "a_trqk_ready", "a_trqk_copied", "a_s_ready", "a_s_masked", "a_max", "a_subtracted",
            "a_exp", "a_sum", "a_recip", "a_probs"))
        a_p0, a_tp_ready, a_tp, a_c_ready, a_c, a_o_ready, a_o = (sem(n) for n in (
            "a_probs_half", "a_trp_ready", "a_trp_copied", "a_ctx_ready", "a_ctx_copied", "a_out_ready", "a_out_added"))

        with nc.Block() as block:
            @block.sync
            def _(sp):
                sp.dma_start(samp_i[:, :, :], io["idx"].partition_broadcast(P)).then_inc(a_small, 16)
                for dst, name in ((ident, "ident"), (cols, "cols"), (btab, "c0_bias"), (mask, "mask0")):
                    sp.dma_start(dst[:, :], io[name]).then_inc(a_small, 16)
                sp.dma_start(rope[:, :, :], io["rope"]).then_inc(a_small, 16)
                sp.dma_start(xT[:, :, 0:N], io["xT"].rearrange("(k p) n -> p k n", p=P)).then_inc(a_x, 16)
                sp.wait_ge(a_small, 96)

                def step(i, par):
                    p = i + 2
                    if not live(p):
                        return
                    wait(sp, a_cond, p - 1)
                    for s in range(2):
                        e = sp.value_load(samp_i[0:1, 0, bass.ds(p * 2 + s, 1)], min_val=0, max_val=E0 - 1)
                        sp.dma_start(wsub[par][:, s, :, :], io["c0_wT"][bass.ds(e, 1), :, :].rearrange(
                            "e (k p) o -> p (e k) o", p=P)).then_inc(a_w[par], 16)
                    if isinstance(p, int) and p == 0:
                        sp.dma_start(wqkv[:, :, :], io["a0_wqkv"].rearrange("(k p) n -> p k n", p=P)).then_inc(a_wqkv, 16)
                        sp.dma_start(wo[:, :, :], io["a0_wo"].rearrange("(k p) n -> p k n", p=P)).then_inc(a_wo, 16)
                        for n in rt:
                            sp.dma_start(rt[n][:], io["rt_" + n]).then_inc(a_route, 16)

                pipeline(sp, step)

            @block.gpsimd
            def _(pool):
                pool.memset(kpad[:, :, :, :], 0.0).then_inc(a_zero, 1)
                pool.memset(pr[:, :, :], 0.0).then_inc(a_zero, 1)
                pool.memset(xT[:, :, N:], 0.0).then_inc(a_zero, 1)
                pool.wait_ge(a_x, 16)

                def step(i, par):
                    p = i + 2
                    if live(p):
                        wait(pool, a_cond, p - 1)
                        pool.tensor_copy(xs[par][:, :, :], xT[:, :, bass.ds(p * P, P)]).then_inc(a_xs, 1)
                    for half in range(2):
                        if live(i):
                            if half == 0:
                                wait(pool, a_tq_ready, 4 * (i - 2) + 4)
                            for c2 in range(2):
                                n = 4 * i + 2 * half + c2
                                wait(pool, a_rope, n + 1)
                                ch = 2 * half + c2
                                pool.tensor_tensor(qk[par][:, ch * 512:(ch + 1) * 512], rc[c2][:, :],
                                                   rs[c2][:, :], ALU.add).then_inc(a_add, 1)
                        if half == 0 and live(i - 2):
                            wait(pool, a_rec, i - 1)
                            if isinstance(i, int) and i == 2:
                                pool.wait_ge(a_zero, 3)
                            wait(pool, a_tp_ready, 4 * (i - 3) + 4)
                            if live(i):
                                pool.wait_ge(a_add, 4 * i + 2)
                            if live(i + 2):
                                pool.wait_ge(a_xs, i + 3)
                            pool.tensor_tensor(pr[0:S, :, 0:S], ex[0:S, :, :], bcast(ri[0:S, :], 2, S), ALU.mult).then_inc(a_p0, 1)
                            pool.wait_ge(a_p0, i - 1)
                            pool.tensor_tensor(pr[S:P, :, S:P], ex[S:P, :, :], bcast(ri[S:P, :], 2, S), ALU.mult).then_inc(a_p, 1)
                            pool.wait_ge(a_p, i - 1)

                pipeline(pool, step)

            @block.tensor
            def _(pe):
                pe.wait_ge(a_tab, 2)
                for k in range(KT):
                    mm = pe.matmul(banks[7][:, k * B:(k + 1) * B], btab[:, k * P:(k + 1) * P], oh_sub[:, :],
                                   start=True, stop=True)
                mm.then_inc(a_bias_ready, 1)

                def qk_chunks(i, par, chunks):
                    for ch in chunks:
                        wait(pe, a_rope, 4 * i + ch - 1)
                        for k in range(KT):
                            mm = pe.matmul(banks[1 + ch % 2][:, :], yT[par][:, k, :],
                                           wqkv[:, k, ch * 512:(ch + 1) * 512], start=k == 0, stop=k == KT - 1)
                        mm.then_inc(a_qk_ready, 1)

                def step(i, par):
                    if live(i):
                        if isinstance(i, int) and i == 0:
                            pe.wait_ge(a_wqkv, 16)
                        pe.wait_ge(a_yt, i + 1)
                        qk_chunks(i, par, (0, 1))
                    if live(i - 3):
                        p = i - 3
                        if isinstance(p, int) and p == 0:
                            pe.wait_ge(a_wo, 16)
                        pe.wait_ge(a_c, 2 * p + 2)
                        wait(pe, a_o, p)
                        for o in range(KT):
                            for k in range(QF // P):
                                mm = pe.matmul(banks[0][:, o * P:(o + 1) * P], wo[:, k, o * P:(o + 1) * P],
                                               ctxT[:, k, :], start=k == 0, stop=k == QF // P - 1)
                        mm.then_inc(a_o_ready, 1)
                    if live(i - 1):
                        p = i - 1
                        for ch in range(2):
                            wait(pe, a_v, 2 * p + ch)
                            for k in range(KT):
                                mm = pe.matmul(banks[3][:, :], yT[1 - par][:, k, :],
                                               wqkv[:, k, 2 * QF + ch * 512:2 * QF + (ch + 1) * 512],
                                               start=k == 0, stop=k == KT - 1)
                            mm.then_inc(a_v_ready, 1)
                    if live(i + 1):
                        p = i + 1
                        wait(pe, a_o, i - 2)
                        pe.wait_ge(a_xs, p + 1)
                        if isinstance(p, int):
                            pe.wait_ge(a_w[1 - par], 32 * (p // 2 + 1))
                        else:
                            pe.wait_ge(a_w[1 - par], 16 * p + (32 if par == 1 else 16))
                        for s in range(2):
                            for k in range(KT):
                                mm = pe.matmul(banks[0][S * s:S * s + S, 0:D], xs[1 - par][:, k, S * s:S * s + S],
                                               wsub[1 - par][:, s, k, :], start=k == 0, stop=k == KT - 1)
                        mm.then_inc(a_cond, 1)
                    if live(i):
                        qk_chunks(i, par, (2, 3))
                    if live(i - 1):
                        p = i - 1
                        pe.wait_ge(a_add, 4 * p + 4)
                        for f in range(4):
                            wait(pe, a_c, 2 * (i - 3) + f + 1) if f < 2 else wait(pe, a_tq, 4 * p + f - 1)
                            for j in range(4):
                                at = (4 * f + j) * P
                                mm = pe.transpose(banks[6 + f % 2][:, j * P:(j + 1) * P],
                                                  qk[1 - par][:, at:at + P], ident[:, :])
                            mm.then_inc(a_tq_ready, 1)
                    if live(i + 1):
                        pe.wait_ge(a_y, i + 2)
                        for k in range(KT):
                            mm = pe.transpose(banks[0][:, k * P:(k + 1) * P], ysb[:, k * P:(k + 1) * P], ident[:, :])
                        mm.then_inc(a_yt_ready, 1)
                    if live(i - 2):
                        p = i - 2
                        pe.wait_ge(a_p, p + 1)
                        for f in range(4):
                            if f >= 2:
                                wait(pe, a_tp, 4 * p + f - 1)
                            elif live(i - 1):
                                wait(pe, a_tq, 4 * (i - 1) + f + 3)
                            for j in range(4):
                                mm = pe.transpose(banks[6 + f % 2][:, j * P:(j + 1) * P], pr[:, 4 * f + j, :], ident[:, :])
                            mm.then_inc(a_tp_ready, 1)
                    if live(i - 1):
                        p = i - 1
                        pe.wait_ge(a_tq, 4 * p + 4)
                        for f in range(4):
                            wait(pe, a_s, 4 * p + f - 1)
                            for j in range(2):
                                t = 2 * f + j
                                mm = pe.matmul(banks[4 + f % 2][:, j * 256:(j + 1) * 256], qT[:, t, :],
                                               kpad[:, t, :, :], start=True, stop=True)
                            mm.then_inc(a_s_ready, 1)
                    if live(i - 2):
                        p = i - 2
                        for g in range(2):
                            pe.wait_ge(a_tp, 4 * p + 3 + g)
                            for j in range(4):
                                for s in range(2):
                                    h = 8 * g + 2 * j + s
                                    mm = pe.matmul(banks[6 + g][HD0 * s:HD0 * s + HD0, j * P:(j + 1) * P],
                                                   v[par][:, h * HD0:(h + 1) * HD0], prT[:, h, :],
                                                   start=True, stop=True)
                            mm.then_inc(a_c_ready, 1)

                pipeline(pe, step)

            @block.scalar
            def _(act):
                def step(i, par):
                    if live(i - 1):
                        p = i - 1
                        for ch in range(2):
                            act.wait_ge(a_v_ready, 2 * p + ch + 1)
                            act.activation(v[1 - par][:, ch * 512:(ch + 1) * 512], banks[3][:, :],
                                           ACT.Copy).then_inc(a_v, 1)
                    if live(i + 1):
                        act.wait_ge(a_cond, i + 2)
                        act.activation(ysb[:, :], banks[0][:, 0:D], ACT.Copy).then_inc(a_y, 1)
                    if live(i - 1):
                        p = i - 1
                        if isinstance(p, int) and p == 0:
                            act.wait_ge(a_zero, 1)
                        for f in range(4):
                            act.wait_ge(a_tq_ready, 4 * p + f + 1)
                            bank = banks[6 + f % 2][:, :].rearrange("p (t n) -> p t n", n=P)
                            if f < 2:
                                last = act.activation(qT[:, 4 * f:4 * f + 4, :], bank, ACT.Copy)
                            else:
                                for s in range(2):
                                    rows = slice(HD0 * s, HD0 * s + HD0)
                                    last = act.activation(kpad[rows, 4 * f - 8:4 * f - 4, s, :], bank[rows], ACT.Copy)
                            last.then_inc(a_tq, 1)
                    if live(i - 2):
                        p = i - 2
                        for f in range(4):
                            act.wait_ge(a_tp_ready, 4 * p + f + 1)
                            act.activation(prT[:, 4 * f:4 * f + 4, :], banks[6 + f % 2][:, :].rearrange(
                                "p (t n) -> p t n", n=P), ACT.Copy).then_inc(a_tp, 1)
                        for g in range(2):
                            act.wait_ge(a_c_ready, 2 * p + g + 1)
                            act.activation(ctxT[:, 4 * g:4 * g + 4, :], banks[6 + g][:, :].rearrange(
                                "p (t n) -> p t n", n=P), ACT.Copy).then_inc(a_c, 1)
                    if live(i - 1):
                        act.wait_ge(a_sub, i)
                        wait(act, a_p, i - 1)
                        act.activation(ex[:, :, :], sc[:, :, :], ACT.Exp).then_inc(a_exp, 1)

                pipeline(act, step)

            @block.vector
            def _(dve):
                dve.wait_ge(a_small, 96)
                dve.tensor_copy(samp[:, :, :], samp_i[:, :, :]).then_inc(a_tab, 1)
                dve.wait_ge(a_tab, 1)
                dve.tensor_scalar(oh_lora[:, :], samp[:, 0, :], cols[:, 1:2], 2.0, ALU.is_equal, ALU.mult)
                for k in range(LT):
                    dve.tensor_scalar(oh_lang[:, k, :], samp[:, 2, :], cols[:, 2 + k:3 + k], None, ALU.is_equal)
                dve.tensor_scalar(oh_lang10[:, :], samp[0:LANG, 2, :], cols[0:LANG, 0:1], None, ALU.is_equal)
                dve.tensor_scalar(oh_sub[:, :], samp[0:E0, 0, :], cols[0:E0, 0:1], None, ALU.is_equal).then_inc(a_tab, 1)
                dve.wait_ge(a_bias_ready, 1)
                dve.tensor_copy(biasT[:, :, :], banks[7][:, 0:KT * B].rearrange("p (k b) -> p k b", k=KT)).then_inc(a_bias, 1)
                dve.wait_ge(a_bias, 1)

                def route():
                    dve.wait_ge(a_route, 16 * len(rt))
                    ty = samp[0:1, 1, :]
                    n = [0]

                    def then(ins):
                        ins.then_inc(a_routed, 1)
                        n[0] += 1
                        dve.wait_ge(a_routed, n[0])

                    then(dve.tensor_tensor(oh[:, :, :], bcast(ty, 1, E2), rt["es"][:, :, :], ALU.is_equal))
                    then(dve.tensor_reduce(cnt[:, :], oh[:, :, :], AX.X, ALU.add))
                    then(dve.tensor_tensor(cmp8[:, :, :], bcast(cnt[:, :], 2, B // SLOTS), rt["j8"][:, :, :], ALU.is_gt))
                    then(dve.tensor_reduce(nblk[:, :], cmp8[:, :, :], AX.X, ALU.add))
                    then(dve.tensor_tensor(lowb[:, :, :], bcast(nblk[:, :], 1, E2), rt["ee"][:, :, :], ALU.mult))
                    then(dve.tensor_reduce(base[:, :], lowb[:, :, :], AX.X, ALU.add))
                    then(dve.tensor_scalar(base4[:, :], base[:, :], float(SLOTS), None, ALU.mult))
                    then(dve.tensor_tensor(same[:, :, :], bcast(ty, 2, B), bcast(ty, 1, B), ALU.is_equal))
                    then(dve.tensor_tensor(same[:, :, :], same[:, :, :], rt["ll"][:, :, :], ALU.mult))
                    then(dve.tensor_reduce(rank[:, :], same[:, :, :], AX.X, ALU.add))
                    then(dve.tensor_tensor(ohb[:, :, :], oh[:, :, :].rearrange("p e b -> p b e"),
                                           bcast(base4[:, :], 1, B), ALU.mult))
                    then(dve.tensor_reduce(pos[:, :], ohb[:, :, :], AX.X, ALU.add))
                    then(dve.tensor_tensor(pos[:, :], pos[:, :], rank[:, :], ALU.add))
                    then(dve.tensor_tensor(hit[:, :, :], bcast(pos[:, :], 1, BLOCKS * SLOTS),
                                           bcast(rt["q"][:, :], 2, B), ALU.is_equal))
                    then(dve.tensor_tensor(hit[:, :, :], hit[:, :, :], rt["sm"][:, :, :], ALU.mult))
                    then(dve.tensor_reduce(sid[:, :], hit[:, :, :], AX.X, ALU.add))
                    then(dve.tensor_tensor(sid[:, :], sid[:, :], rt["em"][:, :], ALU.add))
                    then(dve.tensor_copy(slot_sample[:, :], sid[:, :]))
                    then(dve.tensor_tensor(ble[:, :, 1:E2], bcast(base[:, 1:E2], 1, BLOCKS),
                                           bcast(rt["kk"][:, :], 2, E2 - 1), ALU.is_le))
                    then(dve.tensor_reduce(bex[:, :], ble[:, :, 1:E2], AX.X, ALU.add))
                    then(dve.tensor_copy(block_expert[:, :], bex[:, :]))

                def rotate(i, chunks):
                    for ch in chunks:
                        n = 4 * i + ch
                        dve.wait_ge(a_qk_ready, n + 1)
                        wait(dve, a_add, n - 1)
                        src = banks[1 + ch % 2][:, :].rearrange("p (h t d) -> p h t d", t=2, d=HD0 // 2)
                        w = 2 * (ch // 2)
                        cos = bcast(rope[:, w, :].rearrange("p (t d) -> p t d", t=2), 1, 512 // HD0)
                        sin = bcast(rope[:, w + 1, :].rearrange("p (t d) -> p t d", t=2), 1, 512 // HD0)
                        dst = [r[ch % 2][:, :].rearrange("p (h t d) -> p h t d", t=2, d=HD0 // 2) for r in (rc, rs)]
                        dve.tensor_tensor(dst[0], src, cos, ALU.mult)
                        dve.tensor_tensor(dst[1], src[:, :, ::-1, :], sin, ALU.mult).then_inc(a_rope, 1)

                def step(i, par):
                    if live(i):
                        rotate(i, (0, 1))
                    if live(i - 2):
                        p = i - 2
                        dve.wait_ge(a_exp, p + 1)
                        wait(dve, a_p, p)
                        dve.tensor_reduce(sm[:, :], ex[:, :, :], AX.X, ALU.add).then_inc(a_sum, 1)
                        dve.wait_ge(a_sum, p + 1)
                        dve.reciprocal(ri[:, :], sm[:, :]).then_inc(a_rec, 1)
                    if live(i - 3):
                        p = i - 3
                        dve.wait_ge(a_o_ready, p + 1)
                        at = xT[:, :, bass.ds(p * P, P)]
                        dve.tensor_tensor(at, banks[0][:, 0:D].rearrange("p (k n) -> p k n", k=KT), at,
                                          ALU.add).then_inc(a_o, 1)
                    if live(i):
                        rotate(i, (2, 3))
                    if live(i + 1):
                        p = i + 1
                        dve.wait_ge(a_yt_ready, p + 1)
                        for k in range(KT):
                            last = dve.tensor_tensor(
                                yT[1 - par][:, k, :].rearrange("p (s n) -> p s n", s=2),
                                banks[0][:, k * P:(k + 1) * P].rearrange("p (s n) -> p s n", s=2),
                                bcast(biasT[:, k, bass.ds(p * 2, 2)], 2, S), ALU.add)
                        last.then_inc(a_yt, 1)
                    if live(i - 1):
                        p = i - 1
                        wait(dve, a_exp, p)
                        for f in range(4):
                            dve.wait_ge(a_s_ready, 4 * p + f + 1)
                            for s in range(2):
                                rows = slice(S * s, S * s + S)
                                last = dve.tensor_tensor(
                                    sc[rows, 4 * f:4 * f + 4, :],
                                    banks[4 + f % 2][rows, :].rearrange("p (h n) -> p h n", n=P)[:, :, S * s:S * s + S],
                                    bcast(mask[rows, :], 1, 4), ALU.add)
                            last.then_inc(a_s, 1)
                        dve.wait_ge(a_s, 4 * p + 4)
                        dve.tensor_reduce(mx[:, :], sc[:, :, :], AX.X, ALU.max).then_inc(a_mx, 1)
                        dve.wait_ge(a_mx, p + 1)
                        dve.tensor_tensor(sc[:, :, :], sc[:, :, :], bcast(mx[:, :], 2, S), ALU.subtract).then_inc(a_sub, 1)
                    if isinstance(i, int) and i == 0:
                        route()

                pipeline(dve, step)


def gated_ffn(nc, io, banks, sb0, sem, xT, hT, slot_sample, block_expert):
    with ExitStack() as c:
        def sb(name, shape, dt=F32):
            return sb0(name, shape, dt, c)

        SW = SLOTS * S
        eo = sb("eo", [P, KT, N + SW])
        w0 = [sb(f"w0_{k}", [P, KT, FF]) for k in range(2)]
        w1 = [sb(f"w1_{k}", [P, KT, FF]) for k in range(2)]
        w2 = [sb(f"w2_{k}", [P, FT, D]) for k in range(2)]
        xg = [sb(f"xg{k}", [P, KT, SW]) for k in range(2)]
        ge = [sb(f"ge{k}", [P, TB]) for k in range(2)]
        h = [sb(f"h{k}", [P, TB]) for k in range(2)]
        g0 = sb("g0", [P, 2 * KT, D])
        g1 = sb("g1", [P, KT, 2])
        gi = sb("gi", [P, 2 * KT, B])
        gr = sb("gr", [P, KT, B])
        z = sb("z", [P, 2, B])
        zm = sb("zm", [P, B])
        zs = sb("zs", [P, B])
        tmp = sb("btmp", [P, KT, TB])
        b_w = [sem(f"b_w{k}_in") for k in range(2)]
        b_g_in, b_xg, b_l_ready, b_ge, b_h, b_o_ready, b_o, b_xg_used = (sem(n) for n in (
            "b_gate_weights_in", "b_gathered", "b_up_ready", "b_gelu", "b_hidden", "b_out_ready",
            "b_out_copied", "b_unused"))
        b_step, b_gp, b_ztrue = sem("b_gate_step"), sem("b_gate_pe"), sem("b_mix")

        SH = BLOCKS % 2

        with nc.Block() as block:
            @block.sync
            def _(sp):
                def load(par, s0, s1, s2):
                    for dst, src in ((w0, s0), (w1, s1), (w2, s2)):
                        sp.dma_start(dst[par][:, :, :], src).then_inc(b_w[par], 16)

                def unit(u, par):
                    wait(sp, b_o_ready, u - 1)
                    e = sp.value_load(block_expert[0:1, bass.ds(u, 1)], min_val=0, max_val=E2 - 1)
                    load(par, *(io[n][bass.ds(e, 1), :, :].rearrange("e (k p) n -> p (e k) n", p=P)
                                for n in ("c2_Wi0", "c2_Wi1", "c2_Wo")))

                unit(0, 0)
                unit(1, 1)
                sp.dma_start(g0[:, :, :], io["c2_g0"].rearrange("(k p) n -> p k n", p=P)).then_inc(b_g_in, 16)
                sp.dma_start(g1[:, :, :], io["c2_g1"].rearrange("(k p) n -> p k n", p=P)).then_inc(b_g_in, 16)
                with sp.Fori(1, BLOCKS // 2) as t:
                    for par in range(2):
                        unit(t * 2 + par, par)
                if BLOCKS % 2:
                    unit(BLOCKS - 1, 0)
                sp.wait_ge(b_o_ready, BLOCKS - 1)
                load(SH, *(io[n].rearrange("(k p) n -> p k n", p=P) for n in ("c2_sWi0", "c2_sWi1", "c2_sWo")))

            @block.gpsimd
            def _(pool):
                def unit(u, par):
                    wait(pool, b_o_ready, u - 1)
                    for j in range(SLOTS):
                        s = pool.value_load(slot_sample[0:1, bass.ds(u * SLOTS + j, 1)], min_val=0, max_val=B + SLOTS - 1)
                        last = pool.tensor_copy(xg[par][:, :, j * S:(j + 1) * S], xT[:, :, bass.ds(s * S, S)])
                    last.then_inc(b_xg, 1)

                unit(0, 0)
                unit(1, 1)
                with pool.Fori(1, BLOCKS // 2) as t:
                    for par in range(2):
                        unit(t * 2 + par, par)
                if BLOCKS % 2:
                    unit(BLOCKS - 1, 0)

            @block.tensor
            def _(pe):
                def unit(u, par, n, rhs, buf):
                    def up(f):
                        wait(pe, b_h, FT * u + f - 1)
                        for bank, w in ((f % 2, w0), (2 + f % 2, w1)):
                            for k in range(KT):
                                mm = pe.matmul(banks[bank][:, 0:n], w[buf][:, k, f * P:(f + 1) * P], rhs(k),
                                               start=k == 0, stop=k == KT - 1)
                        mm.then_inc(b_l_ready, 1)

                    def down(f):
                        pe.wait_ge(b_h, FT * u + f + 1)
                        if f == 0:
                            wait(pe, b_o, u - 1)
                        for o in range(KT):
                            mm = pe.matmul(banks[4 + 2 * par + o][:, 0:n], w2[buf][:, f, o * P:(o + 1) * P],
                                           h[f % 2][:, 0:n], start=f == 0, stop=f == FT - 1)
                        if f == FT - 1:
                            mm.then_inc(b_o_ready, 1)

                    for f in range(FT):
                        up(f)
                        if f:
                            down(f - 1)
                    down(FT - 1)

                def expert(u, par, t):
                    pe.wait_ge(b_w[par], 48 * t + 48)
                    pe.wait_ge(b_xg, u + 1)
                    unit(u, par, SW, lambda k: xg[par][:, k, :], par)

                expert(0, 0, 0)
                expert(1, 1, 0)
                with pe.Fori(1, BLOCKS // 2) as t:
                    for par in range(2):
                        expert(t * 2 + par, par, t)
                if BLOCKS % 2:
                    expert(BLOCKS - 1, 0, BLOCKS // 2)
                pe.wait_ge(b_w[SH], 48 * ((BLOCKS - SH) // 2 + SH * 0 + 1) if SH else 48 * (BLOCKS // 2 + 1))
                with pe.Fori(0, NTB // 2) as t:
                    for j in range(2):
                        unit(t * 2 + (BLOCKS + j), (BLOCKS + j) % 2, TB,
                             lambda k: xT[:, k, bass.ds(t * (2 * TB) + j * TB, TB)], SH)
                pe.wait_ge(b_g_in, 32)
                pe.wait_ge(b_step, 1)
                for o in range(KT):
                    for k in range(2 * KT):
                        mm = pe.matmul(banks[0][:, o * B:(o + 1) * B], g0[:, k, o * P:(o + 1) * P], gi[:, k, :],
                                       start=k == 0, stop=k == 2 * KT - 1)
                mm.then_inc(b_gp, 1)
                pe.wait_ge(b_step, 2)
                for r in range(2):
                    for k in range(KT):
                        mm = pe.matmul(banks[1][:, r * B:(r + 1) * B], g1[:, k, r:r + 1].to_broadcast([P, P]),
                                       gr[:, k, :], start=k == 0, stop=k == KT - 1)
                mm.then_inc(b_gp, 1)

            @block.scalar
            def _(act):
                def unit(u, n):
                    for f in range(FT):
                        act.wait_ge(b_l_ready, FT * u + f + 1)
                        wait(act, b_h, FT * u + f - 1)
                        act.activation(ge[f % 2][:, 0:n], banks[f % 2][:, 0:n], ACT.Gelu_apprx_tanh).then_inc(b_ge, 1)

                unit(0, SW)
                with act.Fori(1, BLOCKS) as u:
                    unit(u, SW)
                with act.Fori(BLOCKS, BLOCKS + NTB) as u:
                    unit(u, TB)
                act.wait_ge(b_step, 5)
                act.activation(z[:, :, :], z[:, :, :], ACT.Exp).then_inc(b_gp, 1)

            @block.vector
            def _(dve):
                def hidden(u, n, f):
                    dve.wait_ge(b_ge, FT * u + f + 1)
                    if f >= 2:
                        pass
                    dve.tensor_tensor(h[f % 2][:, 0:n], banks[2 + f % 2][:, 0:n], ge[f % 2][:, 0:n],
                                      ALU.mult).then_inc(b_h, 1)

                def expert(u, par):
                    for f in range(FT):
                        hidden(u, SW, f)
                    dve.wait_ge(b_o_ready, u + 1)
                    wait(dve, b_o, u)
                    for j in range(SLOTS):
                        s = dve.value_load(slot_sample[0:1, bass.ds(u * SLOTS + j, 1)], min_val=0, max_val=B + SLOTS - 1)
                        for o in range(KT):
                            last = dve.tensor_copy(eo[:, o, bass.ds(s * S, S)], banks[4 + 2 * par + o][:, j * S:(j + 1) * S])
                    last.then_inc(b_o, 1)

                with dve.Fori(0, BLOCKS // 2) as t:
                    for par in range(2):
                        expert(t * 2 + par, par)
                if BLOCKS % 2:
                    expert(BLOCKS - 1, 0)
                with dve.Fori(0, NTB // 2) as t:
                    for j in range(2):
                        u = t * 2 + (BLOCKS + j)
                        for f in range(FT):
                            hidden(u, TB, f)
                        dve.wait_ge(b_o_ready, u + 1)
                        for o in range(KT):
                            last = dve.tensor_copy(hT[:, o, bass.ds(t * (2 * TB) + j * TB, TB)],
                                                   banks[4 + 2 * ((BLOCKS + j) % 2) + o][:, :])
                        last.then_inc(b_o, 1)
                dve.wait_ge(b_o, BLOCKS + NTB)
                dve.tensor_copy(gi[:, 0:KT, :], eo[:, :, 0:N:S])
                dve.tensor_copy(gi[:, KT:2 * KT, :], hT[:, :, 0:N:S]).then_inc(b_step, 1)
                dve.wait_ge(b_gp, 1)
                dve.tensor_scalar(gr[:, :, :], banks[0][:, 0:KT * B].rearrange("p (k b) -> p k b", k=KT), 0.0, None,
                                  ALU.max).then_inc(b_step, 1)
                dve.wait_ge(b_gp, 2)
                dve.tensor_copy(z[:, :, :], banks[1][:, 0:2 * B].rearrange("p (k b) -> p k b", k=2)).then_inc(b_step, 1)
                dve.wait_ge(b_step, 3)
                dve.tensor_tensor(zm[:, :], z[:, 0, :], z[:, 1, :], ALU.max).then_inc(b_step, 1)
                dve.wait_ge(b_step, 4)
                dve.tensor_tensor(z[:, :, :], z[:, :, :], bcast(zm[:, :], 1, 2), ALU.subtract).then_inc(b_step, 1)
                dve.wait_ge(b_gp, 3)
                dve.tensor_tensor(zs[:, :], z[:, 0, :], z[:, 1, :], ALU.add).then_inc(b_step, 1)
                dve.wait_ge(b_step, 6)
                dve.reciprocal(zm[:, :], zs[:, :]).then_inc(b_step, 1)
                dve.wait_ge(b_step, 7)
                dve.tensor_tensor(z[:, :, :], z[:, :, :], bcast(zm[:, :], 1, 2), ALU.mult).then_inc(b_step, 1)
                dve.wait_ge(b_step, 8)
                BS = TB // S
                for o in range(KT):
                    for t in range(NTB):
                        m = o * NTB + t
                        def by(ap):
                            return ap.rearrange("p (b n) -> p b n", n=S)
                        e_in, s_in, tp = (by(x) for x in (eo[:, o, t * TB:(t + 1) * TB], hT[:, o, t * TB:(t + 1) * TB],
                                                          tmp[:, m % 2, :]))
                        wt = [bcast(z[:, r, t * BS:(t + 1) * BS], 2, S) for r in range(2)]
                        dve.tensor_tensor(e_in, e_in, wt[0], ALU.mult)
                        dve.tensor_tensor(tp, s_in, wt[1], ALU.mult).then_inc(b_ztrue, 1)
                        dve.wait_ge(b_ztrue, 2 * m + 1)
                        dve.tensor_tensor(s_in, e_in, tp, ALU.add).then_inc(b_ztrue, 1)


def mixture(nc, io, banks, sb0, sem, xT, hT, ident):
    with ExitStack() as c:
        def sb(name, shape, dt=F32):
            return sb0(name, shape, dt, c)

        rw = sb("rw", [P, KT, EM])
        rb = sb("rb", [P, EM])
        lg = sb("lg", [P, PAIRS, EM])
        cb = sb("cb", [P, PAIRS, EM])
        cbT = sb("cbT", [EM, N])
        gt = sb("gt", [P, PAIRS, EM])
        rank = sb("rank", [P, PAIRS, EM])
        m1 = sb("m1", [P, PAIRS])
        m2 = sb("m2", [P, PAIRS])
        gub = sb("gub", [P, EM, 2 * JT])
        db = sb("db", [EM, D])
        acc = sb("acc", [P, PAIRS, D])
        wg = [sb(f"wg{k}", [P, KT, 2 * IM]) for k in range(2)]
        wd = [sb(f"wd{k}", [P, JT, D]) for k in range(2)]
        ga = [sb(f"ga{k}", [P, TB]) for k in range(2)]
        up = [sb(f"up{k}", [P, TB]) for k in range(2)]
        sg = [sb(f"sg{k}", [P, TB]) for k in range(2)]
        gu = [sb(f"gu{k}", [P, TB]) for k in range(2)]
        ac = [sb(f"ac{k}", [P, JT, TB]) for k in range(2)]
        m_in, m_l_ready, m_l, m_step, m_c = (sem(n) for n in (
            "m_small_in", "m_logits_ready", "m_logits_copied", "m_router_step", "m_combine"))
        m_w = [sem(f"m_w{k}_in") for k in range(2)]
        m_gu_ready, m_gu, m_sg, m_t, m_ac, m_d_ready, m_d = (sem(n) for n in (
            "m_gate_up_ready", "m_gate_up_clipped", "m_sigmoid", "m_product", "m_act", "m_down_ready", "m_down_added"))
        m_ct_ready, m_ct, m_f_ready, m_f = (sem(n) for n in (
            "m_combineT_ready", "m_combineT_copied", "m_final_ready", "m_final_added"))

        with nc.Block() as block:
            @block.sync
            def _(sp):
                def expert(e, par):
                    wait(sp, m_d_ready, NTB * (e - 1))
                    sp.dma_start(wg[par][:, :, :], io["m_guT"][bass.ds(e, 1), :, :].rearrange(
                        "e (k p) n -> p (e k) n", p=P)).then_inc(m_w[par], 16)
                    sp.dma_start(wd[par][:, :, :], io["m_dnT"][bass.ds(e, 1), :, :].rearrange(
                        "e (k p) n -> p (e k) n", p=P)).then_inc(m_w[par], 16)

                sp.dma_start(rw[:, :, :], io["m_rwT"].rearrange("(k p) n -> p k n", p=P)).then_inc(m_in, 16)
                sp.dma_start(rb[:, :], io["m_rb"].partition_broadcast(P)).then_inc(m_in, 16)
                sp.dma_start(gub[:, :, :], io["m_gub"]).then_inc(m_in, 16)
                sp.dma_start(db[:, :], io["m_db"]).then_inc(m_in, 16)
                for e in range(2):
                    expert(e, e)
                with sp.Fori(1, EM // 2) as t:
                    for par in range(2):
                        expert(t * 2 + par, par)

            @block.tensor
            def _(pe):
                pe.wait_ge(m_in, 64)
                for t in range(PAIRS):
                    for k in range(KT):
                        mm = pe.matmul(banks[7][:, t * EM:(t + 1) * EM], hT[:, k, t * P:(t + 1) * P], rw[:, k, :],
                                       start=k == 0, stop=k == KT - 1)
                mm.then_inc(m_l_ready, 1)

                def gate_up(e, tb, par, js):
                    for j in js:
                        n = (e * NTB + tb) * JT + j
                        wait(pe, m_gu, n - 1)
                        for r in range(2):
                            for k in range(KT):
                                mm = pe.matmul(banks[2 * r + j % 2][:, :],
                                               wg[par][:, k, (r * JT + j) * P:(r * JT + j + 1) * P],
                                               hT[:, k, tb * TB:(tb + 1) * TB], start=k == 0, stop=k == KT - 1)
                        mm.then_inc(m_gu_ready, 1)

                def down(n, par, wpar):
                    pe.wait_ge(m_ac, n * JT + JT)
                    for b in range(2):
                        wait(pe, m_d, 2 * (n - 2) + b + 1)
                        for tt in range(2):
                            for j in range(JT):
                                at = (2 * b + tt) * P
                                mm = pe.matmul(banks[4 + 2 * par + b][:, tt * D:(tt + 1) * D], ac[par][:, j, at:at + P],
                                               wd[wpar][:, j, :], start=j == 0, stop=j == JT - 1)
                    mm.then_inc(m_d_ready, 1)

                def two_experts(t):
                    for par in range(2):
                        e = t * 2 + par
                        pe.wait_ge(m_w[par], 32 * t + 32)
                        for tb in range(NTB):
                            n = e * NTB + tb
                            gate_up(e, tb, par, range(0, 2))
                            if not (isinstance(n, int) and n == 0):
                                if isinstance(n, int) and n == 1:
                                    pe.wait_ge(m_l, 1)
                                down(n - 1, (tb + 1) % 2, par if tb else 1 - par)
                            gate_up(e, tb, par, range(2, JT))

                two_experts(0)
                with pe.Fori(1, EM // 2) as t:
                    two_experts(t)
                down(EM * NTB - 1, 1, 1)
                pe.wait_ge(m_c, 1)
                for t in range(PAIRS):
                    if t % 4 == 0 and t:
                        pe.wait_ge(m_ct, t // 4)
                    mm = pe.transpose(banks[0][0:EM, (t % 4) * P:(t % 4 + 1) * P], cb[:, t, :], ident[:, :])
                    if t % 4 == 3:
                        mm.then_inc(m_ct_ready, 1)
                pe.wait_ge(m_ct, PAIRS // 4)
                pe.wait_ge(m_d, 2 * EM * NTB)
                for t in range(NTB):
                    for o in range(KT):
                        n = t * KT + o
                        if n >= 2:
                            pe.wait_ge(m_f, n - 1)
                        pe.matmul(banks[1 + n % 2][:, :], db[:, o * P:(o + 1) * P], cbT[:, t * TB:(t + 1) * TB],
                                  start=True, stop=False)
                        for j in range(TB // P):
                            mm = pe.matmul(banks[1 + n % 2][:, j * P:(j + 1) * P], acc[:, t * 4 + j, o * P:(o + 1) * P],
                                           ident[:, :], start=False, stop=j == TB // P - 1)
                        mm.then_inc(m_f_ready, 1)

            @block.gpsimd
            def _(pool):
                def tile(n, j, par):
                    pool.wait_ge(m_t, n * JT + j + 1)
                    wait(pool, m_d_ready, n - 1)
                    pool.tensor_tensor(ac[par][:, j, :], gu[j % 2][:, :], sg[j % 2][:, :], ALU.mult).then_inc(m_ac, 1)

                def two(t):
                    for par in range(2):
                        for j in range(JT):
                            tile(t * 2 + par, j, par)

                two(0)
                with pool.Fori(1, EM * NTB // 2) as t:
                    two(t)

            @block.scalar
            def _(act):
                act.wait_ge(m_step, 100)
                act.activation(lg[:, :, :], lg[:, :, :], ACT.Exp).then_inc(m_step, 1)

                def step(n):
                    for j in range(JT):
                        m = n * JT + j
                        act.wait_ge(m_gu, m + 1)
                        wait(act, m_ac, m - 1)
                        act.activation(sg[j % 2][:, :], ga[j % 2][:, :], ACT.Sigmoid, scale=SWIGLU_ALPHA).then_inc(m_sg, 1)

                step(0)
                with act.Fori(1, EM * NTB) as n:
                    step(n)

            @block.vector
            def _(dve):
                cnt = [0]

                def then(ins, by=1):
                    ins.then_inc(m_step, by)
                    cnt[0] += by
                    dve.wait_ge(m_step, cnt[0])

                dve.memset(acc[:, :, :], 0.0).then_inc(m_step, 1)
                cnt[0] = 1
                dve.wait_ge(m_in, 64)
                then(dve.tensor_scalar(gub[:, :, JT:2 * JT], gub[:, :, JT:2 * JT], 1.0, None, ALU.add))
                dve.wait_ge(m_l_ready, 1)
                then(dve.tensor_tensor(lg[:, :, :], banks[7][:, 0:PAIRS * EM].rearrange("p (t e) -> p t e", e=EM),
                                       bcast(rb[:, :], 1, PAIRS), ALU.add))
                dve.sem_inc(m_l, 1)
                then(dve.memset(rank[:, :, :], 0.0))
                for i in range(EM):
                    li = lg[:, :, i:i + 1]
                    if i:
                        dve.tensor_tensor(gt[:, :, 0:i], li.to_broadcast([P, PAIRS, i]), lg[:, :, 0:i], ALU.is_gt)
                    if i < EM - 1:
                        dve.tensor_tensor(gt[:, :, i + 1:EM], li.to_broadcast([P, PAIRS, EM - 1 - i]), lg[:, :, i + 1:EM],
                                          ALU.is_ge)
                    then(dve.memset(gt[:, :, i:i + 1], 0.0))
                    then(dve.tensor_tensor(rank[:, :, :], rank[:, :, :], gt[:, :, :], ALU.add))
                then(dve.tensor_scalar(rank[:, :, :], rank[:, :, :], float(TOP_K), None, ALU.is_lt))
                then(dve.tensor_reduce(m1[:, :], lg[:, :, :], AX.X, ALU.max))
                then(dve.tensor_tensor(lg[:, :, :], lg[:, :, :], bcast(m1[:, :], 2, EM), ALU.subtract), 100 - cnt[0])
                dve.wait_ge(m_step, 101)
                cnt[0] = 101
                then(dve.tensor_tensor(lg[:, :, :], lg[:, :, :], rank[:, :, :], ALU.mult))
                then(dve.tensor_reduce(m1[:, :], lg[:, :, :], AX.X, ALU.add))
                then(dve.reciprocal(m2[:, :], m1[:, :]))
                then(dve.tensor_tensor(cb[:, :, :], lg[:, :, :], bcast(m2[:, :], 2, EM), ALU.mult))
                dve.sem_inc(m_c, 1)

                def clip(e, n, js):
                    for j in js:
                        m = n * JT + j
                        dve.wait_ge(m_gu_ready, m + 1)
                        wait(dve, m_t, m - 1)
                        dve.tensor_scalar(ga[j % 2][:, :], banks[j % 2][:, :],
                                          gub[:, bass.ds(e, 1), j:j + 1].rearrange("p a b -> p (a b)"), LIMIT,
                                          ALU.add, ALU.min)
                        dve.tensor_scalar(up[j % 2][:, :], banks[2 + j % 2][:, :],
                                          gub[:, bass.ds(e, 1), JT + j:JT + j + 1].rearrange("p a b -> p (a b)"), 1.0 - LIMIT,
                                          ALU.add, ALU.max).then_inc(m_gu, 1)

                def product(n, j):
                    m = n * JT + j
                    dve.wait_ge(m_sg, m + 1)
                    wait(dve, m_ac, m - 1)
                    dve.scalar_tensor_tensor(gu[j % 2][:, :], up[j % 2][:, :], 1.0 + LIMIT, ga[j % 2][:, :],
                                             ALU.min, ALU.mult).then_inc(m_t, 1)

                def add_down(e, n, tb, par):
                    dve.wait_ge(m_d_ready, n + 1)
                    wait(dve, m_d, 2 * n)
                    for b in range(2):
                        for tt in range(2):
                            t = 4 * tb + 2 * b + tt
                            last = dve.scalar_tensor_tensor(
                                acc[:, t, :], banks[4 + 2 * par + b][:, tt * D:(tt + 1) * D],
                                cb[:, t, bass.ds(e, 1)], acc[:, t, :], ALU.mult, ALU.add)
                        last.then_inc(m_d, 1)

                def two_experts(t):
                    for par in range(2):
                        e = t * 2 + par
                        for tb in range(NTB):
                            n = e * NTB + tb
                            for j in range(JT):
                                clip(e, n, (j,))
                                if j == 2 and not (isinstance(n, int) and n == 0):
                                    add_down(e if tb else e - 1, n - 1, (tb - 1) % NTB, (tb + 1) % 2)
                                product(n, j)

                two_experts(0)
                with dve.Fori(1, EM // 2) as t:
                    two_experts(t)
                add_down(EM - 1, EM * NTB - 1, NTB - 1, 1)
                for t in range(PAIRS // 4):
                    dve.wait_ge(m_ct_ready, t + 1)
                    dve.tensor_copy(cbT[:, t * TB:(t + 1) * TB], banks[0][0:EM, :]).then_inc(m_ct, 1)
                for t in range(NTB):
                    for o in range(KT):
                        n = t * KT + o
                        dve.wait_ge(m_f_ready, n + 1)
                        at = xT[:, o, t * TB:(t + 1) * TB]
                        dve.tensor_tensor(at, banks[1 + n % 2][:, :], at, ALU.add).then_inc(m_f, 1)


def lora_ffn(nc, io, banks, sb0, sem, xT, zT, oh_lora):
    with ExitStack() as c:
        def sb(name, shape, dt=F32):
            return sb0(name, shape, dt, c)

        wi = sb("wi", [P, KT, FF])
        wo = sb("l_wo", [P, FT, D])
        cia = sb("cia", [RL, D])
        cib = sb("cib", [RL, FF])
        coa = sb("coa", [RL, FF])
        cob = sb("cob", [RL, D])
        eia = sb("eia", [P, KT, P])
        eib = sb("eib", [P, FF])
        eoa = sb("eoa", [P, FT, P])
        eob = sb("eob", [P, D])
        low = sb("low", [P, TB])
        lowo = sb("lowo", [P, TB])
        hid = [sb(f"hid{k}", [P, TB]) for k in range(4)]
        l_in, l_f_ready, l_f, l_low_ready, l_low, l_h_ready, l_h, l_lo_ready, l_lo, l_o_ready, l_o = (
            sem(n) for n in ("l_in", "l_fold_ready", "l_folded", "l_low_ready", "l_low_masked", "l_hidden_ready",
                             "l_relu", "l_lowo_ready", "l_lowo_masked", "l_out_ready", "l_out_copied"))
        NF = KT * 2 + FT // 2

        with nc.Block() as block:
            @block.sync
            def _(sp):
                for dst, name in ((cia, "l_cia"), (cib, "l_cibT"), (coa, "l_coa"), (cob, "l_cobT"), (eib, "l_eibT"), (eob, "l_eobT")):
                    sp.dma_start(dst[:, :], io[name]).then_inc(l_in, 16)
                for dst, name in ((wi, "l_wiT"), (wo, "l_woT"), (eia, "l_eiaT"), (eoa, "l_eoaT")):
                    sp.dma_start(dst[:, :, :], io[name].rearrange("(k p) n -> p k n", p=P)).then_inc(l_in, 16)

            @block.tensor
            def _(pe):
                pe.wait_ge(l_in, 160)
                n = 0
                for k in range(KT):
                    for f in range(2):
                        if n >= 2:
                            pe.wait_ge(l_f, n - 1)
                        pe.matmul(banks[n % 2][:, :], cia[:, k * P:(k + 1) * P], cib[:, f * 512:(f + 1) * 512],
                                  start=True, stop=True).then_inc(l_f_ready, 1)
                        n += 1
                for f in range(FT // 2):
                    pe.wait_ge(l_f, n - 1)
                    for g in range(2):
                        mm = pe.matmul(banks[n % 2][:, g * D:(g + 1) * D], coa[:, (2 * f + g) * P:(2 * f + g + 1) * P],
                                       cob[:, :], start=True, stop=True)
                    mm.then_inc(l_f_ready, 1)
                    n += 1
                pe.wait_ge(l_f, NF)
                with pe.Fori(0, NTB) as tb:
                    def x(k):
                        return xT[:, k, bass.ds(tb * TB, TB)]
                    for k in range(KT):
                        mm = pe.matmul(banks[2][:, :], eia[:, k, :], x(k), start=k == 0, stop=k == KT - 1)
                    mm.then_inc(l_low_ready, 1)
                    pe.wait_ge(l_low, tb + 1)

                    def second(f):
                        pe.wait_ge(l_h, FT * tb + (f + 1))
                        mm = pe.matmul(banks[3][:, :], eoa[:, f, :], hid[f % 4][:, :], start=f == 0, stop=f == FT - 1)
                        if f == FT - 1:
                            mm.then_inc(l_lo_ready, 1)
                        for o in range(KT):
                            pe.matmul(banks[4 + o][:, :], wo[:, f, o * P:(o + 1) * P], hid[f % 4][:, :],
                                      start=f == 0, stop=False)

                    for f in range(FT):
                        if f >= 2:
                            pe.wait_ge(l_h, FT * tb + (f - 1))
                        for k in range(KT):
                            pe.matmul(banks[f % 2][:, :], wi[:, k, f * P:(f + 1) * P], x(k), start=k == 0, stop=False)
                        pe.matmul(banks[f % 2][:, :], eib[:, f * P:(f + 1) * P], low[:, :], start=False,
                                  stop=True).then_inc(l_h_ready, 1)
                        if f:
                            second(f - 1)
                    second(FT - 1)
                    pe.wait_ge(l_lo, tb + 1)
                    for o in range(KT):
                        mm = pe.matmul(banks[4 + o][:, :], eob[:, o * P:(o + 1) * P], lowo[:, :], start=False, stop=True)
                    mm.then_inc(l_o_ready, 1)
                    pe.wait_ge(l_o, tb + 1)

            @block.scalar
            def _(act):
                with act.Fori(0, NTB) as tb:
                    for f in range(FT):
                        act.wait_ge(l_h_ready, FT * tb + (f + 1))
                        act.activation(hid[f % 4][:, :], banks[f % 2][:, :], ACT.Relu).then_inc(l_h, 1)

            @block.vector
            def _(dve):
                dve.wait_ge(l_in, 160)
                n = 0
                for k in range(KT):
                    for f in range(2):
                        dve.wait_ge(l_f_ready, n + 1)
                        at = wi[:, k, f * 512:(f + 1) * 512]
                        dve.scalar_tensor_tensor(at, banks[n % 2][:, :], 2.0, at, ALU.mult, ALU.add).then_inc(l_f, 1)
                        n += 1
                for f in range(FT // 2):
                    dve.wait_ge(l_f_ready, n + 1)
                    at = wo[:, 2 * f:2 * f + 2, :]
                    dve.scalar_tensor_tensor(at, banks[n % 2][:, :].rearrange("p (g n) -> p g n", g=2), 2.0, at, ALU.mult,
                                             ALU.add).then_inc(l_f, 1)
                    n += 1
                with dve.Fori(0, NTB) as tb:
                    m = bcast(oh_lora[:, bass.ds(tb * (TB // S), TB // S)], 2, S)
                    for ready, bank, dst, done in ((l_low_ready, 2, low, l_low), (l_lo_ready, 3, lowo, l_lo)):
                        dve.wait_ge(ready, tb + 1)
                        dve.tensor_tensor(dst[:, :].rearrange("p (b n) -> p b n", n=S),
                                          banks[bank][:, :].rearrange("p (b n) -> p b n", n=S), m, ALU.mult).then_inc(done, 1)
                    dve.wait_ge(l_o_ready, tb + 1)
                    for o in range(KT):
                        last = dve.tensor_copy(zT[:, o, bass.ds(tb * TB, TB)], banks[4 + o][:, :])
                    last.then_inc(l_o, 1)


def attention1(nc, io, banks, sb0, sem, xT, zT, ident, mask):
    with ExitStack() as c:
        def sb(name, shape, dt=F32):
            return sb0(name, shape, dt, c)

        HT = P // HD1
        wat = sb("wat", [P, KT, 3 * D])
        bat = sb("bat", [P, 4])
        bv = sb("bv", [P, D])
        fac = sb("fac", [P, 2, S])
        hm = sb("hm", [P, HT])
        wp = sb("wp", [P, KT, D])
        bp = sb("bp", [P, KT])
        zs = [sb(f"zs{k}", [P, KT, P]) for k in range(2)]
        qT = [sb(f"qT{k}", [P, 2, P]) for k in range(2)]
        kT = sb("kT", [P, 2, P])
        kpad = sb("k1pad", [P, 2, HT, P])
        v = [sb(f"vp{k}", [P, HEADS, 32]) for k in range(2)]
        sc = sb("sc1", [P, HEADS, S])
        ex = sb("ex1", [P, HEADS, S])
        mx = sb("mx1", [P, HEADS])
        sm = sb("sm1", [P, HEADS])
        ri = sb("ri1", [P, HEADS])
        pr = sb("pr1", [P, HEADS, P])
        prT = sb("prT1", [P, HEADS, P])
        ctxT = sb("ctxT1", [P, 2, P])
        n_in, n_zero, n_zs, n_qk_ready, n_qk, n_kp, n_v_ready, n_v, n_vm = (sem(n) for n in (
            "n_in", "n_zeroed", "n_z_staged", "n_qk_ready", "n_qk_scaled", "n_k_spread", "n_v_ready", "n_v_copied", "n_v_moved"))
        n_s_ready, n_s, n_mx, n_sub, n_exp, n_sum, n_rec, n_p0, n_p, n_tp_ready, n_tp, n_c_ready, n_c, n_o_ready, n_o = (
            sem(n) for n in ("n_s_ready", "n_s_masked", "n_max", "n_subtracted", "n_exp", "n_sum", "n_recip", "n_probs_half", "n_probs",
                             "n_trp_ready", "n_trp_copied", "n_ctx_ready", "n_ctx_copied", "n_out_ready", "n_out_added"))

        with nc.Block() as block:
            @block.sync
            def _(sp):
                for dst, name in ((bat, "n_bat"), (hm, "n_hm"), (bp, "n_bp")):
                    sp.dma_start(dst[:, :], io[name]).then_inc(n_in, 16)
                sp.dma_start(bv[:, :], io["n_bv"].partition_broadcast(P)).then_inc(n_in, 16)
                sp.dma_start(fac[:, :, :], io["n_fac"]).then_inc(n_in, 16)
                for dst, name in ((wat, "n_waT"), (wp, "n_wpT")):
                    sp.dma_start(dst[:, :, :], io[name].rearrange("(k p) n -> p k n", p=P)).then_inc(n_in, 16)

            @block.gpsimd
            def _(pool):
                for t in v:
                    pool.memset(t[:, :, :], 0.0).then_inc(n_zero, 1)
                pool.memset(pr[:, :, :], 0.0).then_inc(n_zero, 1)
                pool.wait_ge(n_in, 112)

                def step(i, par):
                    if live(i + 1):
                        p = i + 1
                        wait(pool, n_v_ready, p - 1)
                        pool.tensor_copy(zs[1 - par][:, :, :], zT[:, :, bass.ds(p * P, P)]).then_inc(n_zs, 1)
                    if live(i - 2):
                        pool.wait_ge(n_rec, i - 1)
                        if isinstance(i, int) and i == 2:
                            pool.wait_ge(n_zero, 3)
                        wait(pool, n_tp_ready, 4 * (i - 3) + 4)
                        pool.wait_ge(n_kp, i if live(i - 1) else PAIRS)
                        if live(i + 1):
                            pool.wait_ge(n_zs, i + 2)
                        pool.tensor_tensor(pr[0:S, :, 0:S], ex[0:S, :, :], bcast(ri[0:S, :], 2, S), ALU.mult).then_inc(n_p0, 1)
                        pool.wait_ge(n_p0, i - 1)
                        pool.tensor_tensor(pr[S:P, :, S:P], ex[S:P, :, :], bcast(ri[S:P, :], 2, S), ALU.mult).then_inc(n_p, 1)
                        pool.wait_ge(n_p, i - 1)
                    if live(i):
                        wait(pool, n_s_ready, 4 * (i - 1) + 4)
                        pool.wait_ge(n_qk, i + 1)
                        for t in range(2):
                            last = pool.tensor_tensor(kpad[:, t, :, :], bcast(kT[:, t, :], 1, HT), bcast(hm[:, :], 2, P), ALU.mult)
                        last.then_inc(n_kp, 1)

                pipeline(pool, step)

            @block.tensor
            def _(pe):
                pe.wait_ge(n_in, 112)

                def step(i, par):
                    if live(i - 1):
                        wait(pe, n_v, i - 1)
                        for k in range(KT):
                            mm = pe.matmul(banks[2][:, 0:D], zs[1 - par][:, k, :], wat[:, k, 2 * D:3 * D], start=k == 0,
                                           stop=k == KT - 1)
                        mm.then_inc(n_v_ready, 1)
                    if live(i):
                        pe.wait_ge(n_zs, i + 1)
                        wait(pe, n_qk, i)
                        for t in range(4):
                            for k in range(KT):
                                mm = pe.matmul(banks[1][:, t * P:(t + 1) * P], wat[:, k, t * P:(t + 1) * P], zs[par][:, k, :],
                                               start=k == 0, stop=k == KT - 1)
                        mm.then_inc(n_qk_ready, 1)
                    if live(i - 3):
                        p = i - 3
                        pe.wait_ge(n_c, p + 1)
                        wait(pe, n_o, p)
                        for o in range(KT):
                            for k in range(KT):
                                mm = pe.matmul(banks[0][:, o * P:(o + 1) * P], wp[:, k, o * P:(o + 1) * P], ctxT[:, k, :],
                                               start=k == 0, stop=k == KT - 1)
                        mm.then_inc(n_o_ready, 1)
                    if live(i - 2):
                        p = i - 2
                        pe.wait_ge(n_p, p + 1)
                        for f in range(4):
                            wait(pe, n_tp, 4 * p + f - 1)
                            for j in range(4):
                                mm = pe.transpose(banks[6 + f % 2][:, j * P:(j + 1) * P], pr[:, 4 * f + j, :], ident[:, :])
                            mm.then_inc(n_tp_ready, 1)
                    if live(i - 1):
                        p = i - 1
                        pe.wait_ge(n_kp, p + 1)
                        for f in range(4):
                            wait(pe, n_s, 4 * p + f - 1)
                            pe.matmul(banks[4 + f % 2][:, :], qT[1 - par][:, f // 2, :],
                                      kpad[:, f // 2, 4 * (f % 2):4 * (f % 2) + 4, :], start=True, stop=True).then_inc(n_s_ready, 1)
                    if live(i - 2):
                        p = i - 2
                        pe.wait_ge(n_tp, 4 * p + 4)
                        for t in range(2):
                            for q in range(4):
                                for s in range(2):
                                    h = 8 * t + 2 * q + s
                                    mm = pe.matmul(banks[3][32 * q:32 * q + 32, t * P:(t + 1) * P], v[par][:, h, :],
                                                   prT[:, h, :], start=s == 0, stop=s == 1)
                        mm.then_inc(n_c_ready, 1)

                pipeline(pe, step)

            @block.scalar
            def _(act):
                def step(i, par):
                    if live(i - 2):
                        p = i - 2
                        for f in range(4):
                            act.wait_ge(n_tp_ready, 4 * p + f + 1)
                            act.activation(prT[:, 4 * f:4 * f + 4, :], banks[6 + f % 2][:, :].rearrange(
                                "p (t n) -> p t n", n=P), ACT.Copy).then_inc(n_tp, 1)
                        act.wait_ge(n_c_ready, p + 1)
                        act.activation(ctxT[:, :, :], banks[3][:, 0:2 * P].rearrange("p (t n) -> p t n", n=P),
                                       ACT.Copy).then_inc(n_c, 1)
                    if live(i - 1):
                        act.wait_ge(n_sub, i)
                        wait(act, n_p, i - 1)
                        act.activation(ex[:, :, :], sc[:, :, :], ACT.Exp).then_inc(n_exp, 1)

                pipeline(act, step)

            @block.vector
            def _(dve):
                dve.wait_ge(n_in, 112)

                def step(i, par):
                    if live(i - 1):
                        dve.wait_ge(n_v_ready, i)
                        if isinstance(i, int) and i == 1:
                            dve.wait_ge(n_zero, 2)
                        for s in range(2):
                            vv = v[1 - par][:, s:HEADS:2, HD1 * s:HD1 * s + HD1]
                            last = dve.tensor_tensor(
                                vv, banks[2][:, 0:D].rearrange("p (h s d) -> p h s d", s=2, d=HD1)[:, :, s, :],
                                bv[:, :].rearrange("p (h s d) -> p h s d", s=2, d=HD1)[:, :, s, :], ALU.add)
                        last.then_inc(n_v, 1)
                    if live(i):
                        dve.wait_ge(n_qk_ready, i + 1)
                        wait(dve, n_kp, i)
                        for t in range(4):
                            dst = (qT[par] if t < 2 else kT)[:, t % 2, :]
                            last = dve.scalar_tensor_tensor(
                                dst.rearrange("p (s n) -> p s n", s=2),
                                banks[1][:, t * P:(t + 1) * P].rearrange("p (s n) -> p s n", s=2), bat[:, t:t + 1],
                                bcast(fac[:, t // 2, :], 1, 2), ALU.add, ALU.mult)
                        last.then_inc(n_qk, 1)
                    if live(i - 2):
                        p = i - 2
                        dve.wait_ge(n_exp, p + 1)
                        wait(dve, n_p, p)
                        dve.tensor_reduce(sm[:, :], ex[:, :, :], AX.X, ALU.add).then_inc(n_sum, 1)
                        dve.wait_ge(n_sum, p + 1)
                        dve.reciprocal(ri[:, :], sm[:, :]).then_inc(n_rec, 1)
                    if live(i - 3):
                        p = i - 3
                        dve.wait_ge(n_o_ready, p + 1)
                        for o in range(KT):
                            at = xT[:, o, bass.ds(p * P, P)]
                            last = dve.scalar_tensor_tensor(at, banks[0][:, o * P:(o + 1) * P], bp[:, o:o + 1], at,
                                                            ALU.add, ALU.add)
                        last.then_inc(n_o, 1)
                    if live(i - 1):
                        p = i - 1
                        wait(dve, n_exp, p)
                        for f in range(4):
                            dve.wait_ge(n_s_ready, 4 * p + f + 1)
                            for s in range(2):
                                rows = slice(S * s, S * s + S)
                                last = dve.tensor_tensor(
                                    sc[rows, 4 * f:4 * f + 4, :],
                                    banks[4 + f % 2][rows, :].rearrange("p (h n) -> p h n", n=P)[:, :, S * s:S * s + S],
                                    bcast(mask[rows, :], 1, 4), ALU.add)
                            last.then_inc(n_s, 1)
                        dve.wait_ge(n_s, 4 * p + 4)
                        dve.tensor_reduce(mx[:, :], sc[:, :, :], AX.X, ALU.max).then_inc(n_mx, 1)
                        dve.wait_ge(n_mx, p + 1)
                        dve.tensor_tensor(sc[:, :, :], sc[:, :, :], bcast(mx[:, :], 2, S), ALU.subtract).then_inc(n_sub, 1)

                pipeline(dve, step)


def adapter_ffn(nc, io, banks, sb0, sem, xT, oh_lang, oh_lang10, out):
    with ExitStack() as c:
        def sb(name, shape, dt=F32):
            return sb0(name, shape, dt, c)

        BS = TB // S
        w1 = sb("f_w1", [P, KT, LANG * A2])
        b1 = sb("f_b1", [P, LT])
        w2 = sb("f_w2", [P, LT, D])
        tab = sb("f_tab", [LANG, 3, D])
        wt = sb("f_wt", [P, KT, D])
        vr = sb("f_vr", [32, D])
        ct = sb("f_ct", [32, D])
        fb = sb("f_b", [P, KT])
        ones = sb("f_ones", [P, P])
        ps = sb("f_ps", [P, 3, KT, B])
        hl = [sb(f"f_h{k}", [P, TB]) for k in range(LT)]
        r = sb("f_r", [P, KT, TB])
        sq = sb("f_sq", [P, KT, TB])
        rstd = sb("f_rstd", [P, TB])

        (f_in, f_t_ready, f_t, f_w_ready, f_w, f_h_ready, f_h, f_hm, f_a_ready, f_a, f_r, f_m_ready, f_cn, f_sq,
         f_v_ready, f_sd, f_rs, f_n, f_o_ready, f_o) = (sem(n) for n in (
             "f_in", "f_tables_ready", "f_tables", "f_fold_ready", "f_folded", "f_h_ready", "f_relu", "f_masked",
             "f_adapter_ready", "f_biased", "f_residual", "f_mean_ready", "f_centred", "f_squared", "f_var_ready",
             "f_std", "f_rstd", "f_normed", "f_out_ready", "f_out_added"))
        f_st = sem("f_stored")

        with nc.Block() as block:
            @block.sync
            def _(sp):
                for dst, name in ((b1, "f_b1"), (vr, "f_vrT"), (ct, "f_cT"), (fb, "f_b"), (ones, "f_ones")):
                    sp.dma_start(dst[:, :], io[name]).then_inc(f_in, 16)
                sp.dma_start(tab[:, :, :], io["f_tab"]).then_inc(f_in, 16)
                for dst, name in ((w1, "f_w1"), (w2, "f_w2"), (wt, "f_wT")):
                    sp.dma_start(dst[:, :, :], io[name].rearrange("(k p) n -> p k n", p=P)).then_inc(f_in, 16)
                for t in range(NTB):
                    sp.wait_ge(f_o, t + 1)
                    sp.dma_start(out[:, t * TB:(t + 1) * TB].rearrange("(k p) n -> p k n", p=P),
                                 xT[:, :, t * TB:(t + 1) * TB]).then_inc(f_st, 16)
                sp.wait_ge(f_st, 16 * NTB)

            @block.tensor
            def _(pe):
                pe.wait_ge(f_in, 144)
                for k in range(KT):
                    mm = pe.matmul(banks[0][:, k * D:(k + 1) * D], vr[:, k * P:(k + 1) * P], ct[:, :], start=True, stop=True)
                mm.then_inc(f_w_ready, 1)
                for w in range(3):
                    for k in range(KT):
                        at = (w * KT + k) * B
                        mm = pe.matmul(banks[1][:, at:at + B], tab[:, w, k * P:(k + 1) * P], oh_lang10[:, :],
                                       start=True, stop=True)
                mm.then_inc(f_t_ready, 1)
                pe.wait_ge(f_w, 1)
                pe.wait_ge(f_t, 1)
                with pe.Fori(0, NTB) as tb:
                    for j in range(LT):
                        if j >= 2:
                            pe.wait_ge(f_h, LT * tb + (j - 1))
                        for k in range(KT):
                            mm = pe.matmul(banks[j % 2][:, :], w1[:, k, j * P:(j + 1) * P], xT[:, k, bass.ds(tb * TB, TB)],
                                           start=k == 0, stop=k == KT - 1)
                        mm.then_inc(f_h_ready, 1)
                    for j in range(LT):
                        pe.wait_ge(f_hm, LT * tb + (j + 1))
                        for o in range(KT):
                            mm = pe.matmul(banks[2 + o][:, :], w2[:, j, o * P:(o + 1) * P], hl[j][:, :], start=j == 0,
                                           stop=j == LT - 1)
                    mm.then_inc(f_a_ready, 1)
                    pe.wait_ge(f_r, tb + 1)
                    for k in range(KT):
                        mm = pe.matmul(banks[4][:, :], ones[:, :], r[:, k, :], start=k == 0, stop=k == KT - 1)
                    mm.then_inc(f_m_ready, 1)
                    pe.wait_ge(f_sq, tb + 1)
                    for k in range(KT):
                        mm = pe.matmul(banks[5][:, :], ones[:, :], sq[:, k, :], start=k == 0, stop=k == KT - 1)
                    mm.then_inc(f_v_ready, 1)
                    pe.wait_ge(f_n, tb + 1)
                    for o in range(KT):
                        for k in range(KT):
                            mm = pe.matmul(banks[6 + o][:, :], wt[:, k, o * P:(o + 1) * P], r[:, k, :], start=k == 0,
                                           stop=k == KT - 1)
                    mm.then_inc(f_o_ready, 1)
                    pe.wait_ge(f_o, tb + 1)

            @block.scalar
            def _(act):
                act.wait_ge(f_in, 144)
                with act.Fori(0, NTB) as tb:
                    for j in range(LT):
                        act.wait_ge(f_h_ready, LT * tb + (j + 1))
                        act.activation(hl[j][:, :], banks[j % 2][:, :], ACT.Relu, bias=b1[:, j:j + 1]).then_inc(f_h, 1)
                    act.wait_ge(f_cn, tb + 1)
                    act.activation(sq[:, :, :], r[:, :, :], ACT.Square).then_inc(f_sq, 1)
                    act.wait_ge(f_rs, tb * 2 + 1)
                    act.activation(rstd[:, :], rstd[:, :], ACT.Sqrt).then_inc(f_sd, 1)

            @block.gpsimd
            def _(pool):
                with pool.Fori(0, NTB) as tb:
                    for j in range(LT):
                        pool.wait_ge(f_h, LT * tb + (j + 1))
                        hj = hl[j][:, :].rearrange("p (b n) -> p b n", n=S)
                        pool.tensor_tensor(hj, hj, bcast(oh_lang[:, j, bass.ds(tb * BS, BS)], 2, S), ALU.mult).then_inc(f_hm, 1)

            @block.vector
            def _(dve):
                dve.wait_ge(f_in, 144)
                dve.wait_ge(f_w_ready, 1)
                dve.tensor_tensor(wt[:, :, :], banks[0][:, :].rearrange("p (k n) -> p k n", k=KT), wt[:, :, :],
                                  ALU.add).then_inc(f_w, 1)
                dve.wait_ge(f_t_ready, 1)
                dve.tensor_copy(ps[:, :, :, :], banks[1][:, 0:3 * KT * B].rearrange("p (w k b) -> p w k b", w=3, k=KT)).then_inc(f_t, 1)
                dve.wait_ge(f_t, 1)

                def by(ap):
                    return ap.rearrange("p (b n) -> p b n", n=S)

                with dve.Fori(0, NTB // 2) as t2:
                    for par in range(2):
                        tb = t2 * 2 + par

                        def of(w, k):
                            return bcast(ps[:, w, k, bass.ds(tb * BS, BS)], 2, S)

                        dve.wait_ge(f_a_ready, tb + 1)
                        for k in range(KT):
                            last = dve.tensor_tensor(by(r[:, k, :]), by(banks[2 + k][:, :]), of(0, k), ALU.add)
                        last.then_inc(f_a, 1)
                        dve.wait_ge(f_a, tb * 2 + 1)
                        dve.tensor_tensor(r[:, :, :], r[:, :, :], xT[:, :, bass.ds(tb * TB, TB)], ALU.add).then_inc(f_r, 1)
                        dve.wait_ge(f_m_ready, tb + 1)
                        for k in range(KT):
                            last = dve.tensor_tensor(r[:, k, :], r[:, k, :], banks[4][:, :], ALU.subtract)
                        last.then_inc(f_cn, 1)
                        dve.wait_ge(f_v_ready, tb + 1)
                        dve.tensor_scalar(rstd[:, :], banks[5][:, :], EPS, None, ALU.add).then_inc(f_rs, 1)
                        dve.wait_ge(f_sd, tb + 1)
                        dve.reciprocal(rstd[:, :], rstd[:, :]).then_inc(f_rs, 1)
                        dve.wait_ge(f_rs, tb * 2 + 2)
                        for k in range(KT):
                            last = dve.tensor_tensor(r[:, k, :], r[:, k, :], rstd[:, :], ALU.mult)
                        last.then_inc(f_a, 1)
                        dve.wait_ge(f_a, tb * 2 + 2)
                        for k in range(KT):
                            last = dve.tensor_tensor(by(r[:, k, :]), by(r[:, k, :]), of(1, k), ALU.mult)
                        last.then_inc(f_t, 1)
                        dve.wait_ge(f_t, tb + 2)
                        for k in range(KT):
                            last = dve.tensor_tensor(by(r[:, k, :]), by(r[:, k, :]), of(2, k), ALU.add)
                        last.then_inc(f_n, 1)
                        dve.wait_ge(f_o_ready, tb + 1)
                        for k in range(KT):
                            at = xT[:, k, bass.ds(tb * TB, TB)]
                            last = dve.scalar_tensor_tensor(at, banks[6 + k][:, :], fb[:, k:k + 1], at, ALU.add, ALU.add)
                        last.then_inc(f_o, 1)


def constants():
    f = np.float32
    pos = np.arange(S, dtype=f)
    half = HD0 // 2
    scale = f(10000.0) ** (f(2.0) * np.arange(half, dtype=f) / f(HD0))
    ang = (pos[:, None] / scale).astype(f)
    cos, sin = np.cos(ang), np.sin(ang)
    cs, sn = np.concatenate([cos, cos], 1), np.concatenate([-sin, sin], 1)
    rope = np.stack([cs / 8, sn / 8, cs, sn], 1).astype(f)
    theta = f(1.0) / f(10000.0) ** (f(2.0) * np.arange(HD1 // 2, dtype=f) / f(HD1))
    ang1 = np.arange(1, S + 1, dtype=f)[:, None] * theta
    ang1 = np.concatenate([ang1, ang1], 1)
    fac = (np.cos(ang1) + np.sin(ang1)).astype(f).T
    fac = np.tile(fac, (P // HD1, 1))
    p = np.arange(P)
    cols = np.zeros((P, 16), f)
    cols[:, 0] = p
    cols[:, 1] = p // RL
    for k in range(LT):
        cols[:, 2 + k] = (k * P + p) // A2
    q = np.arange(P)[:, None] % S
    low = np.arange(S)[None] <= q
    ar = lambda n: np.arange(n, dtype=f)
    return {
        "ident": np.eye(P, dtype=f),
        "mask0": np.where(low, 0.0, -1e10).astype(f),
        "mask1": np.where(low, 0.0, -3e38).astype(f),
        "cols": cols,
        "rope": np.tile(rope, (2, 1, 1)),
        "rt_es": np.broadcast_to(ar(E2)[:, None], (E2, B))[None],
        "rt_j8": np.broadcast_to(SLOTS * ar(B // SLOTS)[None], (E2, B // SLOTS))[None],
        "rt_ee": np.tril(np.ones((E2, E2), f), -1)[None],
        "rt_ll": np.tril(np.ones((B, B), f), -1)[None],
        "rt_q": ar(BLOCKS * SLOTS)[None],
        "rt_em": (B + ar(BLOCKS * SLOTS) % SLOTS)[None],
        "rt_sm": (ar(B)[None] - (B + ar(BLOCKS * SLOTS) % SLOTS)[:, None])[None],
        "rt_kk": ar(BLOCKS)[None],
        "n_fac": np.stack([fac / 4, fac], 1),
        "n_hm": (p[:, None] // HD1 == np.arange(P // HD1)[None]).astype(f),
        "f_ones": np.full((P, P), 1.0 / D, f),
    }


def layouts(i):
    T = lambda a: np.swapaxes(a, -1, -2)
    cols = lambda a: a.reshape(-1, P).T
    return {
        "xT": i["x"].reshape(N, D).T,
        "idx": np.stack([i["itok_B_0_7"], i["itok_B_0_2"], i["itok_B_0_8"]]),
        "c0_wT": T(i["L0_cond_weight"]), "c0_bias": i["L0_cond_bias"],
        "a0_wqkv": i["L0_attn_wqkv"], "a0_wo": i["L0_attn_wo"],
        **{f"c2_{n}": i[f"L0_cond2_{n}"] for n in ("Wi0", "Wi1", "Wo", "sWi0", "sWi1", "sWo", "g0", "g1")},
        "m_rwT": i["L0_ffn_router_weight"].T, "m_rb": i["L0_ffn_router_bias"],
        "m_guT": T(i["L0_ffn_gate_up_proj"]), "m_dnT": T(i["L0_ffn_down_proj"]),
        "m_gub": i["L0_ffn_gate_up_proj_bias"].reshape(EM, 2 * JT, P).transpose(2, 0, 1),
        "m_db": i["L0_ffn_down_proj_bias"],
        "l_wiT": i["L1_cond_wi"].T, "l_woT": i["L1_cond_wo"].T,
        "l_cia": i["L1_cond_common_wi_a"], "l_cibT": i["L1_cond_common_wi_b"].T,
        "l_coa": i["L1_cond_common_wo_a"], "l_cobT": i["L1_cond_common_wo_b"].T,
        "l_eiaT": i["L1_cond_experts_wi_a"].reshape(EL * RL, D).T,
        "l_eibT": T(i["L1_cond_experts_wi_b"]).reshape(EL * RL, FF),
        "l_eoaT": i["L1_cond_experts_wo_a"].reshape(EL * RL, FF).T,
        "l_eobT": T(i["L1_cond_experts_wo_b"]).reshape(EL * RL, D),
        "n_waT": i["L1_attn_W_attn"].T, "n_wpT": i["L1_attn_W_proj"].T,
        "n_bat": cols(i["L1_attn_b_attn"][:2 * D]), "n_bv": i["L1_attn_b_attn"][2 * D:], "n_bp": cols(i["L1_attn_b_proj"]),
        "f_w1": i["L1_cond2_W1"].transpose(1, 0, 2).reshape(D, LANG * A2), "f_b1": cols(i["L1_cond2_b1"].reshape(-1)),
        "f_w2": i["L1_cond2_W2"].reshape(LANG * A2, D),
        "f_tab": np.stack([i["L1_cond2_b2"], i["L1_cond2_gamma"], i["L1_cond2_beta"]], 1),
        "f_wT": i["L1_ffn_W"].T, "f_vrT": i["L1_ffn_V_r"].T, "f_cT": i["L1_ffn_C"].T, "f_b": cols(i["L1_ffn_b"]),
    }


def kernel(**inputs):
    import concourse.bacc as bacc
    from concourse.bass_utils import run_bass_kernel_spmd

    arrays = {n: np.ascontiguousarray(a) for n, a in {**layouts({k: np.asarray(v) for k, v in inputs.items()}),
                                                      **constants()}.items()}
    nc = bacc.Bacc("TRN2", target_bir_lowering=False, num_devices=1)
    io = {n: nc.dram_tensor(f"in_{n}", a.shape, mybir.dt.from_np(a.dtype), kind="ExternalInput").ap()
          for n, a in arrays.items()}
    out = nc.dram_tensor("outT", (D, N), F32, kind="ExternalOutput").ap()
    build_program(nc, io, out)
    r = run_bass_kernel_spmd(nc, [{f"in_{n}": a for n, a in arrays.items()}], core_ids=[0])
    return np.ascontiguousarray(r.results[0]["outT"].T).reshape(B, S, D)
```

```python
from contextlib import ExitStack

import numpy as np

import concourse.bass as bass
from concourse import mybir

F32 = mybir.dt.float32
F32R = mybir.dt.float32r
I32 = mybir.dt.int32
ALU = mybir.AluOpType
ACT = mybir.ActivationFunctionType
AX = mybir.AxisListType

P = 128
B, S, D = 32, 64, 256
N = B * S
KT = D // P
PAIRS = N // P
TB = 512
NTB = N // TB
HEADS = 16
HD0 = 64
HD1 = D // HEADS
QF = HEADS * HD0
FF = 1024
FT = FF // P
E0 = 8
E2 = 5
SLOTS = 4
BLOCKS = (B + E2 * (SLOTS - 1)) // SLOTS
EM, IM = 8, 512
TOP_K = 4
JT = IM // P
LIMIT, SWIGLU_ALPHA = 7.0, 1.702
EL, RL = 8, 16
LANG, A2 = 10, 64
LT = LANG * A2 // P
EPS = 1e-5


def bcast(ap, axis, n):
    ap = ap.unsqueeze(axis)
    shape = list(ap.shape)
    shape[axis] = n
    return ap.to_broadcast(shape)


def wait(eng, sem, value):
    if isinstance(value, int) and value <= 0:
        return
    eng.wait_ge(sem, value)


def live(p):
    return not isinstance(p, int) or 0 <= p < PAIRS


LEAD, TAIL = 3, 3


def pipeline(eng, step):
    for i in range(-2, LEAD):
        step(i, i % 2)
    trips = (PAIRS - 2 - LEAD) // 2
    with eng.Fori(0, trips) as t:
        for u in range(2):
            step(t * 2 + (LEAD + u), (LEAD + u) % 2)
    for i in range(LEAD + 2 * trips, PAIRS + TAIL):
        step(i, i % 2)


def build_program(nc, io, out):
    ctx = ExitStack()
    with ctx:
        def sb(name, shape, dt=F32, c=ctx, side=None):
            return c.enter_context(nc.sbuf_tensor(name, shape, dt, side=side))

        def sem(name, kept=False):
            s = nc.alloc_semaphore(name=name)
            if not kept:
                used.append(s)
            return s

        def clear():
            nc.clear_and_free_semaphores(used)
            used.clear()
            nc.all_engine_barrier()

        used = []

        banks = [ctx.enter_context(nc.psum_tensor(f"bank{k}", [P, 512], F32)) for k in range(8)]
        xT = sb("xT", [P, KT, N + SLOTS * S])
        ident = sb("ident", [P, P])
        mask = sb("mask", [P, S])
        cols = sb("cols", [P, 16])
        samp = sb("samp", [P, 3, B])
        samp_i = sb("samp_i", [P, 3, B], I32)
        oh_sub = sb("oh_sub", [E0, B])
        oh_lora = sb("oh_lora", [P, B])
        oh_lang = sb("oh_lang", [P, LT, B])
        oh_lang10 = sb("oh_lang10", [LANG, B])
        slot_sample = sb("slot_sample", [1, BLOCKS * SLOTS], I32)
        block_expert = sb("block_expert", [1, BLOCKS], I32)

        c0 = ctx.enter_context(ExitStack())
        with ExitStack() as c:
            with ExitStack() as c2:
                b_ws = [sb(n, s, F32, c2, "right") for n, s in (
                    ("w0s", [P, KT, FF]), ("w1s", [P, KT, FF]), ("w2s", [P, FT, D]))]
                b_w = [sem(f"b_w{n}_in", kept=True) for n in range(3)]
                attention0(nc, io, banks, sb, sem, xT, ident, mask, cols, samp, samp_i, oh_sub, oh_lora,
                           oh_lang, oh_lang10, slot_sample, block_expert, b_ws, b_w)
                clear()
                eo = sb("eo", [P, KT, N + SLOTS * S], F32, c2, "right")
                sT = sb("sT", [P, KT, N], F32, c2, "right")
                gated_ffn(nc, io, banks, sb, sem, xT, eo, sT, slot_sample, block_expert, b_ws, b_w)
                h_hi = sb("h_hi", [P, KT, N], F32R, c)
                h_lo = sb("h_lo", [P, KT, N], F32R, c)
                lgT = sb("lgT", [EM, N], F32, c)
                m_ws = [sb("wgs", [P, KT, 2 * IM], F32, c), sb("wds", [P, JT, D], F32, c)]
                m_wh, m_wl = ([[sb(f"mw{n}{part}{k}", list(t.shape), F32R, c) for n, t in enumerate(m_ws)]
                               for k in range(2)] for part in ("h", "l"))
                weights = m_ws, m_wh, m_wl, [sem(f"m_w{k}_in") for k in range(2)], sem("m_weights_hi"), sem("m_weights_lo")
                mix(nc, io, banks, sb, sem, eo, sT, h_hi, h_lo, lgT, weights)
            zT, cbT, db = (sb(n, s, F32, c0, "right") for n, s in (
                ("zT", [P, KT, N]), ("cbT", [EM, N]), ("db", [EM, D])))
            acc = zT[:, :, :].rearrange("p k n -> p (k n)").rearrange("p (t d) -> p t d", d=D)
            mixture(nc, io, banks, sb, sem, xT, h_hi, h_lo, lgT, ident, weights, acc, cbT, db)
        lora_ffn(nc, io, banks, sb, sem, xT, zT, acc, cbT, db, ident, oh_lora)
        attention1(nc, io, banks, sb, sem, xT, zT, ident, mask)
        c0.close()
        adapter_ffn(nc, io, banks, sb, sem, xT, oh_lang, oh_lang10, out)


def load_expert(sp, io, e, w, sems):
    for dst, name, done in zip(w, ("c2_Wi0", "c2_Wi1", "c2_Wo"), sems):
        sp.dma_start(dst[:, :, :], io[name][bass.ds(e, 1), :, :].rearrange("e (k p) n -> p (e k) n", p=P)).then_inc(done, 16)


def attention0(nc, io, banks, sb0, sem, xT, ident, mask, cols, samp, samp_i, oh_sub, oh_lora, oh_lang,
               oh_lang10, slot_sample, block_expert, b_ws, b_w):
    with ExitStack() as c:
        def sb(name, shape, dt=F32):
            return sb0(name, shape, dt, c)

        wqkv = sb("wqkv", [P, KT, 3 * QF])
        wo = sb("wo", [P, QF // P, D])
        rope = sb("rope", [P, 4, HD0])
        btab = sb("btab", [E0, D])
        biasT = sb("biasT", [P, KT, B])
        wsub = [sb(f"wsub{k}", [P, 2, KT, D]) for k in range(2)]
        xs = [sb(f"xs{k}", [P, KT, P]) for k in range(2)]
        ysb = sb("ysb", [P, D])
        yT = [sb(f"yT{k}", [P, KT, P]) for k in range(2)]
        rc = [sb(f"rc{k}", [P, 512]) for k in range(2)]
        rs = [sb(f"rs{k}", [P, 512]) for k in range(2)]
        qk = [sb(f"qk{k}", [P, 2 * QF]) for k in range(2)]
        v = [sb(f"v{k}", [P, QF]) for k in range(2)]
        qT = sb("qT", [P, HEADS // 2, P])
        kpad = sb("kpad", [P, HEADS // 2, 2, P])
        sc = sb("sc", [P, HEADS, S])
        ex = sb("ex", [P, HEADS, S])
        mx = sb("mx", [P, HEADS])
        sm = sb("sm", [P, HEADS])
        ri = sb("ri", [P, HEADS])
        pr = sb("pr", [P, HEADS, P])
        prT = sb("prT", [P, HEADS, P])
        ctxT = sb("ctxT", [P, QF // P, P])
        rt = {n: sb("rt_" + n, [1, *s]) for n, s in dict(
            es=(E2, B), j8=(E2, B // SLOTS), ee=(E2, E2), ll=(B, B), q=(BLOCKS * SLOTS,),
            sm=(BLOCKS * SLOTS, B), em=(BLOCKS * SLOTS,),
            kk=(BLOCKS,)).items()}
        oh = sb("r_oh", [1, E2, B])
        cnt = sb("r_cnt", [1, E2])
        cmp8 = sb("r_cmp8", [1, E2, B // SLOTS])
        nblk = sb("r_nblk", [1, E2])
        lowb = sb("r_lowb", [1, E2, E2])
        base = sb("r_base", [1, E2])
        base4 = sb("r_base4", [1, E2])
        same = sb("r_same", [1, B, B])
        rank = sb("r_rank", [1, B])
        ohb = sb("r_ohb", [1, B, E2])
        pos = sb("r_pos", [1, B])
        hit = sb("r_hit", [1, BLOCKS * SLOTS, B])
        sid = sb("r_sid", [1, BLOCKS * SLOTS])
        ble = sb("r_ble", [1, BLOCKS, E2])
        bex = sb("r_bex", [1, BLOCKS])

        a_small, a_x, a_wqkv, a_wo, a_route = (sem(n) for n in (
            "a_small_in", "a_x_in", "a_wqkv_in", "a_wo_in", "a_route_in"))
        a_w = [sem(f"a_wsub{k}_in") for k in range(2)]
        a_zero, a_tab, a_bias_ready, a_bias, a_routed, a_slots = (sem(n) for n in (
            "a_zeroed", "a_tables", "a_bias_ready", "a_bias_copied", "a_routed", "a_slots_found"))
        a_xs, a_cond, a_y, a_yt_ready, a_yt = (sem(n) for n in (
            "a_xs_staged", "a_cond_ready", "a_y_copied", "a_yt_ready", "a_yt_copied"))
        a_qk_ready, a_rope, a_add, a_v_ready, a_v = (sem(n) for n in (
            "a_qk_ready", "a_rope_done", "a_rope_added", "a_v_ready", "a_v_copied"))
        a_tq_ready, a_tq, a_s_ready, a_s, a_mx, a_sub, a_exp, a_sum, a_rec, a_p = (sem(n) for n in (
            "a_trqk_ready", "a_trqk_copied", "a_s_ready", "a_s_masked", "a_max", "a_subtracted",
            "a_exp", "a_sum", "a_recip", "a_probs"))
        a_p0, a_tp_ready, a_tp, a_c_ready, a_c, a_o_ready, a_o = (sem(n) for n in (
            "a_probs_half", "a_trp_ready", "a_trp_copied", "a_ctx_ready", "a_ctx_copied", "a_out_ready", "a_out_added"))

        with nc.Block() as block:
            @block.sync
            def _(sp):
                sp.dma_start(samp_i[:, :, :], io["idx"].partition_broadcast(P)).then_inc(a_small, 16)
                for dst, name in ((ident, "ident"), (cols, "cols"), (btab, "c0_bias"), (mask, "mask0")):
                    sp.dma_start(dst[:, :], io[name]).then_inc(a_small, 16)
                sp.dma_start(rope[:, :, :], io["rope"]).then_inc(a_small, 16)
                sp.dma_start(xT[:, :, 0:N], io["xT"].rearrange("(k p) n -> p k n", p=P)).then_inc(a_x, 16)
                sp.wait_ge(a_small, 96)

                def step(i, par):
                    p = i + 2
                    if not live(p):
                        return
                    wait(sp, a_cond, p - 1)
                    for s in range(2):
                        e = sp.value_load(samp_i[0:1, 0, bass.ds(p * 2 + s, 1)], min_val=0, max_val=E0 - 1)
                        sp.dma_start(wsub[par][:, s, :, :], io["c0_wT"][bass.ds(e, 1), :, :].rearrange(
                            "e (k p) o -> p (e k) o", p=P)).then_inc(a_w[par], 16)
                    if isinstance(p, int) and p == 0:
                        sp.dma_start(wqkv[:, :, :], io["a0_wqkv"].rearrange("(k p) n -> p k n", p=P)).then_inc(a_wqkv, 16)
                        sp.dma_start(wo[:, :, :], io["a0_wo"].rearrange("(k p) n -> p k n", p=P)).then_inc(a_wo, 16)
                        for n in rt:
                            sp.dma_start(rt[n][:], io["rt_" + n]).then_inc(a_route, 16)

                pipeline(sp, step)
                sp.wait_ge(a_slots, 1)
                e = sp.value_load(block_expert[0:1, 0:1], min_val=0, max_val=E2 - 1)
                load_expert(sp, io, e, b_ws, b_w)

            @block.gpsimd
            def _(pool):
                pool.memset(kpad[:, :, :, :], 0.0).then_inc(a_zero, 1)
                pool.memset(pr[:, :, :], 0.0).then_inc(a_zero, 1)
                pool.memset(xT[:, :, N:], 0.0).then_inc(a_zero, 1)
                pool.wait_ge(a_x, 16)

                def step(i, par):
                    p = i + 2
                    if live(p):
                        wait(pool, a_cond, p - 1)
                        pool.tensor_copy(xs[par][:, :, :], xT[:, :, bass.ds(p * P, P)]).then_inc(a_xs, 1)
                    for half in range(2):
                        if live(i):
                            if half == 0:
                                wait(pool, a_tq_ready, 4 * (i - 2) + 4)
                            for c2 in range(2):
                                n = 4 * i + 2 * half + c2
                                wait(pool, a_rope, n + 1)
                                ch = 2 * half + c2
                                pool.tensor_tensor(qk[par][:, ch * 512:(ch + 1) * 512], rc[c2][:, :],
                                                   rs[c2][:, :], ALU.add).then_inc(a_add, 1)
                        if half == 0 and live(i - 2):
                            wait(pool, a_rec, i - 1)
                            if isinstance(i, int) and i == 2:
                                pool.wait_ge(a_zero, 3)
                            wait(pool, a_tp_ready, 4 * (i - 3) + 4)
                            if live(i):
                                pool.wait_ge(a_add, 4 * i + 2)
                            if live(i + 2):
                                pool.wait_ge(a_xs, i + 3)
                            pool.tensor_tensor(pr[0:S, :, 0:S], ex[0:S, :, :], bcast(ri[0:S, :], 2, S), ALU.mult).then_inc(a_p0, 1)
                            pool.wait_ge(a_p0, i - 1)
                            pool.tensor_tensor(pr[S:P, :, S:P], ex[S:P, :, :], bcast(ri[S:P, :], 2, S), ALU.mult).then_inc(a_p, 1)
                            pool.wait_ge(a_p, i - 1)

                pipeline(pool, step)

            @block.tensor
            def _(pe):
                pe.wait_ge(a_tab, 2)
                for k in range(KT):
                    mm = pe.matmul(banks[7][:, k * B:(k + 1) * B], btab[:, k * P:(k + 1) * P], oh_sub[:, :],
                                   start=True, stop=True)
                mm.then_inc(a_bias_ready, 1)

                def qk_chunks(i, par, chunks):
                    for ch in chunks:
                        wait(pe, a_rope, 4 * i + ch - 1)
                        for k in range(KT):
                            mm = pe.matmul(banks[1 + ch % 2][:, :], yT[par][:, k, :],
                                           wqkv[:, k, ch * 512:(ch + 1) * 512], start=k == 0, stop=k == KT - 1)
                        mm.then_inc(a_qk_ready, 1)

                def step(i, par):
                    if live(i):
                        if isinstance(i, int) and i == 0:
                            pe.wait_ge(a_wqkv, 16)
                        pe.wait_ge(a_yt, i + 1)
                        qk_chunks(i, par, (0, 1))
                    if live(i - 3):
                        p = i - 3
                        if isinstance(p, int) and p == 0:
                            pe.wait_ge(a_wo, 16)
                        pe.wait_ge(a_c, 2 * p + 2)
                        wait(pe, a_o, p)
                        for o in range(KT):
                            for k in range(QF // P):
                                mm = pe.matmul(banks[0][:, o * P:(o + 1) * P], wo[:, k, o * P:(o + 1) * P],
                                               ctxT[:, k, :], start=k == 0, stop=k == QF // P - 1)
                        mm.then_inc(a_o_ready, 1)
                    if live(i - 1):
                        p = i - 1
                        for ch in range(2):
                            wait(pe, a_v, 2 * p + ch)
                            for k in range(KT):
                                mm = pe.matmul(banks[3][:, :], yT[1 - par][:, k, :],
                                               wqkv[:, k, 2 * QF + ch * 512:2 * QF + (ch + 1) * 512],
                                               start=k == 0, stop=k == KT - 1)
                            mm.then_inc(a_v_ready, 1)
                    if live(i + 1):
                        p = i + 1
                        wait(pe, a_o, i - 2)
                        pe.wait_ge(a_xs, p + 1)
                        if isinstance(p, int):
                            pe.wait_ge(a_w[1 - par], 32 * (p // 2 + 1))
                        else:
                            pe.wait_ge(a_w[1 - par], 16 * p + (32 if par == 1 else 16))
                        for s in range(2):
                            for k in range(KT):
                                mm = pe.matmul(banks[0][S * s:S * s + S, 0:D], xs[1 - par][:, k, S * s:S * s + S],
                                               wsub[1 - par][:, s, k, :], start=k == 0, stop=k == KT - 1)
                        mm.then_inc(a_cond, 1)
                    if live(i):
                        qk_chunks(i, par, (2, 3))
                    if live(i - 1):
                        p = i - 1
                        pe.wait_ge(a_add, 4 * p + 4)
                        for f in range(4):
                            wait(pe, a_c, 2 * (i - 3) + f + 1) if f < 2 else wait(pe, a_tq, 4 * p + f - 1)
                            for j in range(4):
                                at = (4 * f + j) * P
                                mm = pe.transpose(banks[6 + f % 2][:, j * P:(j + 1) * P],
                                                  qk[1 - par][:, at:at + P], ident[:, :])
                            mm.then_inc(a_tq_ready, 1)
                    if live(i + 1):
                        pe.wait_ge(a_y, i + 2)
                        for k in range(KT):
                            mm = pe.transpose(banks[0][:, k * P:(k + 1) * P], ysb[:, k * P:(k + 1) * P], ident[:, :])
                        mm.then_inc(a_yt_ready, 1)
                    if live(i - 2):
                        p = i - 2
                        pe.wait_ge(a_p, p + 1)
                        for f in range(4):
                            if f >= 2:
                                wait(pe, a_tp, 4 * p + f - 1)
                            elif live(i - 1):
                                wait(pe, a_tq, 4 * (i - 1) + f + 3)
                            for j in range(4):
                                mm = pe.transpose(banks[6 + f % 2][:, j * P:(j + 1) * P], pr[:, 4 * f + j, :], ident[:, :])
                            mm.then_inc(a_tp_ready, 1)
                    if live(i - 1):
                        p = i - 1
                        pe.wait_ge(a_tq, 4 * p + 4)
                        for f in range(4):
                            wait(pe, a_s, 4 * p + f - 1)
                            for j in range(2):
                                t = 2 * f + j
                                mm = pe.matmul(banks[4 + f % 2][:, j * 256:(j + 1) * 256], qT[:, t, :],
                                               kpad[:, t, :, :], start=True, stop=True)
                            mm.then_inc(a_s_ready, 1)
                    if live(i - 2):
                        p = i - 2
                        for g in range(2):
                            pe.wait_ge(a_tp, 4 * p + 3 + g)
                            for j in range(4):
                                for s in range(2):
                                    h = 8 * g + 2 * j + s
                                    mm = pe.matmul(banks[6 + g][HD0 * s:HD0 * s + HD0, j * P:(j + 1) * P],
                                                   v[par][:, h * HD0:(h + 1) * HD0], prT[:, h, :],
                                                   start=True, stop=True)
                            mm.then_inc(a_c_ready, 1)

                pipeline(pe, step)

            @block.scalar
            def _(act):
                def step(i, par):
                    if live(i - 1):
                        p = i - 1
                        for ch in range(2):
                            act.wait_ge(a_v_ready, 2 * p + ch + 1)
                            act.activation(v[1 - par][:, ch * 512:(ch + 1) * 512], banks[3][:, :],
                                           ACT.Copy).then_inc(a_v, 1)
                    if live(i + 1):
                        act.wait_ge(a_cond, i + 2)
                        act.activation(ysb[:, :], banks[0][:, 0:D], ACT.Copy).then_inc(a_y, 1)
                    if live(i - 1):
                        p = i - 1
                        if isinstance(p, int) and p == 0:
                            act.wait_ge(a_zero, 1)
                        for f in range(4):
                            act.wait_ge(a_tq_ready, 4 * p + f + 1)
                            bank = banks[6 + f % 2][:, :].rearrange("p (t n) -> p t n", n=P)
                            if f < 2:
                                last = act.activation(qT[:, 4 * f:4 * f + 4, :], bank, ACT.Copy)
                            else:
                                for s in range(2):
                                    rows = slice(HD0 * s, HD0 * s + HD0)
                                    last = act.activation(kpad[rows, 4 * f - 8:4 * f - 4, s, :], bank[rows], ACT.Copy)
                            last.then_inc(a_tq, 1)
                    if live(i - 2):
                        p = i - 2
                        for f in range(4):
                            act.wait_ge(a_tp_ready, 4 * p + f + 1)
                            act.activation(prT[:, 4 * f:4 * f + 4, :], banks[6 + f % 2][:, :].rearrange(
                                "p (t n) -> p t n", n=P), ACT.Copy).then_inc(a_tp, 1)
                        for g in range(2):
                            act.wait_ge(a_c_ready, 2 * p + g + 1)
                            act.activation(ctxT[:, 4 * g:4 * g + 4, :], banks[6 + g][:, :].rearrange(
                                "p (t n) -> p t n", n=P), ACT.Copy).then_inc(a_c, 1)
                    if live(i - 1):
                        act.wait_ge(a_sub, i)
                        wait(act, a_p, i - 1)
                        act.activation(ex[:, :, :], sc[:, :, :], ACT.Exp).then_inc(a_exp, 1)

                pipeline(act, step)

            @block.vector
            def _(dve):
                dve.wait_ge(a_small, 96)
                dve.tensor_copy(samp[:, :, :], samp_i[:, :, :]).then_inc(a_tab, 1)
                dve.wait_ge(a_tab, 1)
                dve.tensor_scalar(oh_lora[:, :], samp[:, 0, :], cols[:, 1:2], 2.0, ALU.is_equal, ALU.mult)
                for k in range(LT):
                    dve.tensor_scalar(oh_lang[:, k, :], samp[:, 2, :], cols[:, 2 + k:3 + k], None, ALU.is_equal)
                dve.tensor_scalar(oh_lang10[:, :], samp[0:LANG, 2, :], cols[0:LANG, 0:1], None, ALU.is_equal)
                dve.tensor_scalar(oh_sub[:, :], samp[0:E0, 0, :], cols[0:E0, 0:1], None, ALU.is_equal).then_inc(a_tab, 1)
                dve.wait_ge(a_bias_ready, 1)
                dve.tensor_copy(biasT[:, :, :], banks[7][:, 0:KT * B].rearrange("p (k b) -> p k b", k=KT)).then_inc(a_bias, 1)
                dve.wait_ge(a_bias, 1)

                def route():
                    dve.wait_ge(a_route, 16 * len(rt))
                    ty = samp[0:1, 1, :]
                    n = [0]

                    def then(ins):
                        ins.then_inc(a_routed, 1)
                        n[0] += 1
                        dve.wait_ge(a_routed, n[0])

                    then(dve.tensor_tensor(oh[:, :, :], bcast(ty, 1, E2), rt["es"][:, :, :], ALU.is_equal))
                    then(dve.tensor_reduce(cnt[:, :], oh[:, :, :], AX.X, ALU.add))
                    then(dve.tensor_tensor(cmp8[:, :, :], bcast(cnt[:, :], 2, B // SLOTS), rt["j8"][:, :, :], ALU.is_gt))
                    then(dve.tensor_reduce(nblk[:, :], cmp8[:, :, :], AX.X, ALU.add))
                    then(dve.tensor_tensor(lowb[:, :, :], bcast(nblk[:, :], 1, E2), rt["ee"][:, :, :], ALU.mult))
                    then(dve.tensor_reduce(base[:, :], lowb[:, :, :], AX.X, ALU.add))
                    then(dve.tensor_scalar(base4[:, :], base[:, :], float(SLOTS), None, ALU.mult))
                    then(dve.tensor_tensor(same[:, :, :], bcast(ty, 2, B), bcast(ty, 1, B), ALU.is_equal))
                    then(dve.tensor_tensor(same[:, :, :], same[:, :, :], rt["ll"][:, :, :], ALU.mult))
                    then(dve.tensor_reduce(rank[:, :], same[:, :, :], AX.X, ALU.add))
                    then(dve.tensor_tensor(ohb[:, :, :], oh[:, :, :].rearrange("p e b -> p b e"),
                                           bcast(base4[:, :], 1, B), ALU.mult))
                    then(dve.tensor_reduce(pos[:, :], ohb[:, :, :], AX.X, ALU.add))
                    then(dve.tensor_tensor(pos[:, :], pos[:, :], rank[:, :], ALU.add))
                    then(dve.tensor_tensor(hit[:, :, :], bcast(pos[:, :], 1, BLOCKS * SLOTS),
                                           bcast(rt["q"][:, :], 2, B), ALU.is_equal))
                    then(dve.tensor_tensor(hit[:, :, :], hit[:, :, :], rt["sm"][:, :, :], ALU.mult))
                    then(dve.tensor_reduce(sid[:, :], hit[:, :, :], AX.X, ALU.add))
                    then(dve.tensor_tensor(sid[:, :], sid[:, :], rt["em"][:, :], ALU.add))
                    then(dve.tensor_copy(slot_sample[:, :], sid[:, :]))
                    then(dve.tensor_tensor(ble[:, :, 1:E2], bcast(base[:, 1:E2], 1, BLOCKS),
                                           bcast(rt["kk"][:, :], 2, E2 - 1), ALU.is_le))
                    then(dve.tensor_reduce(bex[:, :], ble[:, :, 1:E2], AX.X, ALU.add))
                    dve.tensor_copy(block_expert[:, :], bex[:, :]).then_inc(a_slots, 1)

                def rotate(i, chunks):
                    for ch in chunks:
                        n = 4 * i + ch
                        dve.wait_ge(a_qk_ready, n + 1)
                        wait(dve, a_add, n - 1)
                        src = banks[1 + ch % 2][:, :].rearrange("p (h t d) -> p h t d", t=2, d=HD0 // 2)
                        w = 2 * (ch // 2)
                        cos = bcast(rope[:, w, :].rearrange("p (t d) -> p t d", t=2), 1, 512 // HD0)
                        sin = bcast(rope[:, w + 1, :].rearrange("p (t d) -> p t d", t=2), 1, 512 // HD0)
                        dst = [r[ch % 2][:, :].rearrange("p (h t d) -> p h t d", t=2, d=HD0 // 2) for r in (rc, rs)]
                        dve.tensor_tensor(dst[0], src, cos, ALU.mult)
                        dve.tensor_tensor(dst[1], src[:, :, ::-1, :], sin, ALU.mult).then_inc(a_rope, 1)

                def step(i, par):
                    if live(i):
                        rotate(i, (0, 1))
                    if live(i - 2):
                        p = i - 2
                        dve.wait_ge(a_exp, p + 1)
                        wait(dve, a_p, p)
                        dve.tensor_reduce(sm[:, :], ex[:, :, :], AX.X, ALU.add).then_inc(a_sum, 1)
                        dve.wait_ge(a_sum, p + 1)
                        dve.reciprocal(ri[:, :], sm[:, :]).then_inc(a_rec, 1)
                    if live(i - 3):
                        p = i - 3
                        dve.wait_ge(a_o_ready, p + 1)
                        at = xT[:, :, bass.ds(p * P, P)]
                        dve.tensor_tensor(at, banks[0][:, 0:D].rearrange("p (k n) -> p k n", k=KT), at,
                                          ALU.add).then_inc(a_o, 1)
                    if live(i):
                        rotate(i, (2, 3))
                    if live(i + 1):
                        p = i + 1
                        dve.wait_ge(a_yt_ready, p + 1)
                        for k in range(KT):
                            last = dve.tensor_tensor(
                                yT[1 - par][:, k, :].rearrange("p (s n) -> p s n", s=2),
                                banks[0][:, k * P:(k + 1) * P].rearrange("p (s n) -> p s n", s=2),
                                bcast(biasT[:, k, bass.ds(p * 2, 2)], 2, S), ALU.add)
                        last.then_inc(a_yt, 1)
                    if live(i - 1):
                        p = i - 1
                        wait(dve, a_exp, p)
                        for f in range(4):
                            dve.wait_ge(a_s_ready, 4 * p + f + 1)
                            for s in range(2):
                                rows = slice(S * s, S * s + S)
                                last = dve.tensor_tensor(
                                    sc[rows, 4 * f:4 * f + 4, :],
                                    banks[4 + f % 2][rows, :].rearrange("p (h n) -> p h n", n=P)[:, :, S * s:S * s + S],
                                    bcast(mask[rows, :], 1, 4), ALU.add)
                            last.then_inc(a_s, 1)
                        dve.wait_ge(a_s, 4 * p + 4)
                        dve.tensor_reduce(mx[:, :], sc[:, :, :], AX.X, ALU.max).then_inc(a_mx, 1)
                        dve.wait_ge(a_mx, p + 1)
                        dve.tensor_tensor(sc[:, :, :], sc[:, :, :], bcast(mx[:, :], 2, S), ALU.subtract).then_inc(a_sub, 1)
                    if isinstance(i, int) and i == 0:
                        route()

                pipeline(dve, step)


def whole(t):
    return t if isinstance(t, bass.AP) else t[tuple(slice(None) for _ in t.shape)]


def mm3(pe, out, w, x, start, stop):
    pe.matmul(out, w[0], x[0], start=start, stop=False)
    pe.matmul(out, w[0], x[1], start=False, stop=False)
    return pe.matmul(out, w[1], x[0], start=False, stop=stop)


def gated_ffn(nc, io, banks, sb0, sem, xT, eo, sT, slot_sample, block_expert, ws, b_w):
    with ExitStack() as c:
        def sb(name, shape, dt=F32):
            return sb0(name, shape, dt, c)

        SW = SLOTS * S
        SHARED = N // SW
        UNITS = BLOCKS + SHARED
        SH = BLOCKS % 2

        wh = [[sb(f"w{n}h{k}", list(t.shape), F32R) for n, t in enumerate(ws)] for k in range(2)]
        wl = [[sb(f"w{n}l{k}", list(t.shape), F32R) for n, t in enumerate(ws)] for k in range(2)]
        xg = sb("xg", [P, KT, SW])
        xh = [sb(f"xgh{k}", [P, KT, SW], F32R) for k in range(2)]
        xl = [sb(f"xgl{k}", [P, KT, SW], F32R) for k in range(2)]
        ge = [sb(f"ge{k}", [P, SW]) for k in range(2)]
        hf = [sb(f"hf{k}", [P, SW]) for k in range(2)]
        hh = [sb(f"hh{k}", [P, SW], F32R) for k in range(2)]
        hl = [sb(f"hl{k}", [P, SW], F32R) for k in range(2)]
        (b_whi, b_wlo01, b_wlo2, b_xg, b_xh, b_xl, b_up, b_ge, b_hf, b_hh, b_hl, b_down, b_o) = (sem(n) for n in (
            "b_weights_hi", "b_weights01_lo", "b_weights2_lo", "b_x_gathered", "b_x_hi", "b_x_lo", "b_up_ready",
            "b_gelu", "b_hidden", "b_hidden_hi", "b_hidden_lo", "b_down_ready", "b_out_copied"))

        PIECES = 6

        def piece(t, q):
            w = t[q // 2]
            half = w.shape[1] // 2
            return w[:, (q % 2) * half:(q % 2 + 1) * half, :]

        with nc.Block() as block:
            @block.sync
            def _(sp):
                def load(v, srcs):
                    for n in range(3):
                        if n < 2:
                            sp.wait_ge(b_wlo01, 4 * (v - 1) + 2 * n + 2)
                        else:
                            sp.wait_ge(b_wlo2, 2 * (v - 1) + 2)
                        sp.dma_start(ws[n][:, :, :], srcs[n]).then_inc(b_w[n], 16)

                with sp.Fori(1, BLOCKS) as v:
                    e = sp.value_load(block_expert[0:1, bass.ds(v, 1)], min_val=0, max_val=E2 - 1)
                    load(v, [io[n][bass.ds(e, 1), :, :].rearrange("e (k p) n -> p (e k) n", p=P)
                             for n in ("c2_Wi0", "c2_Wi1", "c2_Wo")])
                load(BLOCKS, [io[n].rearrange("(k p) n -> p k n", p=P) for n in ("c2_sWi0", "c2_sWi1", "c2_sWo")])

            @block.gpsimd
            def _(pool):
                def gather(v):
                    for j in range(SLOTS):
                        s = pool.value_load(slot_sample[0:1, bass.ds(v * SLOTS + j, 1)], min_val=0, max_val=B + SLOTS - 1)
                        last = pool.tensor_copy(xg[:, :, j * S:(j + 1) * S], xT[:, :, bass.ds(s * S, S)])
                    last.then_inc(b_xg, 1)

                def slice_(v):
                    pool.tensor_copy(xg[:, :, :], xT[:, :, bass.ds((v - BLOCKS) * SW, SW)]).then_inc(b_xg, 1)

                def lo(v, q, par):
                    pool.wait_ge(b_whi, v * PIECES + (q + 1))
                    pool.tensor_tensor(piece(wl[par], q), piece(ws, q), piece(wh[par], q).bitcast(F32),
                                       ALU.subtract).then_inc(b_wlo01, 1)

                def x_lo(v, par):
                    pool.wait_ge(b_xh, v + 1)
                    pool.tensor_tensor(xl[par][:, :, :], xg[:, :, :], xh[par][:, :, :].bitcast(F32),
                                       ALU.subtract).then_inc(b_xl, 1)

                def prepare(v, par, take=gather, weights=True):
                    wait(pool, b_xl, v)
                    take(v)
                    if weights:
                        for q in range(4):
                            lo(v, q, par)
                    x_lo(v, par)

                prepare(0, 0)
                with pool.Fori(0, (BLOCKS - 1) // 2) as t:
                    for j in range(2):
                        prepare(t * 2 + (1 + j), 1 - j)
                prepare(BLOCKS, SH, slice_)
                prepare(BLOCKS + 1, 1 - SH, slice_, False)
                with pool.Fori(1, SHARED // 2) as t:
                    for j in range(2):
                        prepare(t * 2 + (BLOCKS + j), (BLOCKS + j) % 2, slice_, False)

            @block.tensor
            def _(pe):
                def up(u, par, wb, f):
                    wait(pe, b_hf, FT * u + f - 1)
                    for bank, n in ((f % 2, 0), (2 + f % 2, 1)):
                        for k in range(KT):
                            mm = mm3(pe, banks[bank][:, 0:SW], [w[wb][n][:, k, f * P:(f + 1) * P] for w in (wh, wl)],
                                     [x[par][:, k, :] for x in (xh, xl)], k == 0, k == KT - 1)
                    mm.then_inc(b_up, 1)

                def down(u, par, wb, f):
                    pe.wait_ge(b_hl, FT * u + f + 1)
                    if f == 0:
                        wait(pe, b_o, u - 1)
                    for o in range(KT):
                        mm = mm3(pe, banks[4 + 2 * par + o][:, 0:SW], [w[wb][2][:, f, o * P:(o + 1) * P] for w in (wh, wl)],
                                 [h[f % 2][:, :] for h in (hh, hl)], f == 0, f == FT - 1)
                    mm.then_inc(b_down, 1)

                def unit(u, par, wb, before, new_weights=True):
                    pe.wait_ge(b_xl, u + 1)
                    if new_weights:
                        pe.wait_ge(b_wlo01, 4 * u + 4)
                    for f in range(FT):
                        up(u, par, wb, f)
                        if f >= 2:
                            if f == 2 and new_weights:
                                pe.wait_ge(b_wlo2, 2 * u + 2)
                            down(u, par, wb, f - 2)
                        elif before is not None:
                            down(u - 1, 1 - par, before, FT - 2 + f)

                unit(0, 0, 0, None)
                with pe.Fori(0, (BLOCKS - 1) // 2) as t:
                    for j in range(2):
                        unit(t * 2 + (1 + j), 1 - j, 1 - j, j)
                unit(BLOCKS, SH, SH, 1 - SH)
                unit(BLOCKS + 1, 1 - SH, SH, SH, False)
                with pe.Fori(1, SHARED // 2) as t:
                    for j in range(2):
                        unit(t * 2 + (BLOCKS + j), (BLOCKS + j) % 2, SH, SH, False)
                for f in (FT - 2, FT - 1):
                    down(UNITS - 1, (UNITS - 1) % 2, SH, f)

            @block.scalar
            def _(act):
                def hi(v, q, par):
                    if q % 2 == 0:
                        act.wait_ge(b_w[q // 2], 16 * v + 16)
                    act.activation(piece(wh[par], q), piece(ws, q), ACT.Copy).then_inc(b_whi, 1)

                def x_hi(v, par):
                    act.wait_ge(b_xg, v + 1)
                    wait(act, b_up, FT * (v - 1))
                    act.activation(xh[par][:, :, :], xg[:, :, :], ACT.Copy).then_inc(b_xh, 1)

                def h_hi(m, f):
                    act.wait_ge(b_hf, m + 1)
                    wait(act, b_down, m - 1)
                    act.activation(hh[f % 2][:, :], hf[f % 2][:, :], ACT.Copy).then_inc(b_hh, 1)

                def unit(u, par, weights=True, x=True):
                    for f in range(FT):
                        m = FT * u + f
                        act.wait_ge(b_up, m + 1)
                        wait(act, b_hf, m - 1)
                        act.activation(ge[f % 2][:, :], banks[f % 2][:, 0:SW], ACT.Gelu_apprx_tanh).then_inc(b_ge, 1)
                        if not (isinstance(m, int) and m == 0):
                            h_hi(m - 1, (f - 1) % FT)
                        if f == 4 and weights:
                            wait(act, b_down, FT * u)
                        if f < PIECES and weights:
                            hi(u + 1, f, 1 - par)
                        if f == PIECES and x:
                            x_hi(u + 1, 1 - par)

                for q in range(PIECES):
                    hi(0, q, 0)
                x_hi(0, 0)
                unit(0, 0)
                with act.Fori(0, (BLOCKS - 1) // 2) as t:
                    for j in range(2):
                        unit(t * 2 + (1 + j), 1 - j)
                with act.Fori(0, SHARED // 2 - 1) as t:
                    for j in range(2):
                        unit(t * 2 + (BLOCKS + j), (BLOCKS + j) % 2, False)
                unit(UNITS - 2, (UNITS - 2) % 2, False)
                unit(UNITS - 1, (UNITS - 1) % 2, False, False)
                h_hi(FT * UNITS - 1, FT - 1)

            @block.vector
            def _(dve):
                def h_lo(m, f):
                    dve.wait_ge(b_hh, m + 1)
                    dve.tensor_tensor(hl[f % 2][:, :], hf[f % 2][:, :], hh[f % 2][:, :].bitcast(F32),
                                      ALU.subtract).then_inc(b_hl, 1)

                def scatter(u, par, j):
                    if j == 0:
                        dve.wait_ge(b_down, FT * u + FT)
                        wait(dve, b_o, u)
                    s = dve.value_load(slot_sample[0:1, bass.ds(u * SLOTS + j, 1)], min_val=0, max_val=B + SLOTS - 1)
                    for o in range(KT):
                        last = dve.tensor_copy(eo[:, o, bass.ds(s * S, S)], banks[4 + 2 * par + o][:, j * S:(j + 1) * S])
                    if j == SLOTS - 1:
                        last.then_inc(b_o, 1)

                def store(u, par, j):
                    if j:
                        return
                    dve.wait_ge(b_down, FT * u + FT)
                    for o in range(KT):
                        last = dve.tensor_copy(sT[:, o, bass.ds((u - BLOCKS) * SW, SW)], banks[4 + 2 * par + o][:, 0:SW])
                    last.then_inc(b_o, 1)

                def lo(v, q, par):
                    dve.wait_ge(b_whi, v * PIECES + (q + 1))
                    dve.tensor_tensor(piece(wl[par], q), piece(ws, q), piece(wh[par], q).bitcast(F32),
                                      ALU.subtract).then_inc(b_wlo2, 1)

                def unit(u, par, last=scatter, weights=True):
                    for f in range(FT):
                        m = FT * u + f
                        dve.wait_ge(b_ge, m + 1)
                        wait(dve, b_hl, m - 1)
                        dve.tensor_tensor(hf[f % 2][:, :], banks[2 + f % 2][:, 0:SW], ge[f % 2][:, :],
                                          ALU.mult).then_inc(b_hf, 1)
                        if not (isinstance(m, int) and m == 0):
                            h_lo(m - 1, (f - 1) % FT)
                        if 2 <= f < 2 + SLOTS and last:
                            last(u - 1, 1 - par, f - 2)
                        if f >= PIECES and weights:
                            lo(u + 1, f - 2, 1 - par)

                lo(0, 4, 0)
                lo(0, 5, 0)
                unit(0, 0, None)
                with dve.Fori(0, (BLOCKS - 1) // 2) as t:
                    for j in range(2):
                        unit(t * 2 + (1 + j), 1 - j)
                unit(BLOCKS, SH, scatter, False)
                unit(BLOCKS + 1, 1 - SH, store, False)
                with dve.Fori(1, SHARED // 2) as t:
                    for j in range(2):
                        unit(t * 2 + (BLOCKS + j), (BLOCKS + j) % 2, store, False)
                h_lo(FT * UNITS - 1, FT - 1)
                store(UNITS - 1, (UNITS - 1) % 2, 0)


def load_experts_weights(sp, io, e, ws, m_w, m_wlo):
    for n, name in enumerate(("m_guT", "m_dnT")):
        wait(sp, m_wlo, 3 * (e - 1) + 2 + n)
        sp.dma_start(ws[n][:, :, :], io[name][bass.ds(e, 1), :, :].rearrange(
            "e (k p) n -> p (e k) n", p=P)).then_inc(m_w[n], 16)


def weight_piece(t, q):
    return t[0][:, q, :] if q < KT else t[1][:, :, :]


def split_hi(act, e, q, ws, wh, m_w, m_whi):
    if q != 1:
        act.wait_ge(m_w[q // 2], e * 16 + 16)
    act.activation(weight_piece(wh, q), weight_piece(ws, q), ACT.Copy).then_inc(m_whi, 1)


def split_lo(pool, e, q, ws, wh, wl, m_whi, m_wlo):
    pool.wait_ge(m_whi, e * 3 + (q + 1))
    pool.tensor_tensor(weight_piece(wl, q), weight_piece(ws, q), weight_piece(wh, q).bitcast(F32),
                       ALU.subtract).then_inc(m_wlo, 1)


def mix(nc, io, banks, sb0, sem, eo, sT, hh, hl, lgT, weights):
    ws, wh, wl, m_w, m_whi, m_wlo = weights
    with ExitStack() as c:
        def sb(name, shape, dt=F32):
            return sb0(name, shape, dt, c)

        g0 = sb("g0", [P, 2 * KT, D])
        g1 = sb("g1", [P, KT, 2])
        gi = sb("gi", [P, 2 * KT, B])
        gr = sb("gr", [P, KT, B])
        z = sb("z", [P, 2, B])
        zm = sb("zm", [P, B])
        zs = sb("zs", [P, B])
        rw = sb("rw", [P, KT, EM])
        ew = [sb(f"ew{k}", [P, TB]) for k in range(2)]
        g_in, g_step, g_pe, g_ew, g_sw, g_h, g_hh, g_hl, g_l = (sem(n) for n in (
            "g_in", "g_gate_step", "g_gate_products", "g_expert_weighed", "g_shared_weighed", "g_mixed",
            "g_hi", "g_lo", "g_logits_ready"))
        BS = TB // S
        M = NTB * KT

        def by(ap):
            return ap.rearrange("p (b n) -> p b n", n=S)

        def part(t, m):
            return t[:, m % KT, (m // KT) * TB:(m // KT + 1) * TB]

        with nc.Block() as block:
            @block.sync
            def _(sp):
                sp.dma_start(g0[:, :, :], io["c2_g0"].rearrange("(k p) n -> p k n", p=P)).then_inc(g_in, 16)
                sp.dma_start(g1[:, :, :], io["c2_g1"].rearrange("(k p) n -> p k n", p=P)).then_inc(g_in, 16)
                sp.dma_start(rw[:, :, :], io["m_rwT"].rearrange("(k p) n -> p k n", p=P)).then_inc(g_in, 16)
                load_experts_weights(sp, io, 0, ws, m_w, m_wlo)

            @block.tensor
            def _(pe):
                pe.wait_ge(g_in, 48)
                pe.wait_ge(g_step, 1)
                for o in range(KT):
                    for k in range(2 * KT):
                        mm = pe.matmul(banks[0][:, o * B:(o + 1) * B], g0[:, k, o * P:(o + 1) * P], gi[:, k, :],
                                       start=k == 0, stop=k == 2 * KT - 1)
                mm.then_inc(g_pe, 1)
                pe.wait_ge(g_step, 2)
                for r in range(2):
                    for k in range(KT):
                        mm = pe.matmul(banks[1][:, r * B:(r + 1) * B], g1[:, k, r:r + 1].to_broadcast([P, P]),
                                       gr[:, k, :], start=k == 0, stop=k == KT - 1)
                mm.then_inc(g_pe, 1)
                for t in range(NTB):
                    pe.wait_ge(g_h, KT * t + KT)
                    for k in range(KT):
                        mm = pe.matmul(banks[2 + t][0:EM, :], rw[:, k, :], sT[:, k, t * TB:(t + 1) * TB],
                                       start=k == 0, stop=k == KT - 1)
                    mm.then_inc(g_l, 1)

            @block.gpsimd
            def _(pool):
                for q in range(3):
                    split_lo(pool, 0, q, ws, wh[0], wl[0], m_whi, m_wlo)
                pool.wait_ge(g_step, 8)
                for m in range(M):
                    wait(pool, g_h, m - 1)
                    w = bcast(z[:, 0, (m // KT) * BS:(m // KT + 1) * BS], 2, S)
                    pool.tensor_tensor(by(ew[m % 2][:, :]), by(part(eo, m)), w, ALU.mult).then_inc(g_ew, 1)

            @block.scalar
            def _(act):
                for q in range(3):
                    split_hi(act, 0, q, ws, wh[0], m_w, m_whi)
                act.wait_ge(g_step, 5)
                act.activation(z[:, :, :], z[:, :, :], ACT.Exp).then_inc(g_pe, 1)
                for m in range(M):
                    act.wait_ge(g_h, m + 1)
                    act.activation(part(hh, m), part(sT, m), ACT.Copy).then_inc(g_hh, 1)
                for t in range(NTB):
                    act.wait_ge(g_l, t + 1)
                    last = act.activation(lgT[:, t * TB:(t + 1) * TB], banks[2 + t][0:EM, :], ACT.Copy)
                last.then_inc(g_pe, 1)

            @block.vector
            def _(dve):
                dve.tensor_copy(gi[:, 0:KT, :], eo[:, :, 0:N:S])
                dve.tensor_copy(gi[:, KT:2 * KT, :], sT[:, :, 0:N:S]).then_inc(g_step, 1)
                dve.wait_ge(g_pe, 1)
                dve.tensor_scalar(gr[:, :, :], banks[0][:, 0:KT * B].rearrange("p (k b) -> p k b", k=KT), 0.0, None,
                                  ALU.max).then_inc(g_step, 1)
                dve.wait_ge(g_pe, 2)
                dve.tensor_copy(z[:, :, :], banks[1][:, 0:2 * B].rearrange("p (k b) -> p k b", k=2)).then_inc(g_step, 1)
                dve.wait_ge(g_step, 3)
                dve.tensor_tensor(zm[:, :], z[:, 0, :], z[:, 1, :], ALU.max).then_inc(g_step, 1)
                dve.wait_ge(g_step, 4)
                dve.tensor_tensor(z[:, :, :], z[:, :, :], bcast(zm[:, :], 1, 2), ALU.subtract).then_inc(g_step, 1)
                dve.wait_ge(g_pe, 3)
                dve.tensor_tensor(zs[:, :], z[:, 0, :], z[:, 1, :], ALU.add).then_inc(g_step, 1)
                dve.wait_ge(g_step, 6)
                dve.reciprocal(zm[:, :], zs[:, :]).then_inc(g_step, 1)
                dve.wait_ge(g_step, 7)
                dve.tensor_tensor(z[:, :, :], z[:, :, :], bcast(zm[:, :], 1, 2), ALU.mult).then_inc(g_step, 1)
                dve.wait_ge(g_step, 8)

                def lo(m):
                    dve.wait_ge(g_hh, m + 1)
                    dve.tensor_tensor(part(hl, m), part(sT, m), part(hh, m).bitcast(F32), ALU.subtract).then_inc(g_hl, 1)

                for m in range(M):
                    s = part(sT, m)
                    w = bcast(z[:, 1, (m // KT) * BS:(m // KT + 1) * BS], 2, S)
                    dve.tensor_tensor(by(s), by(s), w, ALU.mult).then_inc(g_sw, 1)
                    if m:
                        lo(m - 1)
                    dve.wait_ge(g_sw, m + 1)
                    dve.wait_ge(g_ew, m + 1)
                    dve.tensor_tensor(s, ew[m % 2][:, :], s, ALU.add).then_inc(g_h, 1)
                lo(M - 1)


def mixture(nc, io, banks, sb0, sem, xT, hh, hl, lgT, ident, weights, acc, cbT, db):
    ws, wh, wl, m_w, m_whi, m_wlo = weights
    with ExitStack() as c:
        def sb(name, shape, dt=F32):
            return sb0(name, shape, dt, c)

        rb = sb("rb", [P, EM])
        lg = sb("lg", [P, PAIRS, EM])
        cb = sb("cb", [P, PAIRS, EM])
        gt = sb("gt", [P, PAIRS, EM])
        rank = sb("rank", [P, PAIRS, EM])
        m1 = sb("m1", [P, PAIRS])
        m2 = sb("m2", [P, PAIRS])
        gub = sb("gub", [P, EM, 2 * JT])

        ga, up, sg, gu, af = ([sb(f"m_{n}{k}", [P, TB]) for k in range(2)] for n in ("ga", "up", "sg", "gu", "af"))
        ah = [sb(f"ah{k}", [P, JT, TB], F32R) for k in range(2)]
        al = [sb(f"al{k}", [P, JT, TB], F32R) for k in range(2)]
        m_in, m_zero, m_l_ready, m_soft, m_step, m_c = (sem(n) for n in (
            "m_small_in", "m_acc_zeroed", "m_logits_ready", "m_exp", "m_router_step", "m_combine"))
        m_gu_ready, m_gu, m_sg, m_t, m_a, m_ah, m_al, m_d_ready, m_d = (sem(n) for n in (
            "m_gate_up_ready", "m_gate_up_clipped", "m_sigmoid", "m_product", "m_act",
            "m_act_hi", "m_act_lo", "m_down_ready", "m_down_added"))
        m_ct_ready, m_ct = sem("m_combineT_ready"), sem("m_combineT_copied")
        LAST = EM * NTB * JT - 1

        def steps(two_experts, eng, peel=0):
            two_experts(0)
            with eng.Fori(1, EM // 2 - peel) as t:
                two_experts(t)
            for t in range(EM // 2 - peel, EM // 2):
                two_experts(t)

        def last(t, par):
            return isinstance(t, int) and t * 2 + par == EM - 1

        with nc.Block() as block:
            @block.sync
            def _(sp):


                sp.dma_start(rb[:, :], io["m_rb"].partition_broadcast(P)).then_inc(m_in, 16)
                sp.dma_start(gub[:, :, :], io["m_gub"]).then_inc(m_in, 16)
                sp.dma_start(db[:, :], io["m_db"]).then_inc(m_in, 16)
                with sp.Fori(1, EM) as e:
                    load_experts_weights(sp, io, e, ws, m_w, m_wlo)

            @block.tensor
            def _(pe):
                for t in range(PAIRS):
                    mm = pe.transpose(banks[7][:, t * EM:(t + 1) * EM], lgT[:, t * P:(t + 1) * P], ident[0:EM, 0:EM])
                mm.then_inc(m_l_ready, 1)

                def combine():
                    pe.wait_ge(m_c, 1)
                    for t in range(PAIRS):
                        mm = pe.transpose(banks[4 + t // 4][0:EM, (t % 4) * P:(t % 4 + 1) * P], cb[:, t, :], ident[:, :])
                        if t % 4 == 3:
                            mm.then_inc(m_ct_ready, 1)

                def gate_up(n, tb, par, j):
                    m = n * JT + j
                    wait(pe, m_gu, m - 1)
                    for r in range(2):
                        for k in range(KT):
                            mm = mm3(pe, banks[2 * r + j % 2][:, :],
                                     [w[par][0][:, k, (r * JT + j) * P:(r * JT + j + 1) * P] for w in (wh, wl)],
                                     [h[:, k, tb * TB:(tb + 1) * TB] for h in (hh, hl)], k == 0, k == KT - 1)
                    mm.then_inc(m_gu_ready, 1)

                def down(n, par, wpar, b):
                    pe.wait_ge(m_al, n * JT + JT)
                    wait(pe, m_d, 2 * (n - 2) + b + 1)
                    for tt in range(2):
                        at = (2 * b + tt) * P
                        for j in range(JT):
                            mm = mm3(pe, banks[4 + 2 * par + b][:, tt * D:(tt + 1) * D],
                                     [a[par][:, j, at:at + P] for a in (ah, al)],
                                     [w[wpar][1][:, j, :] for w in (wh, wl)], j == 0, j == JT - 1)
                    mm.then_inc(m_d_ready, 1)

                def two_experts(t):
                    for par in range(2):
                        e = t * 2 + par
                        pe.wait_ge(m_wlo, e * 3 + 3)
                        for tb in range(NTB):
                            n = e * NTB + tb
                            for j in range(JT):
                                gate_up(n, tb, par, j)
                                if isinstance(n, int) and n * JT + j == 1:
                                    combine()
                                if j >= 2 and not (isinstance(n, int) and n == 0):
                                    if isinstance(n, int) and n <= 2:
                                        pe.wait_ge(m_ct, 2 * n)
                                    down(n - 1, (tb + 1) % 2, par if tb else 1 - par, j - 2)

                steps(two_experts, pe)
                for b in range(2):
                    down(EM * NTB - 1, 1, 1, b)

            @block.gpsimd
            def _(pool):


                def two_experts(t):
                    for par in range(2):
                        for tb in range(NTB):
                            for j in range(JT):
                                m = ((t * 2 + par) * NTB + tb) * JT + j
                                pool.wait_ge(m_t, m + 1)
                                wait(pool, m_al, m - 1)
                                pool.tensor_tensor(af[j % 2][:, :], gu[j % 2][:, :], sg[j % 2][:, :], ALU.mult).then_inc(m_a, 1)
                                if tb == 1 and j < 3 and not last(t, par):
                                    split_lo(pool, t * 2 + (par + 1), j, ws, wh[1 - par], wl[1 - par], m_whi, m_wlo)

                pool.memset(acc[:, :, :], 0.0).then_inc(m_zero, 1)
                steps(two_experts, pool, 1)

            @block.scalar
            def _(act):
                act.wait_ge(m_soft, 1)
                act.activation(lg[:, :, :], lg[:, :, :], ACT.Exp).then_inc(m_soft, 1)

                def a_hi(m, j, par):
                    act.wait_ge(m_a, m + 1)
                    act.activation(ah[par][:, j, :], af[j % 2][:, :], ACT.Copy).then_inc(m_ah, 1)

                def two_experts(t):
                    for par in range(2):
                        for tb in range(NTB):
                            n = (t * 2 + par) * NTB + tb
                            for j in range(JT):
                                m = n * JT + j
                                act.wait_ge(m_gu, m + 1)
                                wait(act, m_a, m - 1)
                                act.activation(sg[j % 2][:, :], ga[j % 2][:, :], ACT.Sigmoid, scale=SWIGLU_ALPHA).then_inc(m_sg, 1)
                                if isinstance(m, int) and m == 1:
                                    for q in range(PAIRS // 4):
                                        act.wait_ge(m_ct_ready, q + 1)
                                        act.activation(cbT[:, q * TB:(q + 1) * TB], banks[4 + q][0:EM, :],
                                                       ACT.Copy).then_inc(m_ct, 1)

                                if j == 1:
                                    wait(act, m_d_ready, 2 * (n - 1))
                                if j:
                                    a_hi(m - 1, j - 1, tb % 2)
                                elif not (isinstance(m, int) and m == 0):
                                    a_hi(m - 1, JT - 1, (tb + 1) % 2)
                                if tb == 1 and j < 3 and not last(t, par):
                                    split_hi(act, t * 2 + (par + 1), j, ws, wh[1 - par], m_w, m_whi)

                steps(two_experts, act, 1)
                a_hi(LAST, JT - 1, (NTB - 1) % 2)

            @block.vector
            def _(dve):
                cnt = [0]

                def then(ins):
                    ins.then_inc(m_step, 1)
                    cnt[0] += 1
                    dve.wait_ge(m_step, cnt[0])

                def route():
                    then(dve.memset(rank[:, :, :], 0.0))
                    for i in range(EM):
                        li = lg[:, :, i:i + 1]
                        if i:
                            dve.tensor_tensor(gt[:, :, 0:i], li.to_broadcast([P, PAIRS, i]), lg[:, :, 0:i], ALU.is_gt)
                        if i < EM - 1:
                            dve.tensor_tensor(gt[:, :, i + 1:EM], li.to_broadcast([P, PAIRS, EM - 1 - i]),
                                              lg[:, :, i + 1:EM], ALU.is_ge)
                        then(dve.memset(gt[:, :, i:i + 1], 0.0))
                        then(dve.tensor_tensor(rank[:, :, :], rank[:, :, :], gt[:, :, :], ALU.add))
                    then(dve.tensor_scalar(rank[:, :, :], rank[:, :, :], float(TOP_K), None, ALU.is_lt))
                    then(dve.tensor_reduce(m1[:, :], lg[:, :, :], AX.X, ALU.max))
                    dve.tensor_tensor(lg[:, :, :], lg[:, :, :], bcast(m1[:, :], 2, EM), ALU.subtract).then_inc(m_soft, 1)
                    dve.wait_ge(m_soft, 2)
                    then(dve.tensor_tensor(lg[:, :, :], lg[:, :, :], rank[:, :, :], ALU.mult))
                    then(dve.tensor_reduce(m1[:, :], lg[:, :, :], AX.X, ALU.add))
                    then(dve.reciprocal(m2[:, :], m1[:, :]))
                    dve.tensor_tensor(cb[:, :, :], lg[:, :, :], bcast(m2[:, :], 2, EM), ALU.mult).then_inc(m_c, 1)
                    dve.wait_ge(m_c, 1)

                def clip(e, m, j):
                    dve.wait_ge(m_gu_ready, m + 1)
                    wait(dve, m_t, m - 1)
                    dve.tensor_scalar(ga[j % 2][:, :], banks[j % 2][:, :],
                                      gub[:, bass.ds(e, 1), j:j + 1].rearrange("p a b -> p (a b)"), LIMIT,
                                      ALU.add, ALU.min)
                    dve.tensor_scalar(up[j % 2][:, :], banks[2 + j % 2][:, :],
                                      gub[:, bass.ds(e, 1), JT + j:JT + j + 1].rearrange("p a b -> p (a b)"), 1.0 - LIMIT,
                                      ALU.add, ALU.max).then_inc(m_gu, 1)

                def product(m, j):
                    dve.wait_ge(m_sg, m + 1)
                    wait(dve, m_a, m - 1)
                    dve.scalar_tensor_tensor(gu[j % 2][:, :], up[j % 2][:, :], 1.0 + LIMIT, ga[j % 2][:, :],
                                             ALU.min, ALU.mult).then_inc(m_t, 1)

                def a_lo(m, j, par):
                    dve.wait_ge(m_ah, m + 1)
                    dve.tensor_tensor(al[par][:, j, :], af[j % 2][:, :], ah[par][:, j, :].bitcast(F32),
                                      ALU.subtract).then_inc(m_al, 1)

                def add_down(e, n, tb, b):
                    dve.wait_ge(m_d_ready, 2 * n + b + 1)
                    if isinstance(n, int) and n < NTB:
                        dve.wait_ge(m_zero, 1)
                    wait(dve, m_d, 2 * (n - NTB) + b + 1)
                    for tt in range(2):
                        t = 4 * tb + 2 * b + tt
                        last = dve.scalar_tensor_tensor(
                            acc[:, t, :], banks[4 + 2 * (tb % 2) + b][:, tt * D:(tt + 1) * D],
                            cb[:, t, bass.ds(e, 1)], acc[:, t, :], ALU.mult, ALU.add)
                    last.then_inc(m_d, 1)

                dve.wait_ge(m_in, 48)
                then(dve.tensor_scalar(gub[:, :, JT:2 * JT], gub[:, :, JT:2 * JT], 1.0, None, ALU.add))
                dve.wait_ge(m_l_ready, 1)
                then(dve.tensor_tensor(lg[:, :, :], banks[7][:, 0:PAIRS * EM].rearrange("p (t e) -> p t e", e=EM),
                                       bcast(rb[:, :], 1, PAIRS), ALU.add))
                route()

                def two_experts(t):
                    for par in range(2):
                        e = t * 2 + par
                        for tb in range(NTB):
                            n = e * NTB + tb
                            for j in range(JT):
                                m = n * JT + j
                                clip(e, m, j)
                                if not (isinstance(m, int) and m < 2):
                                    a_lo(m - 2, (j - 2) % JT, (tb if j >= 2 else tb + 1) % 2)
                                if not (isinstance(m, int) and m < 1):
                                    product(m - 1, (j - 1) % JT)
                                for lag, at, b in ((1, JT - 1, 0), (2, JT - 2, 1)):
                                    if j == at and not (isinstance(n, int) and n < lag):
                                        add_down(e if tb >= lag else e - 1, n - lag, (tb - lag) % NTB, b)

                steps(two_experts, dve)
                product(LAST, JT - 1)
                a_lo(LAST - 1, JT - 2, 1)
                a_lo(LAST, JT - 1, 1)
                add_down(EM - 1, EM * NTB - 2, NTB - 2, 1)
                for b in range(2):
                    add_down(EM - 1, EM * NTB - 1, NTB - 1, b)


def lora_ffn(nc, io, banks, sb0, sem, xT, zT, acc, cbT, db, ident, oh_lora):
    with ExitStack() as c:
        def sb(name, shape, dt=F32):
            return sb0(name, shape, dt, c)

        wi = sb("wi", [P, KT, FF])
        wo = sb("l_wo", [P, FT, D])
        cia = sb("cia", [RL, D])
        cib = sb("cib", [RL, FF])
        coa = sb("coa", [RL, FF])
        cob = sb("cob", [RL, D])
        eia = sb("eia", [P, KT, P])
        eib = sb("eib", [P, FF])
        eoa = sb("eoa", [P, FT, P])
        eob = sb("eob", [P, D])

        def halves(name, t):
            return [sb(f"{name}_{part}", list(t.shape), F32R) for part in ("hi", "lo")]

        wi2, wo2, eia2, eib2, eoa2, eob2, x2 = (halves(n, t) for n, t in (
            ("wi", wi), ("l_wo", wo), ("eia", eia), ("eib", eib), ("eoa", eoa), ("eob", eob), ("x", zT)))
        low2 = [sb(f"low_{part}", [P, N], F32R) for part in ("hi", "lo")]
        low = [sb(f"low{k}", [P, TB]) for k in range(2)]
        lowo2 = [sb(f"lowo_{part}", [P, TB], F32R) for part in ("hi", "lo")]
        hid2 = [[sb(f"hid{k}_{part}", [P, TB], F32R) for part in ("hi", "lo")] for k in range(2)]
        l_small, l_wi, l_wo = (sem(n) for n in ("l_common_in", "l_wi_in", "l_wo_in"))
        l_e = [sem(f"l_{n}_in") for n in ("eia", "eib", "eoa", "eob")]
        (l_s_ready, l_x, l_xh, l_xl, l_f_ready, l_f, l_wh, l_wl, l_low_ready, l_low, l_lowh, l_lowl) = (
            sem(n) for n in ("l_sum_ready", "l_x_summed", "l_x_hi", "l_x_lo", "l_fold_ready", "l_folded",
                             "l_weights_hi", "l_weights_lo", "l_low_ready", "l_low_masked", "l_low_hi", "l_low_lo"))
        l_h_ready, l_hh, l_hl, l_lo_ready, l_lo, l_loh, l_lol, l_o_ready, l_o = (
            sem(n) for n in ("l_hidden_ready", "l_relu_hi", "l_relu_lo", "l_lowo_ready", "l_lowo_masked",
                             "l_lowo_hi", "l_lowo_lo", "l_out_ready", "l_out_copied"))
        FW, FO = KT * 2, FT // 2
        XN = NTB * KT

        def fold(t, n):
            wi_, wo_ = t
            if n < FW:
                return wi_[:, n // 2, (n % 2) * 512:(n % 2 + 1) * 512]
            return wo_[:, 2 * (n - FW):2 * (n - FW) + 2, :]

        pieces = [(eia[:, :, :], eia2, 0), (eib[:, :], eib2, 1)]
        pieces += [(fold((wi, wo), n), [fold((wi2[r], wo2[r]), n) for r in range(2)], None) for n in range(FW + FO)]
        pieces += [(eoa[:, :, :], eoa2, 2), (eob[:, :], eob2, 3)]
        UP, OUT = 2 + FW, 3 + FW + FO

        def x_piece(t, n):
            return t[:, n % KT, (n // KT) * TB:(n // KT + 1) * TB]

        def by(ap):
            return ap.rearrange("p (b n) -> p b n", n=S)

        def steps(two, eng):
            two(0)
            with eng.Fori(1, NTB // 2) as t:
                two(t)

        def first(u):
            return isinstance(u, int) and u == 0

        with nc.Block() as block:
            @block.sync
            def _(sp):
                sp.dma_start(eia[:, :, :], io["l_eiaT"].rearrange("(k p) n -> p k n", p=P)).then_inc(l_e[0], 16)
                sp.dma_start(eib[:, :], io["l_eibT"]).then_inc(l_e[1], 16)
                for dst, name in ((cia, "l_cia"), (cib, "l_cibT"), (coa, "l_coa"), (cob, "l_cobT")):
                    sp.dma_start(dst[:, :], io[name]).then_inc(l_small, 16)
                sp.dma_start(wi[:, :, :], io["l_wiT"].rearrange("(k p) n -> p k n", p=P)).then_inc(l_wi, 16)
                sp.dma_start(wo[:, :, :], io["l_woT"].rearrange("(k p) n -> p k n", p=P)).then_inc(l_wo, 16)
                sp.dma_start(eoa[:, :, :], io["l_eoaT"].rearrange("(k p) n -> p k n", p=P)).then_inc(l_e[2], 16)
                sp.dma_start(eob[:, :], io["l_eobT"]).then_inc(l_e[3], 16)

            @block.tensor
            def _(pe):
                for n in range(XN):
                    t, o = n // KT, n % KT
                    if n >= 4:
                        pe.wait_ge(l_x, n - 3)
                    pe.matmul(banks[n % 4][:, :], db[:, o * P:(o + 1) * P], cbT[:, t * TB:(t + 1) * TB],
                              start=True, stop=False)
                    for j in range(TB // P):
                        mm = pe.matmul(banks[n % 4][:, j * P:(j + 1) * P], acc[:, t * 4 + j, o * P:(o + 1) * P],
                                       ident[:, :], start=False, stop=j == TB // P - 1)
                    mm.then_inc(l_s_ready, 1)
                pe.wait_ge(l_small, 64)
                for n in range(FW + FO):
                    if n >= 4:
                        pe.wait_ge(l_f, n - 3)
                    if n < FW:
                        k, f = n // 2, n % 2
                        mm = pe.matmul(banks[4 + n % 4][:, :], cia[:, k * P:(k + 1) * P], cib[:, f * 512:(f + 1) * 512],
                                       start=True, stop=True)
                    else:
                        for g in range(2):
                            at = (2 * (n - FW) + g) * P
                            mm = pe.matmul(banks[4 + n % 4][:, g * D:(g + 1) * D], coa[:, at:at + P], cob[:, :],
                                           start=True, stop=True)
                    mm.then_inc(l_f_ready, 1)
                pe.wait_ge(l_wl, 1)
                for t in range(NTB):
                    pe.wait_ge(l_xl, KT * t + KT)
                    pe.wait_ge(l_x, min(XN, XN - NTB + t + 1))
                    for k in range(KT):
                        mm = mm3(pe, banks[t][:, :], [w[:, k, :] for w in eia2],
                                 [x[:, k, t * TB:(t + 1) * TB] for x in x2], k == 0, k == KT - 1)
                    mm.then_inc(l_low_ready, 1)
                pe.wait_ge(l_wl, UP)

                def up(u, f):
                    m = FT * u + f
                    if isinstance(m, int) and m < 2:
                        pe.wait_ge(l_lowl, m + 1)
                    wait(pe, l_hl, m - 1)
                    at = bass.ds(u * TB, TB)
                    for k in range(KT):
                        mm3(pe, banks[f % 2][:, :], [w[:, k, f * P:(f + 1) * P] for w in wi2],
                            [x[:, k, at] for x in x2], k == 0, False)
                    if f == 0 and isinstance(u, int):
                        pe.wait_ge(l_lowl, u + 1)
                    mm3(pe, banks[f % 2][:, :], [w[:, f * P:(f + 1) * P] for w in eib2], [x[:, at] for x in low2],
                        False, True).then_inc(l_h_ready, 1)

                def second(u, par, f):
                    pe.wait_ge(l_hl, FT * u + (f + 1))
                    if f == 0:
                        if isinstance(u, int) and u < 2:
                            pe.wait_ge(l_low, NTB)
                            pe.wait_ge(l_wl, OUT)
                        wait(pe, l_o, u - 1)
                    mm = mm3(pe, banks[2 + par][:, :], [w[:, f, :] for w in eoa2], [h[:, :] for h in hid2[f % 2]],
                             f == 0, f == FT - 1)
                    if f == FT - 1:
                        mm.then_inc(l_lo_ready, 1)
                    for o in range(KT):
                        mm3(pe, banks[4 + 2 * par + o][:, :], [w[:, f, o * P:(o + 1) * P] for w in wo2],
                            [h[:, :] for h in hid2[f % 2]], f == 0, False)

                def finish(u, par):
                    pe.wait_ge(l_lol, u + 1)
                    if first(u):
                        pe.wait_ge(l_wl, len(pieces))
                    for o in range(KT):
                        mm = mm3(pe, banks[4 + 2 * par + o][:, :], [w[:, o * P:(o + 1) * P] for w in eob2],
                                 [x[:, :] for x in lowo2], False, True)
                    mm.then_inc(l_o_ready, 1)

                def two(t):
                    for par in range(2):
                        u = t * 2 + par
                        for f in range(FT):
                            up(u, f)
                            if f == 0 and not first(u):
                                second(u - 1, 1 - par, FT - 1)
                            if f == 1 and not first(u):
                                finish(u - 1, 1 - par)
                            if f:
                                second(u, par, f - 1)

                steps(two, pe)
                second(NTB - 1, 1, FT - 1)
                finish(NTB - 1, 1)

            @block.gpsimd
            def _(pool):
                for n, (src, (hi, lo), _) in enumerate(pieces):
                    pool.wait_ge(l_wh, n + 1)
                    pool.tensor_tensor(whole(lo), src, whole(hi).bitcast(F32), ALU.subtract).then_inc(l_wl, 1)

            @block.scalar
            def _(act):
                def split(n):
                    src, (hi, _), loaded = pieces[n]
                    if loaded is None:
                        act.wait_ge(l_f, n - 1)
                    else:
                        act.wait_ge(l_e[loaded], 16)
                    act.activation(whole(hi), src, ACT.Copy).then_inc(l_wh, 1)

                for n in range(XN):
                    if n in (2, 4):
                        split(n // 2 - 1)
                    act.wait_ge(l_x, n + 1)
                    act.activation(x_piece(x2[0], n), x_piece(xT, n), ACT.Copy).then_inc(l_xh, 1)
                for n in range(2, 2 + FW + FO):
                    split(n)
                for t in range(NTB):
                    act.wait_ge(l_low, t + 1)
                    act.activation(low2[0][:, t * TB:(t + 1) * TB], low[t % 2][:, :], ACT.Copy).then_inc(l_lowh, 1)
                split(2 + FW + FO)
                split(3 + FW + FO)

                def lowo_hi(u):
                    act.wait_ge(l_lo, u + 1)
                    wait(act, l_o_ready, u)
                    act.activation(lowo2[0][:, :], low[0][:, :], ACT.Copy).then_inc(l_loh, 1)

                def two(t):
                    for par in range(2):
                        u = t * 2 + par
                        for f in range(FT):
                            if f == 1 and not first(u):
                                lowo_hi(u - 1)
                            act.wait_ge(l_h_ready, FT * u + (f + 1))
                            act.activation(hid2[f % 2][0][:, :], banks[f % 2][:, :], ACT.Relu).then_inc(l_hh, 1)

                steps(two, act)
                lowo_hi(NTB - 1)

            @block.vector
            def _(dve):
                def x_lo(n):
                    dve.wait_ge(l_xh, n + 1)
                    dve.tensor_tensor(x_piece(x2[1], n), x_piece(xT, n), x_piece(x2[0], n).bitcast(F32),
                                      ALU.subtract).then_inc(l_xl, 1)

                for n in range(XN):
                    dve.wait_ge(l_s_ready, n + 1)
                    at = x_piece(xT, n)
                    dve.tensor_tensor(at, banks[n % 4][:, :], at, ALU.add).then_inc(l_x, 1)
                    if n:
                        x_lo(n - 1)
                x_lo(XN - 1)
                for n in range(FW + FO):
                    dve.wait_ge(l_f_ready, n + 1)
                    if n == 0:
                        dve.wait_ge(l_wi, 16)
                    if n == FW:
                        dve.wait_ge(l_wo, 16)
                    at = fold((wi, wo), n)
                    bank = banks[4 + n % 4][:, :]
                    if n >= FW:
                        bank = bank.rearrange("p (g n) -> p g n", g=2)
                    dve.scalar_tensor_tensor(at, bank, 2.0, at, ALU.mult, ALU.add).then_inc(l_f, 1)
                for t in range(NTB):
                    dve.wait_ge(l_low_ready, t + 1)
                    if t >= 2:
                        dve.wait_ge(l_lowl, t - 1)
                    dve.tensor_tensor(by(low[t % 2][:, :]), by(banks[t][:, :]),
                                      bcast(oh_lora[:, t * (TB // S):(t + 1) * (TB // S)], 2, S), ALU.mult).then_inc(l_low, 1)
                    dve.wait_ge(l_lowh, t + 1)
                    at = slice(t * TB, (t + 1) * TB)
                    dve.tensor_tensor(low2[1][:, at], low[t % 2][:, :], low2[0][:, at].bitcast(F32),
                                      ALU.subtract).then_inc(l_lowl, 1)

                def mask(u, par):
                    dve.wait_ge(l_lo_ready, u + 1)
                    if first(u):
                        dve.wait_ge(l_lowl, NTB)
                    wait(dve, l_lol, u)
                    dve.tensor_tensor(by(low[0][:, :]), by(banks[2 + par][:, :]),
                                      bcast(oh_lora[:, bass.ds(u * (TB // S), TB // S)], 2, S), ALU.mult).then_inc(l_lo, 1)

                def lowo_lo(u):
                    dve.wait_ge(l_loh, u + 1)
                    dve.tensor_tensor(lowo2[1][:, :], low[0][:, :], lowo2[0][:, :].bitcast(F32),
                                      ALU.subtract).then_inc(l_lol, 1)

                def store(u, par):
                    dve.wait_ge(l_o_ready, u + 1)
                    for o in range(KT):
                        last = dve.tensor_copy(zT[:, o, bass.ds(u * TB, TB)], banks[4 + 2 * par + o][:, :])
                    last.then_inc(l_o, 1)

                def two(t):
                    for par in range(2):
                        u = t * 2 + par
                        for f in range(FT):
                            if f == 1 and not first(u):
                                lowo_lo(u - 1)
                            dve.wait_ge(l_hh, FT * u + (f + 1))
                            dve.scalar_tensor_tensor(hid2[f % 2][1][:, :], banks[f % 2][:, :], 0.0,
                                                     hid2[f % 2][0][:, :].bitcast(F32), ALU.max, ALU.subtract).then_inc(l_hl, 1)
                            if f == 0 and not first(u):
                                mask(u - 1, 1 - par)
                            if f == 2 and not first(u):
                                store(u - 1, 1 - par)

                steps(two, dve)
                mask(NTB - 1, 1)
                lowo_lo(NTB - 1)
                store(NTB - 1, 1)


def attention1(nc, io, banks, sb0, sem, xT, zT, ident, mask):
    with ExitStack() as c:
        def sb(name, shape, dt=F32):
            return sb0(name, shape, dt, c)

        HT = P // HD1
        wat = sb("wat", [P, KT, 3 * D])
        bat = sb("bat", [P, 4])
        bv = sb("bv", [P, D])
        fac = sb("fac", [P, 2, S])
        hm = sb("hm", [P, HT])
        wp = sb("wp", [P, KT, D])
        bp = sb("bp", [P, KT])
        zs = [sb(f"zs{k}", [P, KT, P]) for k in range(2)]
        qT = [sb(f"qT{k}", [P, 2, P]) for k in range(2)]
        kT = sb("kT", [P, 2, P])
        kpad = sb("k1pad", [P, 2, HT, P])
        v = [sb(f"vp{k}", [P, HEADS, 32]) for k in range(2)]
        sc = sb("sc1", [P, HEADS, S])
        ex = sb("ex1", [P, HEADS, S])
        mx = sb("mx1", [P, HEADS])
        sm = sb("sm1", [P, HEADS])
        ri = sb("ri1", [P, HEADS])
        pr = [sb(f"pr1_{k}", [P, HEADS, P]) for k in range(2)]
        prT = sb("prT1", [P, HEADS, P])
        ctxT = sb("ctxT1", [P, 2, P])
        n_in, n_zero, n_zs, n_qk_ready, n_qk, n_kp, n_v_ready, n_v, n_vm = (sem(n) for n in (
            "n_in", "n_zeroed", "n_z_staged", "n_qk_ready", "n_qk_scaled", "n_k_spread", "n_v_ready", "n_v_copied", "n_v_moved"))
        n_s_ready, n_s, n_mx, n_sub, n_exp, n_sum, n_rec, n_p0, n_p, n_tp_ready, n_tp, n_c_ready, n_c, n_o_ready, n_o = (
            sem(n) for n in ("n_s_ready", "n_s_masked", "n_max", "n_subtracted", "n_exp", "n_sum", "n_recip", "n_probs_half", "n_probs",
                             "n_trp_ready", "n_trp_copied", "n_ctx_ready", "n_ctx_copied", "n_out_ready", "n_out_added"))

        with nc.Block() as block:
            @block.sync
            def _(sp):
                for dst, name in ((bat, "n_bat"), (hm, "n_hm"), (bp, "n_bp")):
                    sp.dma_start(dst[:, :], io[name]).then_inc(n_in, 16)
                sp.dma_start(bv[:, :], io["n_bv"].partition_broadcast(P)).then_inc(n_in, 16)
                sp.dma_start(fac[:, :, :], io["n_fac"]).then_inc(n_in, 16)
                for dst, name in ((wat, "n_waT"), (wp, "n_wpT")):
                    sp.dma_start(dst[:, :, :], io[name].rearrange("(k p) n -> p k n", p=P)).then_inc(n_in, 16)

            @block.gpsimd
            def _(pool):
                for t in v + pr:
                    pool.memset(t[:, :, :], 0.0).then_inc(n_zero, 1)
                pool.wait_ge(n_in, 112)

                def step(i, par):
                    if live(i + 1):
                        p = i + 1
                        wait(pool, n_v_ready, p - 1)
                        pool.tensor_copy(zs[1 - par][:, :, :], zT[:, :, bass.ds(p * P, P)]).then_inc(n_zs, 1)

                    if live(i):
                        wait(pool, n_s_ready, 4 * (i - 1) + 4)
                        pool.wait_ge(n_qk, i + 1)
                        for t in range(2):
                            last = pool.tensor_tensor(kpad[:, t, :, :], bcast(kT[:, t, :], 1, HT), bcast(hm[:, :], 2, P), ALU.mult)
                        last.then_inc(n_kp, 1)
                    if live(i - 1):
                        if isinstance(i, int) and i == 1:
                            pool.wait_ge(n_zero, 4)
                        wait(pool, n_tp_ready, 4 * (i - 3) + 4)
                        if live(i):
                            pool.wait_ge(n_kp, i + 1)
                        if live(i + 1):
                            pool.wait_ge(n_zs, i + 2)
                        pool.wait_ge(n_rec, i)
                        dst = pr[1 - par]
                        pool.tensor_tensor(dst[0:S, :, 0:S], ex[0:S, :, :], bcast(ri[0:S, :], 2, S), ALU.mult).then_inc(n_p0, 1)
                        pool.wait_ge(n_p0, i)
                        pool.tensor_tensor(dst[S:P, :, S:P], ex[S:P, :, :], bcast(ri[S:P, :], 2, S), ALU.mult).then_inc(n_p, 1)
                        pool.wait_ge(n_p, i)

                pipeline(pool, step)

            @block.tensor
            def _(pe):
                pe.wait_ge(n_in, 112)

                def step(i, par):
                    if live(i - 1):
                        p = i - 1
                        pe.wait_ge(n_kp, p + 1)
                        for f in range(4):
                            wait(pe, n_s, 4 * p + f - 1)
                            pe.matmul(banks[4 + f % 2][:, :], qT[1 - par][:, f // 2, :],
                                      kpad[:, f // 2, 4 * (f % 2):4 * (f % 2) + 4, :], start=True, stop=True).then_inc(n_s_ready, 1)
                        wait(pe, n_v, i - 1)
                        for k in range(KT):
                            mm = pe.matmul(banks[2][:, 0:D], zs[1 - par][:, k, :], wat[:, k, 2 * D:3 * D], start=k == 0,
                                           stop=k == KT - 1)
                        mm.then_inc(n_v_ready, 1)
                    if live(i):
                        pe.wait_ge(n_zs, i + 1)
                        wait(pe, n_qk, i)
                        for t in range(4):
                            for k in range(KT):
                                mm = pe.matmul(banks[1][:, t * P:(t + 1) * P], wat[:, k, t * P:(t + 1) * P], zs[par][:, k, :],
                                               start=k == 0, stop=k == KT - 1)
                        mm.then_inc(n_qk_ready, 1)
                    if live(i - 3):
                        p = i - 3
                        pe.wait_ge(n_c, p + 1)
                        wait(pe, n_o, p)
                        for o in range(KT):
                            for k in range(KT):
                                mm = pe.matmul(banks[0][:, o * P:(o + 1) * P], wp[:, k, o * P:(o + 1) * P], ctxT[:, k, :],
                                               start=k == 0, stop=k == KT - 1)
                        mm.then_inc(n_o_ready, 1)
                    if live(i - 2):
                        p = i - 2
                        pe.wait_ge(n_p, p + 1)
                        for f in range(4):
                            wait(pe, n_tp, 4 * p + f - 1)
                            for j in range(4):
                                mm = pe.transpose(banks[6 + f % 2][:, j * P:(j + 1) * P], pr[par][:, 4 * f + j, :], ident[:, :])
                            mm.then_inc(n_tp_ready, 1)
                    if live(i - 2):
                        p = i - 2
                        pe.wait_ge(n_tp, 4 * p + 4)
                        for t in range(2):
                            for q in range(4):
                                for s in range(2):
                                    h = 8 * t + 2 * q + s
                                    mm = pe.matmul(banks[3][32 * q:32 * q + 32, t * P:(t + 1) * P], v[par][:, h, :],
                                                   prT[:, h, :], start=s == 0, stop=s == 1)
                        mm.then_inc(n_c_ready, 1)

                pipeline(pe, step)

            @block.scalar
            def _(act):
                def step(i, par):
                    if live(i - 2):
                        p = i - 2
                        for f in range(4):
                            act.wait_ge(n_tp_ready, 4 * p + f + 1)
                            act.activation(prT[:, 4 * f:4 * f + 4, :], banks[6 + f % 2][:, :].rearrange(
                                "p (t n) -> p t n", n=P), ACT.Copy).then_inc(n_tp, 1)
                        act.wait_ge(n_c_ready, p + 1)
                        act.activation(ctxT[:, :, :], banks[3][:, 0:2 * P].rearrange("p (t n) -> p t n", n=P),
                                       ACT.Copy).then_inc(n_c, 1)
                    if live(i - 1):
                        act.wait_ge(n_sub, i)
                        wait(act, n_p, i - 1)
                        act.activation(ex[:, :, :], sc[:, :, :], ACT.Exp).then_inc(n_exp, 1)

                pipeline(act, step)

            @block.vector
            def _(dve):
                dve.wait_ge(n_in, 112)

                def step(i, par):
                    if live(i - 1):
                        p = i - 1
                        wait(dve, n_exp, p)
                        for f in range(4):
                            dve.wait_ge(n_s_ready, 4 * p + f + 1)
                            for s in range(2):
                                rows = slice(S * s, S * s + S)
                                last = dve.tensor_tensor(
                                    sc[rows, 4 * f:4 * f + 4, :],
                                    banks[4 + f % 2][rows, :].rearrange("p (h n) -> p h n", n=P)[:, :, S * s:S * s + S],
                                    bcast(mask[rows, :], 1, 4), ALU.add)
                            last.then_inc(n_s, 1)
                        dve.wait_ge(n_s, 4 * p + 4)
                        dve.tensor_reduce(mx[:, :], sc[:, :, :], AX.X, ALU.max).then_inc(n_mx, 1)
                        dve.wait_ge(n_mx, p + 1)
                        dve.tensor_tensor(sc[:, :, :], sc[:, :, :], bcast(mx[:, :], 2, S), ALU.subtract).then_inc(n_sub, 1)
                    if live(i - 1):
                        dve.wait_ge(n_v_ready, i)
                        if isinstance(i, int) and i == 1:
                            dve.wait_ge(n_zero, 2)
                        for s in range(2):
                            vv = v[1 - par][:, s:HEADS:2, HD1 * s:HD1 * s + HD1]
                            last = dve.tensor_tensor(
                                vv, banks[2][:, 0:D].rearrange("p (h s d) -> p h s d", s=2, d=HD1)[:, :, s, :],
                                bv[:, :].rearrange("p (h s d) -> p h s d", s=2, d=HD1)[:, :, s, :], ALU.add)
                        last.then_inc(n_v, 1)
                    if live(i):
                        dve.wait_ge(n_qk_ready, i + 1)
                        wait(dve, n_kp, i)
                        for t in range(4):
                            dst = (qT[par] if t < 2 else kT)[:, t % 2, :]
                            last = dve.scalar_tensor_tensor(
                                dst.rearrange("p (s n) -> p s n", s=2),
                                banks[1][:, t * P:(t + 1) * P].rearrange("p (s n) -> p s n", s=2), bat[:, t:t + 1],
                                bcast(fac[:, t // 2, :], 1, 2), ALU.add, ALU.mult)
                        last.then_inc(n_qk, 1)
                    if live(i - 1):
                        p = i - 1
                        dve.wait_ge(n_exp, p + 1)
                        wait(dve, n_p, p)
                        dve.tensor_reduce(sm[:, :], ex[:, :, :], AX.X, ALU.add).then_inc(n_sum, 1)
                        dve.wait_ge(n_sum, p + 1)
                        dve.reciprocal(ri[:, :], sm[:, :]).then_inc(n_rec, 1)

                    if live(i - 3):
                        p = i - 3
                        dve.wait_ge(n_o_ready, p + 1)
                        for o in range(KT):
                            at = xT[:, o, bass.ds(p * P, P)]
                            last = dve.scalar_tensor_tensor(at, banks[0][:, o * P:(o + 1) * P], bp[:, o:o + 1], at,
                                                            ALU.add, ALU.add)
                        last.then_inc(n_o, 1)

                pipeline(dve, step)


def adapter_ffn(nc, io, banks, sb0, sem, xT, oh_lang, oh_lang10, out):
    with ExitStack() as c:
        def sb(name, shape, dt=F32):
            return sb0(name, shape, dt, c)

        BS = TB // S
        w1 = sb("f_w1", [P, KT, LANG * A2])
        b1 = sb("f_b1", [P, LT])
        w2 = sb("f_w2", [P, LT, D])
        tab = sb("f_tab", [LANG, 3, D])
        wt = sb("f_wt", [P, KT, D])
        vr = sb("f_vr", [32, D])
        ct = sb("f_ct", [32, D])
        fb = sb("f_b", [P, KT])
        ones = sb("f_ones", [P, P])
        ps = sb("f_ps", [P, 3, KT, B])
        hl = [sb(f"f_h{k}", [P, TB]) for k in range(LT)]
        r = sb("f_r", [P, KT, TB])
        sq = sb("f_sq", [P, KT, TB])
        rstd = sb("f_rstd", [P, TB])

        (f_in, f_t_ready, f_t, f_w_ready, f_w, f_h_ready, f_h, f_hm, f_a_ready, f_a, f_r, f_m_ready, f_cn, f_sq,
         f_v_ready, f_sd, f_rs, f_n, f_o_ready, f_o) = (sem(n) for n in (
             "f_in", "f_tables_ready", "f_tables", "f_fold_ready", "f_folded", "f_h_ready", "f_relu", "f_masked",
             "f_adapter_ready", "f_biased", "f_residual", "f_mean_ready", "f_centred", "f_squared", "f_var_ready",
             "f_std", "f_rstd", "f_normed", "f_out_ready", "f_out_added"))
        f_st = sem("f_stored")

        with nc.Block() as block:
            @block.sync
            def _(sp):
                for dst, name in ((b1, "f_b1"), (vr, "f_vrT"), (ct, "f_cT"), (fb, "f_b"), (ones, "f_ones")):
                    sp.dma_start(dst[:, :], io[name]).then_inc(f_in, 16)
                sp.dma_start(tab[:, :, :], io["f_tab"]).then_inc(f_in, 16)
                for dst, name in ((w1, "f_w1"), (w2, "f_w2"), (wt, "f_wT")):
                    sp.dma_start(dst[:, :, :], io[name].rearrange("(k p) n -> p k n", p=P)).then_inc(f_in, 16)
                for t in range(NTB):
                    sp.wait_ge(f_o, t + 1)
                    sp.dma_start(out[:, t * TB:(t + 1) * TB].rearrange("(k p) n -> p k n", p=P),
                                 xT[:, :, t * TB:(t + 1) * TB]).then_inc(f_st, 16)
                sp.wait_ge(f_st, 16 * NTB)

            @block.tensor
            def _(pe):
                pe.wait_ge(f_in, 144)
                for k in range(KT):
                    mm = pe.matmul(banks[0][:, k * D:(k + 1) * D], vr[:, k * P:(k + 1) * P], ct[:, :], start=True, stop=True)
                mm.then_inc(f_w_ready, 1)
                for w in range(3):
                    for k in range(KT):
                        at = (w * KT + k) * B
                        mm = pe.matmul(banks[1][:, at:at + B], tab[:, w, k * P:(k + 1) * P], oh_lang10[:, :],
                                       start=True, stop=True)
                mm.then_inc(f_t_ready, 1)
                pe.wait_ge(f_w, 1)
                pe.wait_ge(f_t, 1)
                with pe.Fori(0, NTB) as tb:
                    for j in range(LT):
                        if j >= 2:
                            pe.wait_ge(f_h, LT * tb + (j - 1))
                        for k in range(KT):
                            mm = pe.matmul(banks[j % 2][:, :], w1[:, k, j * P:(j + 1) * P], xT[:, k, bass.ds(tb * TB, TB)],
                                           start=k == 0, stop=k == KT - 1)
                        mm.then_inc(f_h_ready, 1)
                    for j in range(LT):
                        pe.wait_ge(f_hm, LT * tb + (j + 1))
                        for o in range(KT):
                            mm = pe.matmul(banks[2 + o][:, :], w2[:, j, o * P:(o + 1) * P], hl[j][:, :], start=j == 0,
                                           stop=j == LT - 1)
                    mm.then_inc(f_a_ready, 1)
                    pe.wait_ge(f_r, tb + 1)
                    for k in range(KT):
                        mm = pe.matmul(banks[4][:, :], ones[:, :], r[:, k, :], start=k == 0, stop=k == KT - 1)
                    mm.then_inc(f_m_ready, 1)
                    pe.wait_ge(f_sq, tb + 1)
                    for k in range(KT):
                        mm = pe.matmul(banks[5][:, :], ones[:, :], sq[:, k, :], start=k == 0, stop=k == KT - 1)
                    mm.then_inc(f_v_ready, 1)
                    pe.wait_ge(f_n, tb + 1)
                    for o in range(KT):
                        for k in range(KT):
                            mm = pe.matmul(banks[6 + o][:, :], wt[:, k, o * P:(o + 1) * P], r[:, k, :], start=k == 0,
                                           stop=k == KT - 1)
                    mm.then_inc(f_o_ready, 1)
                    pe.wait_ge(f_o, tb + 1)

            @block.scalar
            def _(act):
                act.wait_ge(f_in, 144)
                with act.Fori(0, NTB) as tb:
                    for j in range(LT):
                        act.wait_ge(f_h_ready, LT * tb + (j + 1))
                        act.activation(hl[j][:, :], banks[j % 2][:, :], ACT.Relu, bias=b1[:, j:j + 1]).then_inc(f_h, 1)
                    act.wait_ge(f_cn, tb + 1)
                    act.activation(sq[:, :, :], r[:, :, :], ACT.Square).then_inc(f_sq, 1)
                    act.wait_ge(f_rs, tb * 2 + 1)
                    act.activation(rstd[:, :], rstd[:, :], ACT.Sqrt).then_inc(f_sd, 1)

            @block.gpsimd
            def _(pool):
                with pool.Fori(0, NTB) as tb:
                    for j in range(LT):
                        pool.wait_ge(f_h, LT * tb + (j + 1))
                        hj = hl[j][:, :].rearrange("p (b n) -> p b n", n=S)
                        pool.tensor_tensor(hj, hj, bcast(oh_lang[:, j, bass.ds(tb * BS, BS)], 2, S), ALU.mult).then_inc(f_hm, 1)

            @block.vector
            def _(dve):
                dve.wait_ge(f_in, 144)
                dve.wait_ge(f_w_ready, 1)
                dve.tensor_tensor(wt[:, :, :], banks[0][:, :].rearrange("p (k n) -> p k n", k=KT), wt[:, :, :],
                                  ALU.add).then_inc(f_w, 1)
                dve.wait_ge(f_t_ready, 1)
                dve.tensor_copy(ps[:, :, :, :], banks[1][:, 0:3 * KT * B].rearrange("p (w k b) -> p w k b", w=3, k=KT)).then_inc(f_t, 1)
                dve.wait_ge(f_t, 1)

                def by(ap):
                    return ap.rearrange("p (b n) -> p b n", n=S)

                with dve.Fori(0, NTB // 2) as t2:
                    for par in range(2):
                        tb = t2 * 2 + par

                        def of(w, k):
                            return bcast(ps[:, w, k, bass.ds(tb * BS, BS)], 2, S)

                        dve.wait_ge(f_a_ready, tb + 1)
                        for k in range(KT):
                            last = dve.tensor_tensor(by(r[:, k, :]), by(banks[2 + k][:, :]), of(0, k), ALU.add)
                        last.then_inc(f_a, 1)
                        dve.wait_ge(f_a, tb * 2 + 1)
                        dve.tensor_tensor(r[:, :, :], r[:, :, :], xT[:, :, bass.ds(tb * TB, TB)], ALU.add).then_inc(f_r, 1)
                        dve.wait_ge(f_m_ready, tb + 1)
                        for k in range(KT):
                            last = dve.tensor_tensor(r[:, k, :], r[:, k, :], banks[4][:, :], ALU.subtract)
                        last.then_inc(f_cn, 1)
                        dve.wait_ge(f_v_ready, tb + 1)
                        dve.tensor_scalar(rstd[:, :], banks[5][:, :], EPS, None, ALU.add).then_inc(f_rs, 1)
                        dve.wait_ge(f_sd, tb + 1)
                        dve.reciprocal(rstd[:, :], rstd[:, :]).then_inc(f_rs, 1)
                        dve.wait_ge(f_rs, tb * 2 + 2)
                        for k in range(KT):
                            last = dve.tensor_tensor(r[:, k, :], r[:, k, :], rstd[:, :], ALU.mult)
                        last.then_inc(f_a, 1)
                        dve.wait_ge(f_a, tb * 2 + 2)
                        for k in range(KT):
                            last = dve.tensor_tensor(by(r[:, k, :]), by(r[:, k, :]), of(1, k), ALU.mult)
                        last.then_inc(f_t, 1)
                        dve.wait_ge(f_t, tb + 2)
                        for k in range(KT):
                            last = dve.tensor_tensor(by(r[:, k, :]), by(r[:, k, :]), of(2, k), ALU.add)
                        last.then_inc(f_n, 1)
                        dve.wait_ge(f_o_ready, tb + 1)
                        for k in range(KT):
                            at = xT[:, k, bass.ds(tb * TB, TB)]
                            last = dve.scalar_tensor_tensor(at, banks[6 + k][:, :], fb[:, k:k + 1], at, ALU.add, ALU.add)
                        last.then_inc(f_o, 1)


def constants():
    f = np.float32
    pos = np.arange(S, dtype=f)
    half = HD0 // 2
    scale = f(10000.0) ** (f(2.0) * np.arange(half, dtype=f) / f(HD0))
    ang = (pos[:, None] / scale).astype(f)
    cos, sin = np.cos(ang), np.sin(ang)
    cs, sn = np.concatenate([cos, cos], 1), np.concatenate([-sin, sin], 1)
    rope = np.stack([cs / 8, sn / 8, cs, sn], 1).astype(f)
    theta = f(1.0) / f(10000.0) ** (f(2.0) * np.arange(HD1 // 2, dtype=f) / f(HD1))
    ang1 = np.arange(1, S + 1, dtype=f)[:, None] * theta
    ang1 = np.concatenate([ang1, ang1], 1)
    fac = (np.cos(ang1) + np.sin(ang1)).astype(f).T
    fac = np.tile(fac, (P // HD1, 1))
    p = np.arange(P)
    cols = np.zeros((P, 16), f)
    cols[:, 0] = p
    cols[:, 1] = p // RL
    for k in range(LT):
        cols[:, 2 + k] = (k * P + p) // A2
    q = np.arange(P)[:, None] % S
    low = np.arange(S)[None] <= q
    ar = lambda n: np.arange(n, dtype=f)
    return {
        "ident": np.eye(P, dtype=f),
        "mask0": np.where(low, 0.0, -1e10).astype(f),
        "mask1": np.where(low, 0.0, -3e38).astype(f),
        "cols": cols,
        "rope": np.tile(rope, (2, 1, 1)),
        "rt_es": np.broadcast_to(ar(E2)[:, None], (E2, B))[None],
        "rt_j8": np.broadcast_to(SLOTS * ar(B // SLOTS)[None], (E2, B // SLOTS))[None],
        "rt_ee": np.tril(np.ones((E2, E2), f), -1)[None],
        "rt_ll": np.tril(np.ones((B, B), f), -1)[None],
        "rt_q": ar(BLOCKS * SLOTS)[None],
        "rt_em": (B + ar(BLOCKS * SLOTS) % SLOTS)[None],
        "rt_sm": (ar(B)[None] - (B + ar(BLOCKS * SLOTS) % SLOTS)[:, None])[None],
        "rt_kk": ar(BLOCKS)[None],
        "n_fac": np.stack([fac / 4, fac], 1),
        "n_hm": (p[:, None] // HD1 == np.arange(P // HD1)[None]).astype(f),
        "f_ones": np.full((P, P), 1.0 / D, f),
    }


def layouts(i):
    T = lambda a: np.swapaxes(a, -1, -2)
    cols = lambda a: a.reshape(-1, P).T
    return {
        "xT": i["x"].reshape(N, D).T,
        "idx": np.stack([i["itok_B_0_7"], i["itok_B_0_2"], i["itok_B_0_8"]]),
        "c0_wT": T(i["L0_cond_weight"]), "c0_bias": i["L0_cond_bias"],
        "a0_wqkv": i["L0_attn_wqkv"], "a0_wo": i["L0_attn_wo"],
        **{f"c2_{n}": i[f"L0_cond2_{n}"] for n in ("Wi0", "Wi1", "Wo", "sWi0", "sWi1", "sWo", "g0", "g1")},
        "m_rwT": i["L0_ffn_router_weight"].T, "m_rb": i["L0_ffn_router_bias"],
        "m_guT": T(i["L0_ffn_gate_up_proj"]), "m_dnT": T(i["L0_ffn_down_proj"]),
        "m_gub": i["L0_ffn_gate_up_proj_bias"].reshape(EM, 2 * JT, P).transpose(2, 0, 1),
        "m_db": i["L0_ffn_down_proj_bias"],
        "l_wiT": i["L1_cond_wi"].T, "l_woT": i["L1_cond_wo"].T,
        "l_cia": i["L1_cond_common_wi_a"], "l_cibT": i["L1_cond_common_wi_b"].T,
        "l_coa": i["L1_cond_common_wo_a"], "l_cobT": i["L1_cond_common_wo_b"].T,
        "l_eiaT": i["L1_cond_experts_wi_a"].reshape(EL * RL, D).T,
        "l_eibT": T(i["L1_cond_experts_wi_b"]).reshape(EL * RL, FF),
        "l_eoaT": i["L1_cond_experts_wo_a"].reshape(EL * RL, FF).T,
        "l_eobT": T(i["L1_cond_experts_wo_b"]).reshape(EL * RL, D),
        "n_waT": i["L1_attn_W_attn"].T, "n_wpT": i["L1_attn_W_proj"].T,
        "n_bat": cols(i["L1_attn_b_attn"][:2 * D]), "n_bv": i["L1_attn_b_attn"][2 * D:], "n_bp": cols(i["L1_attn_b_proj"]),
        "f_w1": i["L1_cond2_W1"].transpose(1, 0, 2).reshape(D, LANG * A2), "f_b1": cols(i["L1_cond2_b1"].reshape(-1)),
        "f_w2": i["L1_cond2_W2"].reshape(LANG * A2, D),
        "f_tab": np.stack([i["L1_cond2_b2"], i["L1_cond2_gamma"], i["L1_cond2_beta"]], 1),
        "f_wT": i["L1_ffn_W"].T, "f_vrT": i["L1_ffn_V_r"].T, "f_cT": i["L1_ffn_C"].T, "f_b": cols(i["L1_ffn_b"]),
    }


def kernel(**inputs):
    import concourse.bacc as bacc
    from concourse.bass_utils import run_bass_kernel_spmd

    arrays = {n: np.ascontiguousarray(a) for n, a in {**layouts({k: np.asarray(v) for k, v in inputs.items()}),
                                                      **constants()}.items()}
    nc = bacc.Bacc("TRN2", target_bir_lowering=False, num_devices=1)
    io = {n: nc.dram_tensor(f"in_{n}", a.shape, mybir.dt.from_np(a.dtype), kind="ExternalInput").ap()
          for n, a in arrays.items()}
    out = nc.dram_tensor("outT", (D, N), F32, kind="ExternalOutput").ap()
    build_program(nc, io, out)
    r = run_bass_kernel_spmd(nc, [{f"in_{n}": a for n, a in arrays.items()}], core_ids=[0])
    return np.ascontiguousarray(r.results[0]["outT"].T).reshape(B, S, D)
```

```python
from contextlib import ExitStack

import numpy as np

import concourse.bass as bass
from concourse import mybir

F32 = mybir.dt.float32
F32R = mybir.dt.float32r
I32 = mybir.dt.int32
ALU = mybir.AluOpType
ACT = mybir.ActivationFunctionType
AX = mybir.AxisListType

P = 128
B, S, D = 32, 64, 256
N = B * S
KT = D // P
PAIRS = N // P
TB = 512
NTB = N // TB
HEADS = 16
HD0 = 64
HD1 = D // HEADS
QF = HEADS * HD0
FF = 1024
FT = FF // P
E0 = 8
E2 = 5
SLOTS = 4
BLOCKS = (B + E2 * (SLOTS - 1)) // SLOTS
EM, IM = 8, 512
TOP_K = 4
JT = IM // P
LIMIT, SWIGLU_ALPHA = 7.0, 1.702
EL, RL = 8, 16
LANG, A2 = 10, 64
LT = LANG * A2 // P
EPS = 1e-5


def bcast(ap, axis, n):
    ap = ap.unsqueeze(axis)
    shape = list(ap.shape)
    shape[axis] = n
    return ap.to_broadcast(shape)


def wait(eng, sem, value):
    if isinstance(value, int) and value <= 0:
        return
    eng.wait_ge(sem, value)


def live(p):
    return not isinstance(p, int) or 0 <= p < PAIRS


LEAD, TAIL = 3, 3


def pipeline(eng, step):
    for i in range(-2, LEAD):
        step(i, i % 2)
    trips = (PAIRS - 2 - LEAD) // 2
    with eng.Fori(0, trips) as t:
        for u in range(2):
            step(t * 2 + (LEAD + u), (LEAD + u) % 2)
    for i in range(LEAD + 2 * trips, PAIRS + TAIL):
        step(i, i % 2)


def build_program(nc, io, out):
    ctx = ExitStack()
    with ctx:
        def sb(name, shape, dt=F32, c=ctx, side=None):
            return c.enter_context(nc.sbuf_tensor(name, shape, dt, side=side))

        def sem(name, kept=False):
            s = nc.alloc_semaphore(name=name)
            if not kept:
                used.append(s)
            return s

        def clear():
            nc.clear_and_free_semaphores(used)
            used.clear()
            nc.all_engine_barrier()

        used = []

        banks = [ctx.enter_context(nc.psum_tensor(f"bank{k}", [P, 512], F32)) for k in range(8)]
        xT = sb("xT", [P, KT, N + SLOTS * S])
        ident = sb("ident", [P, P])
        mask = sb("mask", [P, S])
        cols = sb("cols", [P, 16])
        samp = sb("samp", [P, 3, B])
        samp_i = sb("samp_i", [P, 3, B], I32)
        oh_sub = sb("oh_sub", [E0, B])
        oh_lora = sb("oh_lora", [P, B])
        oh_lang = sb("oh_lang", [P, LT, B])
        oh_lang10 = sb("oh_lang10", [LANG, B])
        slot_sample = sb("slot_sample", [1, BLOCKS * SLOTS], I32)
        block_expert = sb("block_expert", [1, BLOCKS], I32)

        c0 = ctx.enter_context(ExitStack())
        with ExitStack() as c:
            with ExitStack() as c2:
                b_ws = [sb(n, s, F32, c2, "right") for n, s in (
                    ("w0s", [P, KT, FF]), ("w1s", [P, KT, FF]), ("w2s", [P, FT, D]))]
                b_w = [sem(f"b_w{n}_in", kept=True) for n in range(3)]
                attention0(nc, io, banks, sb, sem, xT, ident, mask, cols, samp, samp_i, oh_sub, oh_lora,
                           oh_lang, oh_lang10, slot_sample, block_expert, b_ws, b_w)
                clear()
                eo = sb("eo", [P, KT, N + SLOTS * S], F32, c2, "right")
                sT = sb("sT", [P, KT, N], F32, c2, "right")
                g_w = [sb(n, s, F32, c2, "right") for n, s in (
                    ("g0", [P, 2 * KT, D]), ("g1", [P, KT, 2]), ("rw", [P, KT, EM]))]
                g_in = sem("g_in")
                gated_ffn(nc, io, banks, sb, sem, xT, eo, sT, slot_sample, block_expert, b_ws, b_w, g_w, g_in)
                h_hi = sb("h_hi", [P, KT, N], F32R, c)
                h_lo = sb("h_lo", [P, KT, N], F32R, c)
                lgT = sb("lgT", [EM, N], F32, c)
                m_ws = [sb("wgs", [P, KT, 2 * IM], F32, c), sb("wds", [P, JT, D], F32, c)]
                m_wh, m_wl = ([[sb(f"mw{n}{part}{k}", list(t.shape), F32R, c) for n, t in enumerate(m_ws)]
                               for k in range(2)] for part in ("h", "l"))
                weights = m_ws, m_wh, m_wl, [sem(f"m_w{k}_in") for k in range(2)], sem("m_weights_hi"), sem("m_weights_lo")
                mix(nc, io, banks, sb, sem, eo, sT, h_hi, h_lo, lgT, weights, g_w, g_in)
            zT = sb("zT", [P, KT, N], F32, c0, "right")
            acc = zT[:, :, :].rearrange("p k n -> p (k n)").rearrange("p (t d) -> p t d", d=D)
            mixture(nc, io, banks, sb, sem, h_hi, h_lo, lgT, ident, weights, acc)
        c1 = ctx.enter_context(ExitStack())
        n_w, n_in = attention1_tensors(sb, sem, c1)
        lora_ffn(nc, io, banks, sb, sem, xT, zT, acc, ident, oh_lora, n_w, n_in)
        f_w, f_in = adapter_tensors(sb, sem, ctx)
        attention1(nc, io, banks, sb, sem, xT, zT, ident, mask, n_w, n_in, f_w, f_in)
        c0.close()
        adapter_ffn(nc, io, banks, sb, sem, xT, oh_lang, oh_lang10, out, f_w, f_in)


def load_expert(sp, io, e, w, sems):
    for dst, name, done in zip(w, ("c2_Wi0", "c2_Wi1", "c2_Wo"), sems):
        sp.dma_start(dst[:, :, :], io[name][bass.ds(e, 1), :, :].rearrange("e (k p) n -> p (e k) n", p=P)).then_inc(done, 16)


def attention0(nc, io, banks, sb0, sem, xT, ident, mask, cols, samp, samp_i, oh_sub, oh_lora, oh_lang,
               oh_lang10, slot_sample, block_expert, b_ws, b_w):
    with ExitStack() as c:
        def sb(name, shape, dt=F32):
            return sb0(name, shape, dt, c)

        w3 = [b_ws[0][:, :, :], b_ws[1][:, :, :],
              b_ws[2][:, :, :].rearrange("p f d -> p (f d)").rearrange("p (k n) -> p k n", k=KT)]
        w3_2 = [[sb(f"wqkv{n}_{part}", [P, KT, QF], F32R) for part in ("hi", "lo")] for n in range(3)]
        wo = sb("wo", [P, QF // P, D])
        rope = sb("rope", [P, 4, HD0])
        btab = sb("btab", [E0, D])
        biasT = sb("biasT", [P, KT, B])
        wsub = [sb(f"wsub{k}", [P, 2, KT, D]) for k in range(2)]
        xs = [sb(f"xs{k}", [P, KT, P]) for k in range(2)]
        ysb = sb("ysb", [P, D])
        yf = sb("yf", [P, KT, P])
        yT = [[sb(f"yT{k}_{part}", [P, KT, P], F32R) for part in ("hi", "lo")] for k in range(2)]
        rc = [sb(f"rc{k}", [P, 512]) for k in range(2)]
        rs = [sb(f"rs{k}", [P, 512]) for k in range(2)]
        qk = [sb(f"qk{k}", [P, 2 * QF]) for k in range(2)]
        v = [sb(f"v{k}", [P, QF]) for k in range(2)]
        qT = sb("qT", [P, HEADS // 2, P])
        kpad = sb("kpad", [P, HEADS // 2, 2, P])
        sc = sb("sc", [P, HEADS, S])
        ex = sb("ex", [P, HEADS, S])
        mx = sb("mx", [P, HEADS])
        sm = sb("sm", [P, HEADS])
        ri = sb("ri", [P, HEADS])
        pr = sb("pr", [P, HEADS, P])
        prT = sb("prT", [P, HEADS, P])
        ctxT = sb("ctxT", [P, QF // P, P])
        same = ctxT[0:1, :, :].rearrange("p k n -> p (k n)").rearrange("p (a b) -> p a b", b=B)
        hit = prT[0:1, :, :].rearrange("p h n -> p (h n)")[:, 0:BLOCKS * SLOTS * B].rearrange("p (q b) -> p q b", b=B)
        rt = {n: sb("rt_" + n, [1, *s]) for n, s in dict(
            es=(E2, B), j8=(E2, B // SLOTS), ee=(E2, E2), ll=(B, B), q=(BLOCKS * SLOTS,),
            sm=(BLOCKS * SLOTS, B), em=(BLOCKS * SLOTS,),
            kk=(BLOCKS,)).items()}
        oh = sb("r_oh", [1, E2, B])
        cnt = sb("r_cnt", [1, E2])
        cmp8 = sb("r_cmp8", [1, E2, B // SLOTS])
        nblk = sb("r_nblk", [1, E2])
        lowb = sb("r_lowb", [1, E2, E2])
        base = sb("r_base", [1, E2])
        base4 = sb("r_base4", [1, E2])

        rank = sb("r_rank", [1, B])
        ohb = sb("r_ohb", [1, B, E2])
        pos = sb("r_pos", [1, B])

        sid = sb("r_sid", [1, BLOCKS * SLOTS])
        ble = sb("r_ble", [1, BLOCKS, E2])
        bex = sb("r_bex", [1, BLOCKS])

        a_small, a_x, a_wo, a_route = (sem(n) for n in ("a_small_in", "a_x_in", "a_wo_in", "a_route_in"))
        a_w3 = [sem(f"a_w{n}_in") for n in "qkv"]
        a_whi, a_wlo, a_wvlo, a_yf, a_yhi = (sem(n) for n in (
            "a_weights_hi", "a_weights_qk_lo", "a_weights_v_lo", "a_y_biased", "a_y_hi"))
        a_w = [sem(f"a_wsub{k}_in") for k in range(2)]
        a_zero, a_tab, a_bias_ready, a_bias, a_routed, a_slots = (sem(n) for n in (
            "a_zeroed", "a_tables", "a_bias_ready", "a_bias_copied", "a_routed", "a_slots_found"))
        a_xs, a_cond, a_y, a_yt_ready, a_yt = (sem(n) for n in (
            "a_xs_staged", "a_cond_ready", "a_y_copied", "a_yt_ready", "a_yt_copied"))
        a_qk_ready, a_rope, a_add, a_v_ready, a_v = (sem(n) for n in (
            "a_qk_ready", "a_rope_done", "a_rope_added", "a_v_ready", "a_v_copied"))
        a_tq_ready, a_tq, a_s_ready, a_s, a_mx, a_sub, a_exp, a_sum, a_rec, a_p = (sem(n) for n in (
            "a_trqk_ready", "a_trqk_copied", "a_s_ready", "a_s_masked", "a_max", "a_subtracted",
            "a_exp", "a_sum", "a_recip", "a_probs"))
        a_p0, a_tp_ready, a_tp, a_c_ready, a_c, a_o_ready, a_o = (sem(n) for n in (
            "a_probs_half", "a_trp_ready", "a_trp_copied", "a_ctx_ready", "a_ctx_copied", "a_out_ready", "a_out_added"))

        with nc.Block() as block:
            @block.sync
            def _(sp):
                sp.dma_start(samp_i[:, :, :], io["idx"].partition_broadcast(P)).then_inc(a_small, 16)
                for dst, name in ((ident, "ident"), (cols, "cols"), (btab, "c0_bias"), (mask, "mask0")):
                    sp.dma_start(dst[:, :], io[name]).then_inc(a_small, 16)
                sp.dma_start(rope[:, :, :], io["rope"]).then_inc(a_small, 16)
                sp.dma_start(xT[:, :, 0:N], io["xT"].rearrange("(k p) n -> p k n", p=P)).then_inc(a_x, 16)
                sp.wait_ge(a_small, 96)

                def step(i, par):
                    p = i + 2
                    if not live(p):
                        return
                    wait(sp, a_cond, p - 1)
                    for s in range(2):
                        e = sp.value_load(samp_i[0:1, 0, bass.ds(p * 2 + s, 1)], min_val=0, max_val=E0 - 1)
                        sp.dma_start(wsub[par][:, s, :, :], io["c0_wT"][bass.ds(e, 1), :, :].rearrange(
                            "e (k p) o -> p (e k) o", p=P)).then_inc(a_w[par], 16)
                    if isinstance(p, int) and p == 0:
                        for n in range(3):
                            sp.dma_start(w3[n], io["a0_wqkv"][:, n * QF:(n + 1) * QF].rearrange(
                                "(k p) n -> p k n", p=P)).then_inc(a_w3[n], 16)
                        sp.dma_start(wo[:, :, :], io["a0_wo"].rearrange("(k p) n -> p k n", p=P)).then_inc(a_wo, 16)
                        for n in rt:
                            sp.dma_start(rt[n][:], io["rt_" + n]).then_inc(a_route, 16)

                pipeline(sp, step)
                sp.wait_ge(a_slots, 1)
                sp.wait_ge(a_wlo, 2)
                sp.wait_ge(a_wvlo, 1)
                e = sp.value_load(block_expert[0:1, 0:1], min_val=0, max_val=E2 - 1)
                load_expert(sp, io, e, b_ws, b_w)

            @block.gpsimd
            def _(pool):
                pool.memset(kpad[:, :, :, :], 0.0).then_inc(a_zero, 1)
                pool.memset(pr[:, :, :], 0.0).then_inc(a_zero, 1)
                pool.memset(xT[:, :, N:], 0.0).then_inc(a_zero, 1)
                pool.wait_ge(a_x, 16)

                def step(i, par):
                    if isinstance(i, int) and i == 0:
                        pool.wait_ge(a_whi, 3)
                        pool.tensor_tensor(w3_2[2][1][:, :, :], w3[2], w3_2[2][0][:, :, :].bitcast(F32),
                                           ALU.subtract).then_inc(a_wvlo, 1)
                    p = i + 2
                    if live(p):
                        wait(pool, a_cond, p - 1)
                        pool.tensor_copy(xs[par][:, :, :], xT[:, :, bass.ds(p * P, P)]).then_inc(a_xs, 1)
                    for half in range(2):
                        if live(i):
                            if half == 0:
                                wait(pool, a_tq_ready, 4 * (i - 2) + 4)
                            for c2 in range(2):
                                n = 4 * i + 2 * half + c2
                                wait(pool, a_rope, n + 1)
                                ch = 2 * half + c2
                                pool.tensor_tensor(qk[par][:, ch * 512:(ch + 1) * 512], rc[c2][:, :],
                                                   rs[c2][:, :], ALU.add).then_inc(a_add, 1)
                        if half == 0 and live(i - 2):
                            wait(pool, a_rec, i - 1)
                            if isinstance(i, int) and i == 2:
                                pool.wait_ge(a_zero, 3)
                            wait(pool, a_tp_ready, 4 * (i - 3) + 4)
                            if live(i):
                                pool.wait_ge(a_add, 4 * i + 2)
                            if live(i + 2):
                                pool.wait_ge(a_xs, i + 3)
                            pool.tensor_tensor(pr[0:S, :, 0:S], ex[0:S, :, :], bcast(ri[0:S, :], 2, S), ALU.mult).then_inc(a_p0, 1)
                            pool.wait_ge(a_p0, i - 1)
                            pool.tensor_tensor(pr[S:P, :, S:P], ex[S:P, :, :], bcast(ri[S:P, :], 2, S), ALU.mult).then_inc(a_p, 1)
                            pool.wait_ge(a_p, i - 1)

                pipeline(pool, step)

            @block.tensor
            def _(pe):
                pe.wait_ge(a_tab, 2)
                for k in range(KT):
                    mm = pe.matmul(banks[7][:, k * B:(k + 1) * B], btab[:, k * P:(k + 1) * P], oh_sub[:, :],
                                   start=True, stop=True)
                mm.then_inc(a_bias_ready, 1)

                def qk_transposed(p, par, f):
                    for j in range(4):
                        at = (4 * f + j) * P
                        mm = pe.transpose(banks[6 + f % 2][:, j * P:(j + 1) * P], qk[par][:, at:at + P], ident[:, :])
                    mm.then_inc(a_tq_ready, 1)

                def v_half(p, par, ch):
                    wait(pe, a_v, 2 * p + ch)
                    for k in range(KT):
                        mm = mm3(pe, banks[3][:, :], [y[:, k, :] for y in yT[par]],
                                 [w[:, k, ch * 512:(ch + 1) * 512] for w in w3_2[2]], k == 0, k == KT - 1)
                    mm.then_inc(a_v_ready, 1)

                def qk_chunks(i, par, chunks):
                    for ch in chunks:
                        wait(pe, a_rope, 4 * i + ch - 1)
                        for k in range(KT):
                            at = (ch % 2) * 512
                            mm = mm3(pe, banks[1 + ch % 2][:, :], [y[:, k, :] for y in yT[par]],
                                     [w[:, k, at:at + 512] for w in w3_2[ch // 2]], k == 0, k == KT - 1)
                        mm.then_inc(a_qk_ready, 1)

                def step(i, par):
                    if live(i):
                        if isinstance(i, int) and i == 0:
                            pe.wait_ge(a_wlo, 1)
                        pe.wait_ge(a_yt, i + 1)
                        qk_chunks(i, par, (0, 1))
                    if live(i - 3):
                        p = i - 3
                        if isinstance(p, int) and p == 0:
                            pe.wait_ge(a_wo, 16)
                        pe.wait_ge(a_c, 2 * p + 2)
                        wait(pe, a_o, p)
                        for o in range(KT):
                            for k in range(QF // P):
                                mm = pe.matmul(banks[0][:, o * P:(o + 1) * P], wo[:, k, o * P:(o + 1) * P],
                                               ctxT[:, k, :], start=k == 0, stop=k == QF // P - 1)
                        mm.then_inc(a_o_ready, 1)
                    if live(i - 1):
                        pe.wait_ge(a_add, 4 * (i - 1) + 4)
                        for f in range(2):
                            wait(pe, a_c, 2 * (i - 3) + f + 1)
                            qk_transposed(i - 1, 1 - par, f)
                    if live(i - 1):
                        if isinstance(i, int) and i == 1:
                            pe.wait_ge(a_wvlo, 1)
                        v_half(i - 1, 1 - par, 0)
                    if live(i + 1):
                        p = i + 1
                        wait(pe, a_o, i - 2)
                        pe.wait_ge(a_xs, p + 1)
                        if isinstance(p, int):
                            pe.wait_ge(a_w[1 - par], 32 * (p // 2 + 1))
                        else:
                            pe.wait_ge(a_w[1 - par], 16 * p + (32 if par == 1 else 16))
                        for s in range(2):
                            for k in range(KT):
                                mm = pe.matmul(banks[0][S * s:S * s + S, 0:D], xs[1 - par][:, k, S * s:S * s + S],
                                               wsub[1 - par][:, s, k, :], start=k == 0, stop=k == KT - 1)
                        mm.then_inc(a_cond, 1)
                    if live(i - 1):
                        v_half(i - 1, 1 - par, 1)
                        for f in range(2, 4):
                            wait(pe, a_tq, 4 * (i - 1) + f - 1)
                            qk_transposed(i - 1, 1 - par, f)
                    if live(i):
                        if isinstance(i, int) and i == 0:
                            pe.wait_ge(a_wlo, 2)
                        qk_chunks(i, par, (2, 3))
                    if live(i + 1):
                        pe.wait_ge(a_y, i + 2)
                        for k in range(KT):
                            mm = pe.transpose(banks[0][:, k * P:(k + 1) * P], ysb[:, k * P:(k + 1) * P], ident[:, :])
                        mm.then_inc(a_yt_ready, 1)
                    if live(i - 2):
                        p = i - 2
                        pe.wait_ge(a_p, p + 1)
                        for f in range(4):
                            if f >= 2:
                                wait(pe, a_tp, 4 * p + f - 1)
                            elif live(i - 1):
                                wait(pe, a_tq, 4 * (i - 1) + f + 3)
                            for j in range(4):
                                mm = pe.transpose(banks[6 + f % 2][:, j * P:(j + 1) * P], pr[:, 4 * f + j, :], ident[:, :])
                            mm.then_inc(a_tp_ready, 1)
                    if live(i - 1):
                        p = i - 1
                        pe.wait_ge(a_tq, 4 * p + 4)
                        for f in range(4):
                            wait(pe, a_s, 4 * p + f - 1)
                            for j in range(2):
                                t = 2 * f + j
                                mm = pe.matmul(banks[4 + f % 2][:, j * 256:(j + 1) * 256], qT[:, t, :],
                                               kpad[:, t, :, :], start=True, stop=True)
                            mm.then_inc(a_s_ready, 1)
                    if live(i - 2):
                        p = i - 2
                        for g in range(2):
                            pe.wait_ge(a_tp, 4 * p + 3 + g)
                            for j in range(4):
                                for s in range(2):
                                    h = 8 * g + 2 * j + s
                                    mm = pe.matmul(banks[6 + g][HD0 * s:HD0 * s + HD0, j * P:(j + 1) * P],
                                                   v[par][:, h * HD0:(h + 1) * HD0], prT[:, h, :],
                                                   start=True, stop=True)
                            mm.then_inc(a_c_ready, 1)

                pipeline(pe, step)

            @block.scalar
            def _(act):
                def v_copy(p, par, ch):
                    act.wait_ge(a_v_ready, 2 * p + ch + 1)
                    act.activation(v[par][:, ch * 512:(ch + 1) * 512], banks[3][:, :], ACT.Copy).then_inc(a_v, 1)

                def step(i, par):
                    if isinstance(i, int) and i == 0:
                        for n in range(3):
                            act.wait_ge(a_w3[n], 16)
                            act.activation(w3_2[n][0][:, :, :], w3[n], ACT.Copy).then_inc(a_whi, 1)
                    if live(i - 1):
                        for f in range(2):
                            act.wait_ge(a_tq_ready, 4 * (i - 1) + f + 1)
                            act.activation(qT[:, 4 * f:4 * f + 4, :], banks[6 + f][:, :].rearrange("p (t n) -> p t n", n=P),
                                           ACT.Copy).then_inc(a_tq, 1)
                        v_copy(i - 1, 1 - par, 0)
                    if live(i + 1):
                        act.wait_ge(a_cond, i + 2)
                        act.activation(ysb[:, :], banks[0][:, 0:D], ACT.Copy).then_inc(a_y, 1)
                    if live(i - 1):
                        v_copy(i - 1, 1 - par, 1)
                    if live(i - 1):
                        p = i - 1
                        if isinstance(p, int) and p == 0:
                            act.wait_ge(a_zero, 1)
                        for f in range(2, 4):
                            act.wait_ge(a_tq_ready, 4 * p + f + 1)
                            bank = banks[6 + f % 2][:, :].rearrange("p (t n) -> p t n", n=P)
                            for s in range(2):
                                rows = slice(HD0 * s, HD0 * s + HD0)
                                last = act.activation(kpad[rows, 4 * f - 8:4 * f - 4, s, :], bank[rows], ACT.Copy)
                            last.then_inc(a_tq, 1)
                    for f in range(4):
                        if f == 2 and live(i + 1):
                            act.wait_ge(a_yf, i + 2)
                            act.activation(yT[1 - par][0][:, :, :], yf[:, :, :], ACT.Copy).then_inc(a_yhi, 1)
                        if live(i - 2):
                            act.wait_ge(a_tp_ready, 4 * (i - 2) + f + 1)
                            act.activation(prT[:, 4 * f:4 * f + 4, :], banks[6 + f % 2][:, :].rearrange(
                                "p (t n) -> p t n", n=P), ACT.Copy).then_inc(a_tp, 1)
                    if live(i - 2):
                        p = i - 2
                        for g in range(2):
                            act.wait_ge(a_c_ready, 2 * p + g + 1)
                            act.activation(ctxT[:, 4 * g:4 * g + 4, :], banks[6 + g][:, :].rearrange(
                                "p (t n) -> p t n", n=P), ACT.Copy).then_inc(a_c, 1)
                    if live(i - 1):
                        act.wait_ge(a_sub, i)
                        wait(act, a_p, i - 1)
                        act.activation(ex[:, :, :], sc[:, :, :], ACT.Exp).then_inc(a_exp, 1)

                pipeline(act, step)

            @block.vector
            def _(dve):
                dve.wait_ge(a_small, 96)
                dve.tensor_copy(samp[:, :, :], samp_i[:, :, :]).then_inc(a_tab, 1)
                dve.wait_ge(a_tab, 1)
                dve.tensor_scalar(oh_lora[:, :], samp[:, 0, :], cols[:, 1:2], 2.0, ALU.is_equal, ALU.mult)
                for k in range(LT):
                    dve.tensor_scalar(oh_lang[:, k, :], samp[:, 2, :], cols[:, 2 + k:3 + k], None, ALU.is_equal)
                dve.tensor_scalar(oh_lang10[:, :], samp[0:LANG, 2, :], cols[0:LANG, 0:1], None, ALU.is_equal)
                dve.tensor_scalar(oh_sub[:, :], samp[0:E0, 0, :], cols[0:E0, 0:1], None, ALU.is_equal).then_inc(a_tab, 1)
                dve.wait_ge(a_bias_ready, 1)
                dve.tensor_copy(biasT[:, :, :], banks[7][:, 0:KT * B].rearrange("p (k b) -> p k b", k=KT)).then_inc(a_bias, 1)
                dve.wait_ge(a_bias, 1)

                def route():
                    dve.wait_ge(a_route, 16 * len(rt))
                    ty = samp[0:1, 1, :]
                    n = [0]

                    def then(ins):
                        ins.then_inc(a_routed, 1)
                        n[0] += 1
                        dve.wait_ge(a_routed, n[0])

                    then(dve.tensor_tensor(oh[:, :, :], bcast(ty, 1, E2), rt["es"][:, :, :], ALU.is_equal))
                    then(dve.tensor_reduce(cnt[:, :], oh[:, :, :], AX.X, ALU.add))
                    then(dve.tensor_tensor(cmp8[:, :, :], bcast(cnt[:, :], 2, B // SLOTS), rt["j8"][:, :, :], ALU.is_gt))
                    then(dve.tensor_reduce(nblk[:, :], cmp8[:, :, :], AX.X, ALU.add))
                    then(dve.tensor_tensor(lowb[:, :, :], bcast(nblk[:, :], 1, E2), rt["ee"][:, :, :], ALU.mult))
                    then(dve.tensor_reduce(base[:, :], lowb[:, :, :], AX.X, ALU.add))
                    then(dve.tensor_scalar(base4[:, :], base[:, :], float(SLOTS), None, ALU.mult))
                    then(dve.tensor_tensor(same[:, :, :], bcast(ty, 2, B), bcast(ty, 1, B), ALU.is_equal))
                    then(dve.tensor_tensor(same[:, :, :], same[:, :, :], rt["ll"][:, :, :], ALU.mult))
                    then(dve.tensor_reduce(rank[:, :], same[:, :, :], AX.X, ALU.add))
                    then(dve.tensor_tensor(ohb[:, :, :], oh[:, :, :].rearrange("p e b -> p b e"),
                                           bcast(base4[:, :], 1, B), ALU.mult))
                    then(dve.tensor_reduce(pos[:, :], ohb[:, :, :], AX.X, ALU.add))
                    then(dve.tensor_tensor(pos[:, :], pos[:, :], rank[:, :], ALU.add))
                    then(dve.tensor_tensor(hit[:, :, :], bcast(pos[:, :], 1, BLOCKS * SLOTS),
                                           bcast(rt["q"][:, :], 2, B), ALU.is_equal))
                    then(dve.tensor_tensor(hit[:, :, :], hit[:, :, :], rt["sm"][:, :, :], ALU.mult))
                    then(dve.tensor_reduce(sid[:, :], hit[:, :, :], AX.X, ALU.add))
                    then(dve.tensor_tensor(sid[:, :], sid[:, :], rt["em"][:, :], ALU.add))
                    then(dve.tensor_copy(slot_sample[:, :], sid[:, :]))
                    then(dve.tensor_tensor(ble[:, :, 1:E2], bcast(base[:, 1:E2], 1, BLOCKS),
                                           bcast(rt["kk"][:, :], 2, E2 - 1), ALU.is_le))
                    then(dve.tensor_reduce(bex[:, :], ble[:, :, 1:E2], AX.X, ALU.add))
                    dve.tensor_copy(block_expert[:, :], bex[:, :]).then_inc(a_slots, 1)

                def rotate(i, chunks):
                    for ch in chunks:
                        n = 4 * i + ch
                        dve.wait_ge(a_qk_ready, n + 1)
                        wait(dve, a_add, n - 1)
                        src = banks[1 + ch % 2][:, :].rearrange("p (h t d) -> p h t d", t=2, d=HD0 // 2)
                        w = 2 * (ch // 2)
                        cos = bcast(rope[:, w, :].rearrange("p (t d) -> p t d", t=2), 1, 512 // HD0)
                        sin = bcast(rope[:, w + 1, :].rearrange("p (t d) -> p t d", t=2), 1, 512 // HD0)
                        dst = [r[ch % 2][:, :].rearrange("p (h t d) -> p h t d", t=2, d=HD0 // 2) for r in (rc, rs)]
                        dve.tensor_tensor(dst[0], src, cos, ALU.mult)
                        dve.tensor_tensor(dst[1], src[:, :, ::-1, :], sin, ALU.mult).then_inc(a_rope, 1)

                def step(i, par):
                    if isinstance(i, int) and i == 0:
                        for n in range(2):
                            dve.wait_ge(a_whi, n + 1)
                            dve.tensor_tensor(w3_2[n][1][:, :, :], w3[n], w3_2[n][0][:, :, :].bitcast(F32),
                                              ALU.subtract).then_inc(a_wlo, 1)
                    if live(i):
                        rotate(i, (0, 1))
                    if live(i - 2):
                        p = i - 2
                        dve.wait_ge(a_exp, p + 1)
                        wait(dve, a_p, p)
                        dve.tensor_reduce(sm[:, :], ex[:, :, :], AX.X, ALU.add).then_inc(a_sum, 1)
                        dve.wait_ge(a_sum, p + 1)
                        dve.reciprocal(ri[:, :], sm[:, :]).then_inc(a_rec, 1)
                    if live(i - 3):
                        p = i - 3
                        dve.wait_ge(a_o_ready, p + 1)
                        at = xT[:, :, bass.ds(p * P, P)]
                        dve.tensor_tensor(at, banks[0][:, 0:D].rearrange("p (k n) -> p k n", k=KT), at,
                                          ALU.add).then_inc(a_o, 1)
                    if live(i):
                        rotate(i, (2, 3))
                    if live(i + 1):
                        p = i + 1
                        dve.wait_ge(a_yt_ready, p + 1)
                        wait(dve, a_yt, p)
                        for k in range(KT):
                            last = dve.tensor_tensor(
                                yf[:, k, :].rearrange("p (s n) -> p s n", s=2),
                                banks[0][:, k * P:(k + 1) * P].rearrange("p (s n) -> p s n", s=2),
                                bcast(biasT[:, k, bass.ds(p * 2, 2)], 2, S), ALU.add)
                        last.then_inc(a_yf, 1)
                        dve.wait_ge(a_yhi, p + 1)
                        dve.tensor_tensor(yT[1 - par][1][:, :, :], yf[:, :, :], yT[1 - par][0][:, :, :].bitcast(F32),
                                          ALU.subtract).then_inc(a_yt, 1)
                    if live(i - 1):
                        p = i - 1
                        wait(dve, a_exp, p)
                        for f in range(4):
                            dve.wait_ge(a_s_ready, 4 * p + f + 1)
                            for s in range(2):
                                rows = slice(S * s, S * s + S)
                                last = dve.tensor_tensor(
                                    sc[rows, 4 * f:4 * f + 4, :],
                                    banks[4 + f % 2][rows, :].rearrange("p (h n) -> p h n", n=P)[:, :, S * s:S * s + S],
                                    bcast(mask[rows, :], 1, 4), ALU.add)
                            last.then_inc(a_s, 1)
                        dve.wait_ge(a_s, 4 * p + 4)
                        dve.tensor_reduce(mx[:, :], sc[:, :, :], AX.X, ALU.max).then_inc(a_mx, 1)
                        dve.wait_ge(a_mx, p + 1)
                        dve.tensor_tensor(sc[:, :, :], sc[:, :, :], bcast(mx[:, :], 2, S), ALU.subtract).then_inc(a_sub, 1)
                    if isinstance(i, int) and i == 0:
                        route()

                pipeline(dve, step)


def whole(t):
    return t if isinstance(t, bass.AP) else t[tuple(slice(None) for _ in t.shape)]


def mm3(pe, out, w, x, start, stop):
    pe.matmul(out, w[0], x[0], start=start, stop=False)
    pe.matmul(out, w[0], x[1], start=False, stop=False)
    return pe.matmul(out, w[1], x[0], start=False, stop=stop)


def gated_ffn(nc, io, banks, sb0, sem, xT, eo, sT, slot_sample, block_expert, ws, b_w, g_w, g_in):
    with ExitStack() as c:
        def sb(name, shape, dt=F32):
            return sb0(name, shape, dt, c)

        SW = SLOTS * S
        SHARED = N // SW
        UNITS = BLOCKS + SHARED
        SH = BLOCKS % 2

        wh = [[sb(f"w{n}h{k}", list(t.shape), F32R) for n, t in enumerate(ws)] for k in range(2)]
        wl = [[sb(f"w{n}l{k}", list(t.shape), F32R) for n, t in enumerate(ws)] for k in range(2)]
        xg = sb("xg", [P, KT, SW])
        xh = [sb(f"xgh{k}", [P, KT, SW], F32R) for k in range(2)]
        xl = [sb(f"xgl{k}", [P, KT, SW], F32R) for k in range(2)]
        ge = [sb(f"ge{k}", [P, SW]) for k in range(2)]
        hf = [sb(f"hf{k}", [P, SW]) for k in range(2)]
        hh = [sb(f"hh{k}", [P, SW], F32R) for k in range(2)]
        hl = [sb(f"hl{k}", [P, SW], F32R) for k in range(2)]
        (b_whi, b_wlo01, b_wlo2, b_xg, b_xh, b_xl, b_up, b_ge, b_hf, b_hh, b_hl, b_down, b_o) = (sem(n) for n in (
            "b_weights_hi", "b_weights01_lo", "b_weights2_lo", "b_x_gathered", "b_x_hi", "b_x_lo", "b_up_ready",
            "b_gelu", "b_hidden", "b_hidden_hi", "b_hidden_lo", "b_down_ready", "b_out_copied"))

        PIECES = 6

        def piece(t, q):
            w = t[q // 2]
            half = w.shape[1] // 2
            return w[:, (q % 2) * half:(q % 2 + 1) * half, :]

        with nc.Block() as block:
            @block.sync
            def _(sp):
                def load(v, srcs):
                    for n in range(3):
                        if n < 2:
                            sp.wait_ge(b_wlo01, 4 * (v - 1) + 2 * n + 2)
                        else:
                            sp.wait_ge(b_wlo2, 2 * (v - 1) + 2)
                        sp.dma_start(ws[n][:, :, :], srcs[n]).then_inc(b_w[n], 16)

                with sp.Fori(1, BLOCKS) as v:
                    e = sp.value_load(block_expert[0:1, bass.ds(v, 1)], min_val=0, max_val=E2 - 1)
                    load(v, [io[n][bass.ds(e, 1), :, :].rearrange("e (k p) n -> p (e k) n", p=P)
                             for n in ("c2_Wi0", "c2_Wi1", "c2_Wo")])
                load(BLOCKS, [io[n].rearrange("(k p) n -> p k n", p=P) for n in ("c2_sWi0", "c2_sWi1", "c2_sWo")])
                for t, name in zip(g_w, ("c2_g0", "c2_g1", "m_rwT")):
                    sp.dma_start(t[:, :, :], io[name].rearrange("(k p) n -> p k n", p=P)).then_inc(g_in, 16)

            @block.gpsimd
            def _(pool):
                def gather(v):
                    for j in range(SLOTS):
                        s = pool.value_load(slot_sample[0:1, bass.ds(v * SLOTS + j, 1)], min_val=0, max_val=B + SLOTS - 1)
                        last = pool.tensor_copy(xg[:, :, j * S:(j + 1) * S], xT[:, :, bass.ds(s * S, S)])
                    last.then_inc(b_xg, 1)

                def slice_(v):
                    pool.tensor_copy(xg[:, :, :], xT[:, :, bass.ds((v - BLOCKS) * SW, SW)]).then_inc(b_xg, 1)

                def lo(v, q, par):
                    pool.wait_ge(b_whi, v * PIECES + (q + 1))
                    pool.tensor_tensor(piece(wl[par], q), piece(ws, q), piece(wh[par], q).bitcast(F32),
                                       ALU.subtract).then_inc(b_wlo01, 1)

                def x_lo(v, par):
                    pool.wait_ge(b_xh, v + 1)
                    pool.tensor_tensor(xl[par][:, :, :], xg[:, :, :], xh[par][:, :, :].bitcast(F32),
                                       ALU.subtract).then_inc(b_xl, 1)

                def prepare(v, par, take=gather, weights=True):
                    wait(pool, b_xl, v)
                    take(v)
                    if weights:
                        for q in range(4):
                            lo(v, q, par)
                    x_lo(v, par)

                gather(0)
                lo(0, 0, 0)
                pool.wait_ge(b_wlo01, 2)
                lo(0, 2, 0)
                with pool.Fori(0, (BLOCKS - 1) // 2) as t:
                    for j in range(2):
                        prepare(t * 2 + (1 + j), 1 - j)
                prepare(BLOCKS, SH, slice_)
                prepare(BLOCKS + 1, 1 - SH, slice_, False)
                with pool.Fori(1, SHARED // 2) as t:
                    for j in range(2):
                        prepare(t * 2 + (BLOCKS + j), (BLOCKS + j) % 2, slice_, False)

            @block.tensor
            def _(pe):
                def up(u, par, wb, f):
                    wait(pe, b_hf, FT * u + f - 1)
                    for bank, n in ((f % 2, 0), (2 + f % 2, 1)):
                        for k in range(KT):
                            mm = mm3(pe, banks[bank][:, 0:SW], [w[wb][n][:, k, f * P:(f + 1) * P] for w in (wh, wl)],
                                     [x[par][:, k, :] for x in (xh, xl)], k == 0, k == KT - 1)
                    mm.then_inc(b_up, 1)

                def down(u, par, wb, f):
                    pe.wait_ge(b_hl, FT * u + f + 1)
                    if f == 0:
                        wait(pe, b_o, u - 1)
                    for o in range(KT):
                        mm = mm3(pe, banks[4 + 2 * par + o][:, 0:SW], [w[wb][2][:, f, o * P:(o + 1) * P] for w in (wh, wl)],
                                 [h[f % 2][:, :] for h in (hh, hl)], f == 0, f == FT - 1)
                    mm.then_inc(b_down, 1)

                def unit(u, par, wb, before, new_weights=True):
                    pe.wait_ge(b_xl, u + 1)
                    if new_weights:
                        pe.wait_ge(b_wlo01, 4 * u + 4)
                    for f in range(FT):
                        up(u, par, wb, f)
                        if f >= 2:
                            if f == 2 and new_weights:
                                pe.wait_ge(b_wlo2, 2 * u + 2)
                            down(u, par, wb, f - 2)
                        elif before is not None:
                            down(u - 1, 1 - par, before, FT - 2 + f)

                unit(0, 0, 0, None)
                with pe.Fori(0, (BLOCKS - 1) // 2) as t:
                    for j in range(2):
                        unit(t * 2 + (1 + j), 1 - j, 1 - j, j)
                unit(BLOCKS, SH, SH, 1 - SH)
                unit(BLOCKS + 1, 1 - SH, SH, SH, False)
                with pe.Fori(1, SHARED // 2) as t:
                    for j in range(2):
                        unit(t * 2 + (BLOCKS + j), (BLOCKS + j) % 2, SH, SH, False)
                for f in (FT - 2, FT - 1):
                    down(UNITS - 1, (UNITS - 1) % 2, SH, f)

            @block.scalar
            def _(act):
                def hi(v, q, par):
                    if q % 2 == 0:
                        act.wait_ge(b_w[q // 2], 16 * v + 16)
                    act.activation(piece(wh[par], q), piece(ws, q), ACT.Copy).then_inc(b_whi, 1)

                def x_hi(v, par):
                    act.wait_ge(b_xg, v + 1)
                    wait(act, b_up, FT * (v - 1))
                    act.activation(xh[par][:, :, :], xg[:, :, :], ACT.Copy).then_inc(b_xh, 1)

                def h_hi(m, f):
                    act.wait_ge(b_hf, m + 1)
                    wait(act, b_down, m - 1)
                    act.activation(hh[f % 2][:, :], hf[f % 2][:, :], ACT.Copy).then_inc(b_hh, 1)

                def unit(u, par, weights=True, x=True):
                    for f in range(FT):
                        m = FT * u + f
                        act.wait_ge(b_up, m + 1)
                        wait(act, b_hf, m - 1)
                        act.activation(ge[f % 2][:, :], banks[f % 2][:, 0:SW], ACT.Gelu_apprx_tanh).then_inc(b_ge, 1)
                        if not (isinstance(m, int) and m == 0):
                            h_hi(m - 1, (f - 1) % FT)
                        if f == 4 and weights:
                            wait(act, b_down, FT * u)
                        if f < PIECES and weights:
                            hi(u + 1, f, 1 - par)
                        if f == PIECES and x:
                            x_hi(u + 1, 1 - par)

                for q in range(PIECES):
                    hi(0, q, 0)
                    if q == 3:
                        x_hi(0, 0)
                unit(0, 0)
                with act.Fori(0, (BLOCKS - 1) // 2) as t:
                    for j in range(2):
                        unit(t * 2 + (1 + j), 1 - j)
                with act.Fori(0, SHARED // 2 - 1) as t:
                    for j in range(2):
                        unit(t * 2 + (BLOCKS + j), (BLOCKS + j) % 2, False)
                unit(UNITS - 2, (UNITS - 2) % 2, False)
                unit(UNITS - 1, (UNITS - 1) % 2, False, False)
                h_hi(FT * UNITS - 1, FT - 1)

            @block.vector
            def _(dve):
                def h_lo(m, f):
                    dve.wait_ge(b_hh, m + 1)
                    dve.tensor_tensor(hl[f % 2][:, :], hf[f % 2][:, :], hh[f % 2][:, :].bitcast(F32),
                                      ALU.subtract).then_inc(b_hl, 1)

                def scatter(u, par, j):
                    if j == 0:
                        dve.wait_ge(b_down, FT * u + FT)
                        wait(dve, b_o, u)
                    s = dve.value_load(slot_sample[0:1, bass.ds(u * SLOTS + j, 1)], min_val=0, max_val=B + SLOTS - 1)
                    for o in range(KT):
                        last = dve.tensor_copy(eo[:, o, bass.ds(s * S, S)], banks[4 + 2 * par + o][:, j * S:(j + 1) * S])
                    if j == SLOTS - 1:
                        last.then_inc(b_o, 1)

                def store(u, par, j):
                    if j:
                        return
                    dve.wait_ge(b_down, FT * u + FT)
                    for o in range(KT):
                        last = dve.tensor_copy(sT[:, o, bass.ds((u - BLOCKS) * SW, SW)], banks[4 + 2 * par + o][:, 0:SW])
                    last.then_inc(b_o, 1)

                def lo(v, q, par, done=b_wlo2):
                    dve.wait_ge(b_whi, v * PIECES + (q + 1))
                    dve.tensor_tensor(piece(wl[par], q), piece(ws, q), piece(wh[par], q).bitcast(F32),
                                      ALU.subtract).then_inc(done, 1)

                def unit(u, par, last=scatter, weights=True):
                    for f in range(FT):
                        m = FT * u + f
                        dve.wait_ge(b_ge, m + 1)
                        wait(dve, b_hl, m - 1)
                        dve.tensor_tensor(hf[f % 2][:, :], banks[2 + f % 2][:, 0:SW], ge[f % 2][:, :],
                                          ALU.mult).then_inc(b_hf, 1)
                        if not (isinstance(m, int) and m == 0):
                            h_lo(m - 1, (f - 1) % FT)
                        if 2 <= f < 2 + SLOTS and last:
                            last(u - 1, 1 - par, f - 2)
                        if f >= PIECES and weights:
                            lo(u + 1, f - 2, 1 - par)

                lo(0, 1, 0, b_wlo01)
                dve.wait_ge(b_wlo01, 2)
                lo(0, 3, 0, b_wlo01)
                dve.wait_ge(b_xh, 1)
                dve.tensor_tensor(xl[0][:, :, :], xg[:, :, :], xh[0][:, :, :].bitcast(F32), ALU.subtract).then_inc(b_xl, 1)
                lo(0, 4, 0)
                lo(0, 5, 0)
                unit(0, 0, None)
                with dve.Fori(0, (BLOCKS - 1) // 2) as t:
                    for j in range(2):
                        unit(t * 2 + (1 + j), 1 - j)
                unit(BLOCKS, SH, scatter, False)
                unit(BLOCKS + 1, 1 - SH, store, False)
                with dve.Fori(1, SHARED // 2) as t:
                    for j in range(2):
                        unit(t * 2 + (BLOCKS + j), (BLOCKS + j) % 2, store, False)
                h_lo(FT * UNITS - 1, FT - 1)
                store(UNITS - 1, (UNITS - 1) % 2, 0)


def load_experts_weights(sp, io, e, ws, m_w, m_wlo):
    for n, name in enumerate(("m_guT", "m_dnT")):
        wait(sp, m_wlo, 3 * (e - 1) + 2 + n)
        sp.dma_start(ws[n][:, :, :], io[name][bass.ds(e, 1), :, :].rearrange(
            "e (k p) n -> p (e k) n", p=P)).then_inc(m_w[n], 16)


def weight_piece(t, q):
    return t[0][:, q, :] if q < KT else t[1][:, :, :]


def split_hi(act, e, q, ws, wh, m_w, m_whi):
    if q != 1:
        act.wait_ge(m_w[q // 2], e * 16 + 16)
    act.activation(weight_piece(wh, q), weight_piece(ws, q), ACT.Copy).then_inc(m_whi, 1)


def split_lo(pool, e, q, ws, wh, wl, m_whi, m_wlo):
    pool.wait_ge(m_whi, e * 3 + (q + 1))
    pool.tensor_tensor(weight_piece(wl, q), weight_piece(ws, q), weight_piece(wh, q).bitcast(F32),
                       ALU.subtract).then_inc(m_wlo, 1)


def mix(nc, io, banks, sb0, sem, eo, sT, hh, hl, lgT, weights, g_w, g_in):
    ws, wh, wl, m_w, m_whi, m_wlo = weights
    with ExitStack() as c:
        def sb(name, shape, dt=F32):
            return sb0(name, shape, dt, c)

        g0, g1, rw = g_w
        gi = sb("gi", [P, 2 * KT, B])
        gr = sb("gr", [P, KT, B])
        z = sb("z", [P, 2, B])
        zm = sb("zm", [P, B])
        zs = sb("zs", [P, B])
        ew = [sb(f"ew{k}", [P, TB]) for k in range(2)]
        g_step, g_pe, g_ew, g_sw, g_h, g_hh, g_hl, g_l = (sem(n) for n in (
            "g_gate_step", "g_gate_products", "g_expert_weighed", "g_shared_weighed", "g_mixed",
            "g_hi", "g_lo", "g_logits_ready"))
        BS = TB // S
        M = NTB * KT

        def by(ap):
            return ap.rearrange("p (b n) -> p b n", n=S)

        def part(t, m):
            return t[:, m % KT, (m // KT) * TB:(m // KT + 1) * TB]

        POOL_LO = range(1, M - 2, 2)

        def lo(eng, m):
            eng.wait_ge(g_hh, m + 1)
            eng.tensor_tensor(part(hl, m), part(sT, m), part(hh, m).bitcast(F32), ALU.subtract).then_inc(g_hl, 1)

        with nc.Block() as block:
            @block.sync
            def _(sp):

                load_experts_weights(sp, io, 0, ws, m_w, m_wlo)

            @block.tensor
            def _(pe):
                pe.wait_ge(g_in, 48)
                pe.wait_ge(g_step, 1)
                for o in range(KT):
                    for k in range(2 * KT):
                        mm = pe.matmul(banks[0][:, o * B:(o + 1) * B], g0[:, k, o * P:(o + 1) * P], gi[:, k, :],
                                       start=k == 0, stop=k == 2 * KT - 1)
                mm.then_inc(g_pe, 1)
                pe.wait_ge(g_step, 2)
                for r in range(2):
                    for k in range(KT):
                        mm = pe.matmul(banks[1][:, r * B:(r + 1) * B], g1[:, k, r:r + 1].to_broadcast([P, P]),
                                       gr[:, k, :], start=k == 0, stop=k == KT - 1)
                mm.then_inc(g_pe, 1)
                for t in range(NTB):
                    pe.wait_ge(g_h, KT * t + KT)
                    for k in range(KT):
                        mm = pe.matmul(banks[2 + t][0:EM, :], rw[:, k, :], sT[:, k, t * TB:(t + 1) * TB],
                                       start=k == 0, stop=k == KT - 1)
                    mm.then_inc(g_l, 1)

            @block.gpsimd
            def _(pool):
                for q in range(2):
                    split_lo(pool, 0, q, ws, wh[0], wl[0], m_whi, m_wlo)
                pool.wait_ge(g_step, 8)
                for m in range(M):
                    wait(pool, g_h, m - 1)
                    w = bcast(z[:, 0, (m // KT) * BS:(m // KT + 1) * BS], 2, S)
                    pool.tensor_tensor(by(ew[m % 2][:, :]), by(part(eo, m)), w, ALU.mult).then_inc(g_ew, 1)
                    if m - 2 in POOL_LO:
                        lo(pool, m - 2)
                split_lo(pool, 0, 2, ws, wh[0], wl[0], m_whi, m_wlo)

            @block.scalar
            def _(act):
                for q in range(3):
                    split_hi(act, 0, q, ws, wh[0], m_w, m_whi)
                act.wait_ge(g_step, 5)
                act.activation(z[:, :, :], z[:, :, :], ACT.Exp).then_inc(g_pe, 1)
                for m in range(M):
                    act.wait_ge(g_h, m + 1)
                    act.activation(part(hh, m), part(sT, m), ACT.Copy).then_inc(g_hh, 1)
                for t in range(NTB):
                    act.wait_ge(g_l, t + 1)
                    last = act.activation(lgT[:, t * TB:(t + 1) * TB], banks[2 + t][0:EM, :], ACT.Copy)
                last.then_inc(g_pe, 1)

            @block.vector
            def _(dve):
                dve.tensor_copy(gi[:, 0:KT, :], eo[:, :, 0:N:S])
                dve.tensor_copy(gi[:, KT:2 * KT, :], sT[:, :, 0:N:S]).then_inc(g_step, 1)
                dve.wait_ge(g_pe, 1)
                dve.tensor_scalar(gr[:, :, :], banks[0][:, 0:KT * B].rearrange("p (k b) -> p k b", k=KT), 0.0, None,
                                  ALU.max).then_inc(g_step, 1)
                dve.wait_ge(g_pe, 2)
                dve.tensor_copy(z[:, :, :], banks[1][:, 0:2 * B].rearrange("p (k b) -> p k b", k=2)).then_inc(g_step, 1)
                dve.wait_ge(g_step, 3)
                dve.tensor_tensor(zm[:, :], z[:, 0, :], z[:, 1, :], ALU.max).then_inc(g_step, 1)
                dve.wait_ge(g_step, 4)
                dve.tensor_tensor(z[:, :, :], z[:, :, :], bcast(zm[:, :], 1, 2), ALU.subtract).then_inc(g_step, 1)
                dve.wait_ge(g_pe, 3)
                dve.tensor_tensor(zs[:, :], z[:, 0, :], z[:, 1, :], ALU.add).then_inc(g_step, 1)
                dve.wait_ge(g_step, 6)
                dve.reciprocal(zm[:, :], zs[:, :]).then_inc(g_step, 1)
                dve.wait_ge(g_step, 7)
                dve.tensor_tensor(z[:, :, :], z[:, :, :], bcast(zm[:, :], 1, 2), ALU.mult).then_inc(g_step, 1)
                dve.wait_ge(g_step, 8)



                for m in range(M):
                    s = part(sT, m)
                    w = bcast(z[:, 1, (m // KT) * BS:(m // KT + 1) * BS], 2, S)
                    dve.tensor_tensor(by(s), by(s), w, ALU.mult).then_inc(g_sw, 1)
                    if m and m - 1 not in POOL_LO:
                        lo(dve, m - 1)
                    dve.wait_ge(g_sw, m + 1)
                    dve.wait_ge(g_ew, m + 1)
                    dve.tensor_tensor(s, ew[m % 2][:, :], s, ALU.add).then_inc(g_h, 1)
                lo(dve, M - 1)


def mixture(nc, io, banks, sb0, sem, hh, hl, lgT, ident, weights, acc):
    ws, wh, wl, m_w, m_whi, m_wlo = weights
    with ExitStack() as c:
        def sb(name, shape, dt=F32):
            return sb0(name, shape, dt, c)

        rb = sb("rb", [P, EM])
        lg = sb("lg", [P, PAIRS, EM])
        cb = sb("cb", [P, PAIRS, EM])
        gt = sb("gt", [P, PAIRS, EM])
        rank = sb("rank", [P, PAIRS, EM])
        m1 = sb("m1", [P, PAIRS])
        m2 = sb("m2", [P, PAIRS])
        gub = sb("gub", [P, EM, 2 * JT])

        ga, up, sg, gu, af = ([sb(f"m_{n}{k}", [P, TB]) for k in range(2)] for n in ("ga", "up", "sg", "gu", "af"))
        ah = [sb(f"ah{k}", [P, JT, TB], F32R) for k in range(2)]
        al = [sb(f"al{k}", [P, JT, TB], F32R) for k in range(2)]
        cbT = sb("cbT", [EM, N])
        db = sb("db", [EM, D])
        m_in, m_l_ready, m_soft, m_step, m_c = (sem(n) for n in (
            "m_small_in", "m_logits_ready", "m_exp", "m_router_step", "m_combine"))
        m_gu_ready, m_gu, m_sg, m_t, m_a, m_ah, m_al, m_d_ready, m_d = (sem(n) for n in (
            "m_gate_up_ready", "m_gate_up_clipped", "m_sigmoid", "m_product", "m_act",
            "m_act_hi", "m_act_lo", "m_down_ready", "m_down_added"))
        m_ct_ready, m_ct, m_b_ready, m_b = (sem(n) for n in (
            "m_combineT_ready", "m_combineT_copied", "m_bias_ready", "m_bias_copied"))
        LAST = EM * NTB * JT - 1

        def steps(two_experts, eng, peel=0):
            two_experts(0)
            with eng.Fori(1, EM // 2 - peel) as t:
                two_experts(t)
            for t in range(EM // 2 - peel, EM // 2):
                two_experts(t)

        def last(t, par):
            return isinstance(t, int) and t * 2 + par == EM - 1

        with nc.Block() as block:
            @block.sync
            def _(sp):


                sp.dma_start(rb[:, :], io["m_rb"].partition_broadcast(P)).then_inc(m_in, 16)
                sp.dma_start(gub[:, :, :], io["m_gub"]).then_inc(m_in, 16)
                sp.dma_start(db[:, :], io["m_db"]).then_inc(m_in, 16)
                with sp.Fori(1, EM) as e:
                    load_experts_weights(sp, io, e, ws, m_w, m_wlo)

            @block.tensor
            def _(pe):
                for t in range(PAIRS):
                    mm = pe.transpose(banks[7][:, t * EM:(t + 1) * EM], lgT[:, t * P:(t + 1) * P], ident[0:EM, 0:EM])
                mm.then_inc(m_l_ready, 1)

                def combine():
                    pe.wait_ge(m_c, 1)
                    for t in range(PAIRS):
                        mm = pe.transpose(banks[4 + t // 4][0:EM, (t % 4) * P:(t % 4 + 1) * P], cb[:, t, :], ident[:, :])
                        if t % 4 == 3:
                            mm.then_inc(m_ct_ready, 1)

                def bias(tb):
                    pe.wait_ge(m_ct, 2 if tb == 0 else PAIRS // 4)
                    wait(pe, m_b, 2 * (tb - 1))
                    for b in range(2):
                        for tt in range(2):
                            at = (4 * tb + 2 * b + tt) * P
                            mm = pe.matmul(banks[4 + 2 * (tb % 2) + b][:, tt * D:(tt + 1) * D], cbT[:, at:at + P],
                                           db[:, :], start=True, stop=True)
                    mm.then_inc(m_b_ready, 1)

                def gate_up(n, tb, par, j):
                    m = n * JT + j
                    wait(pe, m_gu, m - 1)
                    for r in range(2):
                        for k in range(KT):
                            mm = mm3(pe, banks[2 * r + j % 2][:, :],
                                     [w[par][0][:, k, (r * JT + j) * P:(r * JT + j + 1) * P] for w in (wh, wl)],
                                     [h[:, k, tb * TB:(tb + 1) * TB] for h in (hh, hl)], k == 0, k == KT - 1)
                    mm.then_inc(m_gu_ready, 1)

                def down(n, par, wpar, b):
                    pe.wait_ge(m_al, n * JT + JT)
                    wait(pe, m_d, 2 * (n - 2) + b + 1)
                    for tt in range(2):
                        at = (2 * b + tt) * P
                        for j in range(JT):
                            mm = mm3(pe, banks[4 + 2 * par + b][:, tt * D:(tt + 1) * D],
                                     [a[par][:, j, at:at + P] for a in (ah, al)],
                                     [w[wpar][1][:, j, :] for w in (wh, wl)], j == 0, j == JT - 1)
                    mm.then_inc(m_d_ready, 1)

                def two_experts(t):
                    for par in range(2):
                        e = t * 2 + par
                        pe.wait_ge(m_wlo, e * 3 + 3)
                        for tb in range(NTB):
                            n = e * NTB + tb
                            for j in range(JT):
                                gate_up(n, tb, par, j)
                                if isinstance(n, int) and n * JT + j == 1:
                                    combine()
                                if isinstance(n, int) and 2 <= n * JT + j < 2 + NTB:
                                    bias(n * JT + j - 2)
                                if j >= 2 and not (isinstance(n, int) and n == 0):
                                    if isinstance(n, int) and n <= 2:
                                        pe.wait_ge(m_b, 2 * n + 4)
                                    down(n - 1, (tb + 1) % 2, par if tb else 1 - par, j - 2)

                steps(two_experts, pe)
                for b in range(2):
                    down(EM * NTB - 1, 1, 1, b)

            @block.gpsimd
            def _(pool):


                def two_experts(t):
                    for par in range(2):
                        for tb in range(NTB):
                            for j in range(JT):
                                m = ((t * 2 + par) * NTB + tb) * JT + j
                                pool.wait_ge(m_t, m + 1)
                                wait(pool, m_al, m - 1)
                                pool.tensor_tensor(af[j % 2][:, :], gu[j % 2][:, :], sg[j % 2][:, :], ALU.mult).then_inc(m_a, 1)
                                if tb == 1 and j < 3 and not last(t, par):
                                    split_lo(pool, t * 2 + (par + 1), j, ws, wh[1 - par], wl[1 - par], m_whi, m_wlo)


                steps(two_experts, pool, 1)

            @block.scalar
            def _(act):
                act.wait_ge(m_soft, 1)
                act.activation(lg[:, :, :], lg[:, :, :], ACT.Exp).then_inc(m_soft, 1)

                def a_hi(m, j, par):
                    act.wait_ge(m_a, m + 1)
                    act.activation(ah[par][:, j, :], af[j % 2][:, :], ACT.Copy).then_inc(m_ah, 1)

                def two_experts(t):
                    for par in range(2):
                        for tb in range(NTB):
                            n = (t * 2 + par) * NTB + tb
                            for j in range(JT):
                                m = n * JT + j
                                act.wait_ge(m_gu, m + 1)
                                wait(act, m_a, m - 1)
                                act.activation(sg[j % 2][:, :], ga[j % 2][:, :], ACT.Sigmoid, scale=SWIGLU_ALPHA).then_inc(m_sg, 1)
                                if isinstance(m, int) and m == 1:
                                    for q in range(PAIRS // 4):
                                        act.wait_ge(m_ct_ready, q + 1)
                                        act.activation(cbT[:, q * TB:(q + 1) * TB], banks[4 + q][0:EM, :],
                                                       ACT.Copy).then_inc(m_ct, 1)
                                if isinstance(m, int) and 3 <= m < 3 + NTB:
                                    act.wait_ge(m_b_ready, m - 2)
                                    for b in range(2):
                                        at = 4 * (m - 3) + 2 * b
                                        act.activation(acc[:, at:at + 2, :],
                                                       banks[4 + 2 * ((m - 3) % 2) + b][:, :].rearrange("p (t d) -> p t d", d=D),
                                                       ACT.Copy).then_inc(m_b, 1)

                                if j == 1:
                                    wait(act, m_d_ready, 2 * (n - 1))
                                if j:
                                    a_hi(m - 1, j - 1, tb % 2)
                                elif not (isinstance(m, int) and m == 0):
                                    a_hi(m - 1, JT - 1, (tb + 1) % 2)
                                if tb == 1 and j < 3 and not last(t, par):
                                    split_hi(act, t * 2 + (par + 1), j, ws, wh[1 - par], m_w, m_whi)

                steps(two_experts, act, 1)
                a_hi(LAST, JT - 1, (NTB - 1) % 2)

            @block.vector
            def _(dve):
                cnt = [0]

                def then(ins):
                    ins.then_inc(m_step, 1)
                    cnt[0] += 1
                    dve.wait_ge(m_step, cnt[0])

                def route():
                    then(dve.memset(rank[:, :, :], 0.0))
                    for i in range(EM):
                        li = lg[:, :, i:i + 1]
                        if i:
                            dve.tensor_tensor(gt[:, :, 0:i], li.to_broadcast([P, PAIRS, i]), lg[:, :, 0:i], ALU.is_gt)
                        if i < EM - 1:
                            dve.tensor_tensor(gt[:, :, i + 1:EM], li.to_broadcast([P, PAIRS, EM - 1 - i]),
                                              lg[:, :, i + 1:EM], ALU.is_ge)
                        then(dve.memset(gt[:, :, i:i + 1], 0.0))
                        then(dve.tensor_tensor(rank[:, :, :], rank[:, :, :], gt[:, :, :], ALU.add))
                    then(dve.tensor_scalar(rank[:, :, :], rank[:, :, :], float(TOP_K), None, ALU.is_lt))
                    then(dve.tensor_reduce(m1[:, :], lg[:, :, :], AX.X, ALU.max))
                    dve.tensor_tensor(lg[:, :, :], lg[:, :, :], bcast(m1[:, :], 2, EM), ALU.subtract).then_inc(m_soft, 1)
                    dve.wait_ge(m_soft, 2)
                    then(dve.tensor_tensor(lg[:, :, :], lg[:, :, :], rank[:, :, :], ALU.mult))
                    then(dve.tensor_reduce(m1[:, :], lg[:, :, :], AX.X, ALU.add))
                    then(dve.reciprocal(m2[:, :], m1[:, :]))
                    dve.tensor_tensor(cb[:, :, :], lg[:, :, :], bcast(m2[:, :], 2, EM), ALU.mult).then_inc(m_c, 1)
                    dve.wait_ge(m_c, 1)

                def clip(e, m, j):
                    dve.wait_ge(m_gu_ready, m + 1)
                    wait(dve, m_t, m - 1)
                    dve.tensor_scalar(ga[j % 2][:, :], banks[j % 2][:, :],
                                      gub[:, bass.ds(e, 1), j:j + 1].rearrange("p a b -> p (a b)"), LIMIT,
                                      ALU.add, ALU.min)
                    dve.tensor_scalar(up[j % 2][:, :], banks[2 + j % 2][:, :],
                                      gub[:, bass.ds(e, 1), JT + j:JT + j + 1].rearrange("p a b -> p (a b)"), 1.0 - LIMIT,
                                      ALU.add, ALU.max).then_inc(m_gu, 1)

                def product(m, j):
                    dve.wait_ge(m_sg, m + 1)
                    wait(dve, m_a, m - 1)
                    dve.scalar_tensor_tensor(gu[j % 2][:, :], up[j % 2][:, :], 1.0 + LIMIT, ga[j % 2][:, :],
                                             ALU.min, ALU.mult).then_inc(m_t, 1)

                def a_lo(m, j, par):
                    dve.wait_ge(m_ah, m + 1)
                    dve.tensor_tensor(al[par][:, j, :], af[j % 2][:, :], ah[par][:, j, :].bitcast(F32),
                                      ALU.subtract).then_inc(m_al, 1)

                def add_down(e, n, tb, b):
                    dve.wait_ge(m_d_ready, 2 * n + b + 1)
                    if isinstance(n, int) and n < NTB:
                        dve.wait_ge(m_b, 2 * n + b + 1)
                    wait(dve, m_d, 2 * (n - NTB) + b + 1)
                    for tt in range(2):
                        t = 4 * tb + 2 * b + tt
                        last = dve.scalar_tensor_tensor(
                            acc[:, t, :], banks[4 + 2 * (tb % 2) + b][:, tt * D:(tt + 1) * D],
                            cb[:, t, bass.ds(e, 1)], acc[:, t, :], ALU.mult, ALU.add)
                    last.then_inc(m_d, 1)

                dve.wait_ge(m_in, 48)
                then(dve.tensor_scalar(gub[:, :, JT:2 * JT], gub[:, :, JT:2 * JT], 1.0, None, ALU.add))
                dve.wait_ge(m_l_ready, 1)
                then(dve.tensor_tensor(lg[:, :, :], banks[7][:, 0:PAIRS * EM].rearrange("p (t e) -> p t e", e=EM),
                                       bcast(rb[:, :], 1, PAIRS), ALU.add))
                route()

                def two_experts(t):
                    for par in range(2):
                        e = t * 2 + par
                        for tb in range(NTB):
                            n = e * NTB + tb
                            for j in range(JT):
                                m = n * JT + j
                                clip(e, m, j)
                                if not (isinstance(m, int) and m < 2):
                                    a_lo(m - 2, (j - 2) % JT, (tb if j >= 2 else tb + 1) % 2)
                                if not (isinstance(m, int) and m < 1):
                                    product(m - 1, (j - 1) % JT)
                                for lag, at, b in ((1, JT - 1, 0), (2, JT - 2, 1)):
                                    if j == at and not (isinstance(n, int) and n < lag):
                                        add_down(e if tb >= lag else e - 1, n - lag, (tb - lag) % NTB, b)

                steps(two_experts, dve)
                product(LAST, JT - 1)
                a_lo(LAST - 1, JT - 2, 1)
                a_lo(LAST, JT - 1, 1)
                add_down(EM - 1, EM * NTB - 2, NTB - 2, 1)
                for b in range(2):
                    add_down(EM - 1, EM * NTB - 1, NTB - 1, b)


def attention1_tensors(sb, sem, c):
    w = {n: sb("n_" + n, s, F32, c) for n, s in dict(
        wat=[P, KT, 3 * D], bv=[P, D], wp=[P, KT, D], bp=[P, KT],
        bat=[P, 4],
        fac=[P, 2, S],
        hm=[P, P // HD1]).items()}
    return w, sem("n_in")


def load_attention1(sp, io, w, n_in):
    for n, name in (("bat", "n_bat"), ("hm", "n_hm"), ("bp", "n_bp")):
        sp.dma_start(w[n][:, :], io[name]).then_inc(n_in, 16)
    sp.dma_start(w["bv"][:, :], io["n_bv"].partition_broadcast(P)).then_inc(n_in, 16)
    sp.dma_start(w["fac"][:, :, :], io["n_fac"]).then_inc(n_in, 16)
    for n, name in (("wat", "n_waT"), ("wp", "n_wpT")):
        sp.dma_start(w[n][:, :, :], io[name].rearrange("(k p) n -> p k n", p=P)).then_inc(n_in, 16)


def lora_ffn(nc, io, banks, sb0, sem, xT, zT, acc, ident, oh_lora, n_w, n_in):
    with ExitStack() as c:
        def sb(name, shape, dt=F32):
            return sb0(name, shape, dt, c)

        wi = sb("wi", [P, KT, FF])
        wo = sb("l_wo", [P, FT, D])
        cia = sb("cia", [RL, D])
        cib = sb("cib", [RL, FF])
        coa = sb("coa", [RL, FF])
        cob = sb("cob", [RL, D])
        eia = sb("eia", [P, KT, P])
        eib = sb("eib", [P, FF])
        eoa = sb("eoa", [P, FT, P])
        eob = sb("eob", [P, D])

        def halves(name, t):
            return [sb(f"{name}_{part}", list(t.shape), F32R) for part in ("hi", "lo")]

        wi2, wo2, eia2, eib2, eoa2, eob2, x2 = (halves(n, t) for n, t in (
            ("wi", wi), ("l_wo", wo), ("eia", eia), ("eib", eib), ("eoa", eoa), ("eob", eob), ("x", zT)))
        low2 = [sb(f"low_{part}", [P, N], F32R) for part in ("hi", "lo")]
        low = [sb(f"low{k}", [P, TB]) for k in range(2)]
        lowo2 = [sb(f"lowo_{part}", [P, TB], F32R) for part in ("hi", "lo")]
        hid2 = [[sb(f"hid{k}_{part}", [P, TB], F32R) for part in ("hi", "lo")] for k in range(2)]
        l_small, l_wi, l_wo = (sem(n) for n in ("l_common_in", "l_wi_in", "l_wo_in"))
        l_e = [sem(f"l_{n}_in") for n in ("eia", "eib", "eoa", "eob")]
        (l_s_ready, l_x, l_xh, l_xl, l_f_ready, l_f, l_wh, l_wl, l_low_ready, l_low, l_lowh, l_lowl) = (
            sem(n) for n in ("l_sum_ready", "l_x_summed", "l_x_hi", "l_x_lo", "l_fold_ready", "l_folded",
                             "l_weights_hi", "l_weights_lo", "l_low_ready", "l_low_masked", "l_low_hi", "l_low_lo"))
        l_h_ready, l_hh, l_hl, l_lo_ready, l_lo, l_loh, l_lol, l_o_ready, l_o = (
            sem(n) for n in ("l_hidden_ready", "l_relu_hi", "l_relu_lo", "l_lowo_ready", "l_lowo_masked",
                             "l_lowo_hi", "l_lowo_lo", "l_out_ready", "l_out_copied"))
        FW, FO = KT * 2, FT // 2
        XN = NTB * KT

        def fold(t, n):
            wi_, wo_ = t
            if n < FW:
                return wi_[:, n // 2, (n % 2) * 512:(n % 2 + 1) * 512]
            return wo_[:, 2 * (n - FW):2 * (n - FW) + 2, :]

        pieces = [(eia[:, :, :], eia2, 0), (eib[:, :], eib2, 1)]
        pieces += [(fold((wi, wo), n), [fold((wi2[r], wo2[r]), n) for r in range(2)], None) for n in range(FW + FO)]
        pieces += [(eoa[:, :, :], eoa2, 2), (eob[:, :], eob2, 3)]
        UP, OUT = 2 + FW, 3 + FW + FO

        def x_piece(t, n):
            return t[:, n % KT, (n // KT) * TB:(n // KT + 1) * TB]

        def by(ap):
            return ap.rearrange("p (b n) -> p b n", n=S)

        def steps(two, eng):
            two(0)
            with eng.Fori(1, NTB // 2) as t:
                two(t)

        def first(u):
            return isinstance(u, int) and u == 0

        with nc.Block() as block:
            @block.sync
            def _(sp):
                sp.dma_start(eia[:, :, :], io["l_eiaT"].rearrange("(k p) n -> p k n", p=P)).then_inc(l_e[0], 16)
                sp.dma_start(eib[:, :], io["l_eibT"]).then_inc(l_e[1], 16)
                for dst, name in ((cia, "l_cia"), (cib, "l_cibT"), (coa, "l_coa"), (cob, "l_cobT")):
                    sp.dma_start(dst[:, :], io[name]).then_inc(l_small, 16)
                sp.dma_start(wi[:, :, :], io["l_wiT"].rearrange("(k p) n -> p k n", p=P)).then_inc(l_wi, 16)
                sp.dma_start(wo[:, :, :], io["l_woT"].rearrange("(k p) n -> p k n", p=P)).then_inc(l_wo, 16)
                sp.dma_start(eoa[:, :, :], io["l_eoaT"].rearrange("(k p) n -> p k n", p=P)).then_inc(l_e[2], 16)
                sp.dma_start(eob[:, :], io["l_eobT"]).then_inc(l_e[3], 16)
                load_attention1(sp, io, n_w, n_in)

            @block.tensor
            def _(pe):
                for n in range(XN):
                    t, o = n // KT, n % KT
                    if n >= 4:
                        pe.wait_ge(l_x, n - 3)
                    for j in range(TB // P):
                        mm = pe.transpose(banks[n % 4][:, j * P:(j + 1) * P], acc[:, t * 4 + j, o * P:(o + 1) * P],
                                          ident[:, :])
                    mm.then_inc(l_s_ready, 1)
                pe.wait_ge(l_small, 64)
                for n in range(FW + FO):
                    if n >= 4:
                        pe.wait_ge(l_f, n - 3)
                    if n < FW:
                        k, f = n // 2, n % 2
                        mm = pe.matmul(banks[4 + n % 4][:, :], cia[:, k * P:(k + 1) * P], cib[:, f * 512:(f + 1) * 512],
                                       start=True, stop=True)
                    else:
                        for g in range(2):
                            at = (2 * (n - FW) + g) * P
                            mm = pe.matmul(banks[4 + n % 4][:, g * D:(g + 1) * D], coa[:, at:at + P], cob[:, :],
                                           start=True, stop=True)
                    mm.then_inc(l_f_ready, 1)
                pe.wait_ge(l_wl, 1)
                for t in range(NTB):
                    pe.wait_ge(l_xl, KT * t + KT)
                    pe.wait_ge(l_x, min(XN, XN - NTB + t + 1))
                    for k in range(KT):
                        mm = mm3(pe, banks[t][:, :], [w[:, k, :] for w in eia2],
                                 [x[:, k, t * TB:(t + 1) * TB] for x in x2], k == 0, k == KT - 1)
                    mm.then_inc(l_low_ready, 1)
                pe.wait_ge(l_wl, UP)

                def up(u, f):
                    m = FT * u + f
                    if isinstance(m, int) and m < 2:
                        pe.wait_ge(l_lowl, m + 1)
                    wait(pe, l_hl, m - 1)
                    at = bass.ds(u * TB, TB)
                    for k in range(KT):
                        mm3(pe, banks[f % 2][:, :], [w[:, k, f * P:(f + 1) * P] for w in wi2],
                            [x[:, k, at] for x in x2], k == 0, False)
                    if f == 0 and isinstance(u, int):
                        pe.wait_ge(l_lowl, u + 1)
                    mm3(pe, banks[f % 2][:, :], [w[:, f * P:(f + 1) * P] for w in eib2], [x[:, at] for x in low2],
                        False, True).then_inc(l_h_ready, 1)

                def second(u, par, f):
                    pe.wait_ge(l_hl, FT * u + (f + 1))
                    if f == 0:
                        if isinstance(u, int) and u < 2:
                            pe.wait_ge(l_low, NTB)
                            pe.wait_ge(l_wl, OUT)
                        wait(pe, l_o, u - 1)
                    mm = mm3(pe, banks[2 + par][:, :], [w[:, f, :] for w in eoa2], [h[:, :] for h in hid2[f % 2]],
                             f == 0, f == FT - 1)
                    if f == FT - 1:
                        mm.then_inc(l_lo_ready, 1)
                    for o in range(KT):
                        mm3(pe, banks[4 + 2 * par + o][:, :], [w[:, f, o * P:(o + 1) * P] for w in wo2],
                            [h[:, :] for h in hid2[f % 2]], f == 0, False)

                def finish(u, par):
                    pe.wait_ge(l_lol, u + 1)
                    if first(u):
                        pe.wait_ge(l_wl, len(pieces))
                    for o in range(KT):
                        mm = mm3(pe, banks[4 + 2 * par + o][:, :], [w[:, o * P:(o + 1) * P] for w in eob2],
                                 [x[:, :] for x in lowo2], False, True)
                    mm.then_inc(l_o_ready, 1)

                def two(t):
                    for par in range(2):
                        u = t * 2 + par
                        for f in range(FT):
                            up(u, f)
                            if f == 0 and not first(u):
                                second(u - 1, 1 - par, FT - 1)
                            if f == 1 and not first(u):
                                finish(u - 1, 1 - par)
                            if f:
                                second(u, par, f - 1)

                steps(two, pe)
                second(NTB - 1, 1, FT - 1)
                finish(NTB - 1, 1)

            @block.gpsimd
            def _(pool):
                for n, (src, (hi, lo), _) in enumerate(pieces):
                    pool.wait_ge(l_wh, n + 1)
                    pool.tensor_tensor(whole(lo), src, whole(hi).bitcast(F32), ALU.subtract).then_inc(l_wl, 1)

            @block.scalar
            def _(act):
                def split(n):
                    src, (hi, _), loaded = pieces[n]
                    if loaded is None:
                        act.wait_ge(l_f, n - 1)
                    else:
                        act.wait_ge(l_e[loaded], 16)
                    act.activation(whole(hi), src, ACT.Copy).then_inc(l_wh, 1)

                for n in range(XN):
                    if n in (2, 4):
                        split(n // 2 - 1)
                    act.wait_ge(l_x, n + 1)
                    act.activation(x_piece(x2[0], n), x_piece(xT, n), ACT.Copy).then_inc(l_xh, 1)
                for n in range(2, 2 + FW + FO):
                    split(n)
                for t in range(NTB):
                    act.wait_ge(l_low, t + 1)
                    act.activation(low2[0][:, t * TB:(t + 1) * TB], low[t % 2][:, :], ACT.Copy).then_inc(l_lowh, 1)
                split(2 + FW + FO)
                split(3 + FW + FO)

                def lowo_hi(u):
                    act.wait_ge(l_lo, u + 1)
                    wait(act, l_o_ready, u)
                    act.activation(lowo2[0][:, :], low[0][:, :], ACT.Copy).then_inc(l_loh, 1)

                def two(t):
                    for par in range(2):
                        u = t * 2 + par
                        for f in range(FT):
                            if f == 1 and not first(u):
                                lowo_hi(u - 1)
                            act.wait_ge(l_h_ready, FT * u + (f + 1))
                            act.activation(hid2[f % 2][0][:, :], banks[f % 2][:, :], ACT.Relu).then_inc(l_hh, 1)

                steps(two, act)
                lowo_hi(NTB - 1)

            @block.vector
            def _(dve):
                def x_lo(n):
                    dve.wait_ge(l_xh, n + 1)
                    dve.tensor_tensor(x_piece(x2[1], n), x_piece(xT, n), x_piece(x2[0], n).bitcast(F32),
                                      ALU.subtract).then_inc(l_xl, 1)

                for n in range(XN):
                    dve.wait_ge(l_s_ready, n + 1)
                    at = x_piece(xT, n)
                    dve.tensor_tensor(at, banks[n % 4][:, :], at, ALU.add).then_inc(l_x, 1)
                    if n:
                        x_lo(n - 1)
                x_lo(XN - 1)
                for n in range(FW + FO):
                    dve.wait_ge(l_f_ready, n + 1)
                    if n == 0:
                        dve.wait_ge(l_wi, 16)
                    if n == FW:
                        dve.wait_ge(l_wo, 16)
                    at = fold((wi, wo), n)
                    bank = banks[4 + n % 4][:, :]
                    if n >= FW:
                        bank = bank.rearrange("p (g n) -> p g n", g=2)
                    dve.scalar_tensor_tensor(at, bank, 2.0, at, ALU.mult, ALU.add).then_inc(l_f, 1)
                for t in range(NTB):
                    dve.wait_ge(l_low_ready, t + 1)
                    if t >= 2:
                        dve.wait_ge(l_lowl, t - 1)
                    dve.tensor_tensor(by(low[t % 2][:, :]), by(banks[t][:, :]),
                                      bcast(oh_lora[:, t * (TB // S):(t + 1) * (TB // S)], 2, S), ALU.mult).then_inc(l_low, 1)
                    dve.wait_ge(l_lowh, t + 1)
                    at = slice(t * TB, (t + 1) * TB)
                    dve.tensor_tensor(low2[1][:, at], low[t % 2][:, :], low2[0][:, at].bitcast(F32),
                                      ALU.subtract).then_inc(l_lowl, 1)

                def mask(u, par):
                    dve.wait_ge(l_lo_ready, u + 1)
                    if first(u):
                        dve.wait_ge(l_lowl, NTB)
                    wait(dve, l_lol, u)
                    dve.tensor_tensor(by(low[0][:, :]), by(banks[2 + par][:, :]),
                                      bcast(oh_lora[:, bass.ds(u * (TB // S), TB // S)], 2, S), ALU.mult).then_inc(l_lo, 1)

                def lowo_lo(u):
                    dve.wait_ge(l_loh, u + 1)
                    dve.tensor_tensor(lowo2[1][:, :], low[0][:, :], lowo2[0][:, :].bitcast(F32),
                                      ALU.subtract).then_inc(l_lol, 1)

                def store(u, par):
                    dve.wait_ge(l_o_ready, u + 1)
                    for o in range(KT):
                        last = dve.tensor_copy(zT[:, o, bass.ds(u * TB, TB)], banks[4 + 2 * par + o][:, :])
                    last.then_inc(l_o, 1)

                def two(t):
                    for par in range(2):
                        u = t * 2 + par
                        for f in range(FT):
                            if f == 1 and not first(u):
                                lowo_lo(u - 1)
                            dve.wait_ge(l_hh, FT * u + (f + 1))
                            dve.scalar_tensor_tensor(hid2[f % 2][1][:, :], banks[f % 2][:, :], 0.0,
                                                     hid2[f % 2][0][:, :].bitcast(F32), ALU.max, ALU.subtract).then_inc(l_hl, 1)
                            if f == 0 and not first(u):
                                mask(u - 1, 1 - par)
                            if f == 2 and not first(u):
                                store(u - 1, 1 - par)

                steps(two, dve)
                mask(NTB - 1, 1)
                lowo_lo(NTB - 1)
                store(NTB - 1, 1)


def attention1(nc, io, banks, sb0, sem, xT, zT, ident, mask, n_w, n_in, f_w, f_in):
    with ExitStack() as c:
        def sb(name, shape, dt=F32):
            return sb0(name, shape, dt, c)

        HT = P // HD1
        wat, bat, bv, fac, hm, wp, bp = (n_w[n] for n in ("wat", "bat", "bv", "fac", "hm", "wp", "bp"))
        zs = [sb(f"zs{k}", [P, KT, P]) for k in range(2)]
        qT = [sb(f"qT{k}", [P, 2, P]) for k in range(2)]
        kT = [sb(f"kT{k}", [P, 2, P]) for k in range(2)]
        kpad = [sb(f"k1pad{k}", [P, 2, HT, P]) for k in range(2)]
        v = [sb(f"vp{k}", [P, HEADS, 32]) for k in range(2)]
        sc = sb("sc1", [P, HEADS, S])
        ex = [sb(f"ex1_{k}", [P, HEADS, S]) for k in range(2)]
        mx = sb("mx1", [P, HEADS])
        sm = sb("sm1", [P, HEADS])
        ri = sb("ri1", [P, HEADS])
        pr = [sb(f"pr1_{k}", [P, HEADS, P]) for k in range(2)]
        prT = sb("prT1", [P, HEADS, P])
        ctxT = sb("ctxT1", [P, 2, P])
        n_zero, n_zs, n_qk_ready, n_qk, n_kp, n_v_ready, n_v = (sem(n) for n in (
            "n_zeroed", "n_z_staged", "n_qk_ready", "n_qk_scaled", "n_k_spread", "n_v_ready", "n_v_copied"))
        n_s_ready, n_s, n_mx, n_sub, n_exp, n_sum, n_rec, n_p0, n_p, n_tp_ready, n_tp, n_c_ready, n_c, n_o_ready, n_o = (
            sem(n) for n in ("n_s_ready", "n_s_masked", "n_max", "n_subtracted", "n_exp", "n_sum", "n_recip", "n_probs_half", "n_probs",
                             "n_trp_ready", "n_trp_copied", "n_ctx_ready", "n_ctx_copied", "n_out_ready", "n_out_added"))

        with nc.Block() as block:
            @block.sync
            def _(sp):
                load_adapter(sp, io, f_w, f_in)

            @block.gpsimd
            def _(pool):
                for t in v + pr:
                    pool.memset(t[:, :, :], 0.0).then_inc(n_zero, 1)
                pool.wait_ge(n_in, 112)

                def step(i, par):
                    if live(i - 2):
                        if isinstance(i, int) and i == 2:
                            pool.wait_ge(n_zero, 4)
                        wait(pool, n_tp_ready, 4 * (i - 3) + 4)
                        if live(i - 1):
                            pool.wait_ge(n_kp, i)
                        pool.wait_ge(n_rec, i - 1)
                        pool.tensor_tensor(pr[par][0:S, :, 0:S], ex[par][0:S, :, :], bcast(ri[0:S, :], 2, S),
                                           ALU.mult).then_inc(n_p0, 1)
                        pool.wait_ge(n_p0, i - 1)
                        pool.tensor_tensor(pr[par][S:P, :, S:P], ex[par][S:P, :, :], bcast(ri[S:P, :], 2, S),
                                           ALU.mult).then_inc(n_p, 1)
                        pool.wait_ge(n_p, i - 1)
                    if live(i):
                        wait(pool, n_s_ready, 4 * (i - 1))
                        pool.wait_ge(n_qk, i + 1)
                        for t in range(2):
                            last = pool.tensor_tensor(kpad[par][:, t, :, :], bcast(kT[par][:, t, :], 1, HT),
                                                      bcast(hm[:, :], 2, P), ALU.mult)
                        last.then_inc(n_kp, 1)

                pipeline(pool, step)

            @block.tensor
            def _(pe):
                pe.wait_ge(n_in, 112)

                def step(i, par):
                    if live(i - 1):
                        p = i - 1
                        pe.wait_ge(n_kp, p + 1)
                        for f in range(4):
                            if f == 2:
                                wait(pe, n_v, i - 1)
                                for k in range(KT):
                                    mm = pe.matmul(banks[2][:, 0:D], zs[1 - par][:, k, :], wat[:, k, 2 * D:3 * D], start=k == 0,
                                                   stop=k == KT - 1)
                                mm.then_inc(n_v_ready, 1)
                            wait(pe, n_s, 4 * p + f - 1)
                            pe.matmul(banks[4 + f % 2][:, :], qT[1 - par][:, f // 2, :],
                                      kpad[1 - par][:, f // 2, 4 * (f % 2):4 * (f % 2) + 4, :], start=True, stop=True).then_inc(n_s_ready, 1)
                    if live(i - 3):
                        p = i - 3
                        pe.wait_ge(n_c, p + 1)
                        wait(pe, n_o, p)
                        for o in range(KT):
                            for k in range(KT):
                                mm = pe.matmul(banks[0][:, o * P:(o + 1) * P], wp[:, k, o * P:(o + 1) * P], ctxT[:, k, :],
                                               start=k == 0, stop=k == KT - 1)
                        mm.then_inc(n_o_ready, 1)
                    if live(i + 1):
                        pe.wait_ge(n_zs, i + 2)
                        wait(pe, n_qk, i + 1)
                        for t in range(4):
                            for k in range(KT):
                                mm = pe.matmul(banks[1][:, t * P:(t + 1) * P], wat[:, k, t * P:(t + 1) * P], zs[1 - par][:, k, :],
                                               start=k == 0, stop=k == KT - 1)
                        mm.then_inc(n_qk_ready, 1)
                    if live(i - 2):
                        p = i - 2
                        pe.wait_ge(n_p, p + 1)
                        for f in range(4):
                            wait(pe, n_tp, 4 * p + f - 1)
                            for j in range(4):
                                mm = pe.transpose(banks[6 + f % 2][:, j * P:(j + 1) * P], pr[par][:, 4 * f + j, :], ident[:, :])
                            mm.then_inc(n_tp_ready, 1)
                    if live(i - 2):
                        p = i - 2
                        pe.wait_ge(n_tp, 4 * p + 4)
                        for t in range(2):
                            for q in range(4):
                                for s in range(2):
                                    h = 8 * t + 2 * q + s
                                    mm = pe.matmul(banks[3][32 * q:32 * q + 32, t * P:(t + 1) * P], v[par][:, h, :],
                                                   prT[:, h, :], start=s == 0, stop=s == 1)
                        mm.then_inc(n_c_ready, 1)

                pipeline(pe, step)

            @block.scalar
            def _(act):
                def step(i, par):
                    if live(i + 1):
                        wait(act, n_v_ready, i)
                        act.activation(zs[1 - par][:, :, :], zT[:, :, bass.ds((i + 1) * P, P)], ACT.Copy).then_inc(n_zs, 1)
                    if live(i - 2):
                        p = i - 2
                        for f in range(4):
                            act.wait_ge(n_tp_ready, 4 * p + f + 1)
                            act.activation(prT[:, 4 * f:4 * f + 4, :], banks[6 + f % 2][:, :].rearrange(
                                "p (t n) -> p t n", n=P), ACT.Copy).then_inc(n_tp, 1)
                    if live(i - 1):
                        act.wait_ge(n_sub, i)
                        wait(act, n_p, i - 2)
                        act.activation(ex[1 - par][:, :, :], sc[:, :, :], ACT.Exp).then_inc(n_exp, 1)
                    if live(i - 2):
                        act.wait_ge(n_c_ready, i - 1)
                        act.activation(ctxT[:, :, :], banks[3][:, 0:2 * P].rearrange("p (t n) -> p t n", n=P),
                                       ACT.Copy).then_inc(n_c, 1)

                pipeline(act, step)

            @block.vector
            def _(dve):
                dve.wait_ge(n_in, 112)

                def step(i, par):
                    if live(i - 2):
                        p = i - 2
                        dve.wait_ge(n_exp, p + 1)
                        wait(dve, n_p, p)
                        dve.tensor_reduce(sm[:, :], ex[par][:, :, :], AX.X, ALU.add).then_inc(n_sum, 1)
                        dve.wait_ge(n_sum, p + 1)
                        dve.reciprocal(ri[:, :], sm[:, :]).then_inc(n_rec, 1)
                    if live(i - 1):
                        p = i - 1
                        wait(dve, n_exp, p)
                        for f in range(4):
                            dve.wait_ge(n_s_ready, 4 * p + f + 1)
                            for s in range(2):
                                rows = slice(S * s, S * s + S)
                                last = dve.tensor_tensor(
                                    sc[rows, 4 * f:4 * f + 4, :],
                                    banks[4 + f % 2][rows, :].rearrange("p (h n) -> p h n", n=P)[:, :, S * s:S * s + S],
                                    bcast(mask[rows, :], 1, 4), ALU.add)
                            last.then_inc(n_s, 1)
                        dve.wait_ge(n_s, 4 * p + 4)
                        dve.tensor_reduce(mx[:, :], sc[:, :, :], AX.X, ALU.max).then_inc(n_mx, 1)
                        dve.wait_ge(n_mx, p + 1)
                        dve.tensor_tensor(sc[:, :, :], sc[:, :, :], bcast(mx[:, :], 2, S), ALU.subtract).then_inc(n_sub, 1)
                    if live(i - 1):
                        dve.wait_ge(n_v_ready, i)
                        if isinstance(i, int) and i == 1:
                            dve.wait_ge(n_zero, 2)
                        for s in range(2):
                            vv = v[1 - par][:, s:HEADS:2, HD1 * s:HD1 * s + HD1]
                            last = dve.tensor_tensor(
                                vv, banks[2][:, 0:D].rearrange("p (h s d) -> p h s d", s=2, d=HD1)[:, :, s, :],
                                bv[:, :].rearrange("p (h s d) -> p h s d", s=2, d=HD1)[:, :, s, :], ALU.add)
                        last.then_inc(n_v, 1)
                    if live(i - 3):
                        p = i - 3
                        dve.wait_ge(n_o_ready, p + 1)
                        for o in range(KT):
                            at = xT[:, o, bass.ds(p * P, P)]
                            last = dve.scalar_tensor_tensor(at, banks[0][:, o * P:(o + 1) * P], bp[:, o:o + 1], at,
                                                            ALU.add, ALU.add)
                        last.then_inc(n_o, 1)
                    if live(i + 1):
                        dve.wait_ge(n_qk_ready, i + 2)
                        wait(dve, n_kp, i)
                        for t in range(4):
                            dst = (qT[1 - par] if t < 2 else kT[1 - par])[:, t % 2, :]
                            last = dve.scalar_tensor_tensor(
                                dst.rearrange("p (s n) -> p s n", s=2),
                                banks[1][:, t * P:(t + 1) * P].rearrange("p (s n) -> p s n", s=2), bat[:, t:t + 1],
                                bcast(fac[:, t // 2, :], 1, 2), ALU.add, ALU.mult)
                        last.then_inc(n_qk, 1)

                pipeline(dve, step)


def adapter_tensors(sb, sem, c):
    w = {n: sb("f_" + n, s, F32, c) for n, s in dict(
        w1=[P, KT, LANG * A2], b1=[P, LT], w2=[P, LT, D], tab=[LANG, 3, D],
        wt=[P, KT, D], vr=[32, D], ct=[32, D], fb=[P, KT], ones=[P, P]).items()}
    return w, sem("f_in")


def load_adapter(sp, io, w, f_in):
    for n, name in (("b1", "f_b1"), ("vr", "f_vrT"), ("ct", "f_cT"), ("fb", "f_b"), ("ones", "f_ones")):
        sp.dma_start(w[n][:, :], io[name]).then_inc(f_in, 16)
    sp.dma_start(w["tab"][:, :, :], io["f_tab"]).then_inc(f_in, 16)
    for n, name in (("w1", "f_w1"), ("w2", "f_w2"), ("wt", "f_wT")):
        sp.dma_start(w[n][:, :, :], io[name].rearrange("(k p) n -> p k n", p=P)).then_inc(f_in, 16)


def adapter_ffn(nc, io, banks, sb0, sem, xT, oh_lang, oh_lang10, out, w, f_in):
    with ExitStack() as c:
        def sb(name, shape, dt=F32):
            return sb0(name, shape, dt, c)

        def halves(name, shape):
            return [sb(f"f_{name}_{part}", shape, F32R) for part in ("hi", "lo")]

        FB = 256
        NB = N // FB
        BS = FB // S
        b1, w2, tab, wt, vr, ct, fb, ones = (w[n] for n in ("b1", "w2", "tab", "wt", "vr", "ct", "fb", "ones"))
        ones_r = sb("f_ones_r", [P, P], F32R)
        w1_2, w2_2, wt_2 = (halves(n, list(w[n].shape)) for n in ("w1", "w2", "wt"))
        ps = sb("f_ps", [P, 3, KT, B])
        x2 = [halves(f"x{k}", [P, KT, FB]) for k in range(2)]
        h = [sb(f"f_h{k}", [P, FB]) for k in range(LT)]
        h2 = [halves(f"h{k}", [P, FB]) for k in range(LT)]
        xb = sb("f_xb", [P, KT, FB])
        r = [sb(f"f_r{k}", [P, KT, FB]) for k in range(2)]
        nm = [sb(f"f_n{k}", [P, KT, FB]) for k in range(2)]
        r2 = halves("r", [P, KT, FB])
        n2 = halves("n", [P, KT, FB])
        sq = sb("f_sq", [P, KT, FB])
        sd = sb("f_sd", [P, FB])

        (f_t_ready, f_t, f_w_ready, f_w, f_whi, f_wlo, f_xh, f_xl, f_h_ready, f_h, f_hm, f_hh, f_hl, f_xb) = (
            sem(n) for n in ("f_tables_ready", "f_tables", "f_fold_ready", "f_folded", "f_weights_hi", "f_weights_lo",
                             "f_x_hi", "f_x_lo", "f_h_ready", "f_relu", "f_masked", "f_hidden_hi", "f_hidden_lo",
                             "f_x_plus_b2"))
        (f_a_ready, f_r, f_rh, f_rl, f_m_ready, f_c, f_sq, f_v_ready, f_var, f_sd, f_rs, f_n, f_g, f_be, f_nh, f_nl,
         f_o_ready, f_o, f_st) = (sem(n) for n in (
             "f_adapter_ready", "f_residual", "f_residual_hi", "f_residual_lo", "f_mean_ready", "f_centred",
             "f_squared", "f_var_ready", "f_var_eps", "f_std", "f_rstd", "f_normed", "f_scaled", "f_shifted", "f_n_hi",
             "f_n_lo", "f_out_ready", "f_out_added", "f_stored"))

        def steps(eng, step):
            for i in range(4):
                step(i, i % 2)
            with eng.Fori(2, NB // 2) as t:
                for par in range(2):
                    step(t * 2 + par, par)
            for i in range(NB, NB + 3):
                step(i, i % 2)

        def on(i):
            return not isinstance(i, int) or 0 <= i < NB

        def tokens(i):
            return bass.ds(i * FB, FB)

        def by(ap):
            return ap.rearrange("p k (b n) -> p k b n", n=S)

        def of(what, i):
            return bcast(ps[:, what, :, bass.ds(i * BS, BS)], 3, S)

        def both(bank):
            return bank[:, :].rearrange("p (k n) -> p k n", k=KT)

        with nc.Block() as block:
            @block.sync
            def _(sp):
                def step(i, par):
                    if on(i - 3):
                        sp.wait_ge(f_o, i - 2)
                        sp.dma_start(out[:, tokens(i - 3)].rearrange("(k p) n -> p k n", p=P),
                                     xT[:, :, tokens(i - 3)]).then_inc(f_st, 16)

                steps(sp, step)
                sp.wait_ge(f_st, 16 * NB)

            @block.tensor
            def _(pe):
                pe.wait_ge(f_in, 144)
                for k in range(KT):
                    mm = pe.matmul(banks[7][:, k * D:(k + 1) * D], vr[:, k * P:(k + 1) * P], ct[:, :], start=True, stop=True)
                mm.then_inc(f_w_ready, 1)
                for what in range(3):
                    for k in range(KT):
                        at = (what * KT + k) * B
                        mm = pe.matmul(banks[6][:, at:at + B], tab[:, what, k * P:(k + 1) * P], oh_lang10[:, :],
                                       start=True, stop=True)
                mm.then_inc(f_t_ready, 1)

                def hidden(i, par, j):
                    wait(pe, f_h, LT * i + (j - 1))
                    for k in range(KT):
                        mm = mm3(pe, banks[(LT * par + j) % 2][:, 0:FB], [t[:, k, j * P:(j + 1) * P] for t in w1_2],
                                 [t[:, k, :] for t in x2[par]], k == 0, k == KT - 1)
                    mm.then_inc(f_h_ready, 1)

                def adapter(i, par, o):
                    for j in range(LT):
                        if o == 0:
                            pe.wait_ge(f_hl, LT * i + (j + 1))
                        mm = mm3(pe, banks[2 + par][:, o * FB:(o + 1) * FB], [t[:, j, o * P:(o + 1) * P] for t in w2_2],
                                 [t[:, :] for t in h2[j]], j == 0, j == LT - 1)
                    if o == KT - 1:
                        mm.then_inc(f_a_ready, 1)

                def step(i, par):
                    if on(i):
                        if isinstance(i, int) and i == 0:
                            pe.wait_ge(f_wlo, 1)
                        pe.wait_ge(f_xl, i + 1)
                        for j in range(LT):
                            hidden(i, par, j)
                    if on(i - 1):
                        pe.wait_ge(f_rl, i)
                        for k in range(KT):
                            for part in range(2):
                                mm = pe.matmul(banks[4][:, 0:FB], ones_r[:, :], r2[part][:, k, :], start=k + part == 0,
                                               stop=k == KT - 1 and part == 1)
                        mm.then_inc(f_m_ready, 1)
                    if on(i - 3):
                        pe.wait_ge(f_nl, i - 2)
                        if isinstance(i, int) and i < 5:
                            pe.wait_ge(f_t, 1)
                            pe.wait_ge(f_wlo, 3)
                        wait(pe, f_o, i - 4)
                        for o in range(KT):
                            for k in range(KT):
                                mm = mm3(pe, banks[7 - par][:, o * FB:(o + 1) * FB], [t[:, k, o * P:(o + 1) * P] for t in wt_2],
                                         [t[:, k, :] for t in n2], k == 0, k == KT - 1)
                        mm.then_inc(f_o_ready, 1)
                    if on(i):
                        if isinstance(i, int) and i == 0:
                            pe.wait_ge(f_wlo, 2)
                        wait(pe, f_r, i - 1)
                        adapter(i, par, 0)
                    if on(i - 1):
                        pe.wait_ge(f_sq, i)
                        for k in range(KT):
                            mm = pe.matmul(banks[5][:, 0:FB], ones[:, :], sq[:, k, :], start=k == 0, stop=k == KT - 1)
                        mm.then_inc(f_v_ready, 1)
                    if on(i):
                        adapter(i, par, 1)

                steps(pe, step)

            @block.scalar
            def _(act):
                act.wait_ge(f_in, 144)

                def x_hi(i, par):
                    wait(act, f_a_ready, i - 1)
                    act.activation(x2[par][0][:, :, :], xT[:, :, tokens(i)], ACT.Copy).then_inc(f_xh, 1)

                x_hi(0, 0)
                act.activation(w1_2[0][:, :, :], w["w1"][:, :, :], ACT.Copy).then_inc(f_whi, 1)
                act.activation(w2_2[0][:, :, :], w2[:, :, :], ACT.Copy).then_inc(f_whi, 1)
                act.activation(ones_r[:, :], ones[:, :], ACT.Copy)
                act.wait_ge(f_w, 1)
                act.activation(wt_2[0][:, :, :], wt[:, :, :], ACT.Copy).then_inc(f_whi, 1)

                def relu(i, j, par):
                    act.wait_ge(f_h_ready, LT * i + (j + 1))
                    act.activation(h[j][:, :], banks[(LT * par + j) % 2][:, 0:FB], ACT.Relu,
                                   bias=b1[:, j:j + 1]).then_inc(f_h, 1)

                def h_hi(i, j):
                    act.wait_ge(f_hm, LT * i + (j + 1))
                    act.activation(h2[j][0][:, :], h[j][:, :], ACT.Copy).then_inc(f_hh, 1)

                def step(i, par):
                    if on(i):
                        relu(i, 0, par)
                        relu(i, 1, par)
                        h_hi(i, 0)
                    if on(i - 1):
                        act.wait_ge(f_r, i)
                        wait(act, f_m_ready, i - 1)
                        act.activation(r2[0][:, :, :], r[1 - par][:, :, :], ACT.Copy).then_inc(f_rh, 1)
                    if on(i):
                        for j in range(2, LT):
                            relu(i, j, par)
                            h_hi(i, j - 1)
                    if on(i - 1):
                        act.wait_ge(f_c, i)
                        wait(act, f_v_ready, i - 1)
                        act.activation(sq[:, :, :], r[1 - par][:, :, :], ACT.Square).then_inc(f_sq, 1)
                    if on(i):
                        h_hi(i, LT - 1)
                        if on(i + 1):
                            x_hi(i + 1, 1 - par)
                    if on(i - 1):
                        act.wait_ge(f_var, i)
                        act.activation(sd[:, :], sd[:, :], ACT.Sqrt).then_inc(f_sd, 1)
                    if on(i - 2):
                        act.wait_ge(f_be, i - 1)
                        wait(act, f_o_ready, i - 2)
                        act.activation(n2[0][:, :, :], nm[par][:, :, :], ACT.Copy).then_inc(f_nh, 1)

                steps(act, step)

            @block.gpsimd
            def _(pool):
                def x_lo(i, par):
                    pool.wait_ge(f_xh, i + 1)
                    pool.tensor_tensor(x2[par][1][:, :, :], xT[:, :, tokens(i)], x2[par][0][:, :, :].bitcast(F32),
                                       ALU.subtract).then_inc(f_xl, 1)

                def mask(i, j):
                    pool.wait_ge(f_h, LT * i + (j + 1))
                    hj = h[j][:, :].rearrange("p (b n) -> p b n", n=S)
                    pool.tensor_tensor(hj, hj, bcast(oh_lang[:, j, bass.ds(i * BS, BS)], 2, S), ALU.mult).then_inc(f_hm, 1)

                def step(i, par):
                    if on(i):
                        for j in range(LT):
                            mask(i, j)
                    if on(i - 2):
                        at = by(nm[par][:, :, :])
                        pool.wait_ge(f_n, i - 1)
                        pool.tensor_tensor(at, at, of(1, i - 2), ALU.mult).then_inc(f_g, 1)
                        pool.wait_ge(f_g, i - 1)
                        pool.tensor_tensor(at, at, of(2, i - 2), ALU.add).then_inc(f_be, 1)
                    if on(i):
                        wait(pool, f_r, i)
                        if isinstance(i, int) and i == 0:
                            pool.wait_ge(f_t, 1)
                        pool.tensor_tensor(by(xb[:, :, :]), by(xT[:, :, tokens(i)]), of(0, i), ALU.add).then_inc(f_xb, 1)
                        if on(i + 1):
                            x_lo(i + 1, 1 - par)

                x_lo(0, 0)
                steps(pool, step)

            @block.vector
            def _(dve):
                def lo(dst, src, hi, done):
                    dve.tensor_tensor(dst, src, hi.bitcast(F32), ALU.subtract).then_inc(done, 1)

                dve.wait_ge(f_in, 144)
                dve.wait_ge(f_whi, 1)
                lo(w1_2[1][:, :, :], w["w1"][:, :, :], w1_2[0][:, :, :], f_wlo)
                dve.wait_ge(f_w_ready, 1)
                dve.tensor_tensor(wt[:, :, :], banks[7][:, :].rearrange("p (k n) -> p k n", k=KT), wt[:, :, :],
                                  ALU.add).then_inc(f_w, 1)
                dve.wait_ge(f_t_ready, 1)
                dve.tensor_copy(ps[:, :, :, :], banks[6][:, 0:3 * KT * B].rearrange("p (w k b) -> p w k b", w=3, k=KT)).then_inc(f_t, 1)
                for n, (src, t) in enumerate(((w2, w2_2), (wt, wt_2))):
                    dve.wait_ge(f_whi, n + 2)
                    if src is wt:
                        dve.wait_ge(f_w, 1)
                    lo(t[1][:, :, :], src[:, :, :], t[0][:, :, :], f_wlo)

                def h_lo(i, j):
                    dve.wait_ge(f_hh, LT * i + (j + 1))
                    lo(h2[j][1][:, :], h[j][:, :], h2[j][0][:, :], f_hl)

                def step(i, par):
                    if on(i - 1):
                        dve.wait_ge(f_a_ready, i)
                        dve.wait_ge(f_xb, i)
                        wait(dve, f_n, i - 2)
                        dve.tensor_tensor(r[1 - par][:, :, :], both(banks[3 - par]), xb[:, :, :], ALU.add).then_inc(f_r, 1)
                    if on(i - 2):
                        dve.wait_ge(f_rs, i - 1)
                        wait(dve, f_nl, i - 3)
                        dve.tensor_tensor(nm[par][:, :, :], r[par][:, :, :], bcast(sd[:, :], 1, KT), ALU.mult).then_inc(f_n, 1)
                    if on(i - 1):
                        dve.wait_ge(f_rh, i)
                        lo(r2[1][:, :, :], r[1 - par][:, :, :], r2[0][:, :, :], f_rl)
                    if on(i):
                        h_lo(i, 0)
                    if on(i - 3):
                        dve.wait_ge(f_nh, i - 2)
                        lo(n2[1][:, :, :], nm[1 - par][:, :, :], n2[0][:, :, :], f_nl)
                    if on(i):
                        h_lo(i, 1)
                        h_lo(i, 2)
                    if on(i - 1):
                        at = r[1 - par][:, :, :]
                        dve.wait_ge(f_m_ready, i)
                        dve.wait_ge(f_rl, i)
                        dve.tensor_tensor(at, at, bcast(banks[4][:, 0:FB], 1, KT), ALU.subtract).then_inc(f_c, 1)
                    if on(i):
                        for j in range(3, LT):
                            h_lo(i, j)
                    if on(i - 3):
                        dve.wait_ge(f_o_ready, i - 2)
                        for k in range(KT):
                            at = xT[:, k, tokens(i - 3)]
                            last = dve.scalar_tensor_tensor(at, banks[7 - par][:, k * FB:(k + 1) * FB], fb[:, k:k + 1], at,
                                                            ALU.add, ALU.add)
                        last.then_inc(f_o, 1)
                    if on(i - 1):
                        dve.wait_ge(f_v_ready, i)
                        wait(dve, f_n, i - 1)
                        dve.tensor_scalar(sd[:, :], banks[5][:, 0:FB], EPS, None, ALU.add).then_inc(f_var, 1)
                        dve.wait_ge(f_sd, i)
                        dve.reciprocal(sd[:, :], sd[:, :]).then_inc(f_rs, 1)

                steps(dve, step)


def constants():
    f = np.float32
    pos = np.arange(S, dtype=f)
    half = HD0 // 2
    scale = f(10000.0) ** (f(2.0) * np.arange(half, dtype=f) / f(HD0))
    ang = (pos[:, None] / scale).astype(f)
    cos, sin = np.cos(ang), np.sin(ang)
    cs, sn = np.concatenate([cos, cos], 1), np.concatenate([-sin, sin], 1)
    rope = np.stack([cs / 8, sn / 8, cs, sn], 1).astype(f)
    theta = f(1.0) / f(10000.0) ** (f(2.0) * np.arange(HD1 // 2, dtype=f) / f(HD1))
    ang1 = np.arange(1, S + 1, dtype=f)[:, None] * theta
    ang1 = np.concatenate([ang1, ang1], 1)
    fac = (np.cos(ang1) + np.sin(ang1)).astype(f).T
    fac = np.tile(fac, (P // HD1, 1))
    p = np.arange(P)
    cols = np.zeros((P, 16), f)
    cols[:, 0] = p
    cols[:, 1] = p // RL
    for k in range(LT):
        cols[:, 2 + k] = (k * P + p) // A2
    q = np.arange(P)[:, None] % S
    low = np.arange(S)[None] <= q
    ar = lambda n: np.arange(n, dtype=f)
    return {
        "ident": np.eye(P, dtype=f),
        "mask0": np.where(low, 0.0, -1e10).astype(f),
        "mask1": np.where(low, 0.0, -3e38).astype(f),
        "cols": cols,
        "rope": np.tile(rope, (2, 1, 1)),
        "rt_es": np.broadcast_to(ar(E2)[:, None], (E2, B))[None],
        "rt_j8": np.broadcast_to(SLOTS * ar(B // SLOTS)[None], (E2, B // SLOTS))[None],
        "rt_ee": np.tril(np.ones((E2, E2), f), -1)[None],
        "rt_ll": np.tril(np.ones((B, B), f), -1)[None],
        "rt_q": ar(BLOCKS * SLOTS)[None],
        "rt_em": (B + ar(BLOCKS * SLOTS) % SLOTS)[None],
        "rt_sm": (ar(B)[None] - (B + ar(BLOCKS * SLOTS) % SLOTS)[:, None])[None],
        "rt_kk": ar(BLOCKS)[None],
        "n_fac": np.stack([fac / 4, fac], 1),
        "n_hm": (p[:, None] // HD1 == np.arange(P // HD1)[None]).astype(f),
        "f_ones": np.full((P, P), 1.0 / D, f),
    }


def layouts(i):
    T = lambda a: np.swapaxes(a, -1, -2)
    cols = lambda a: a.reshape(-1, P).T
    return {
        "xT": i["x"].reshape(N, D).T,
        "idx": np.stack([i["itok_B_0_7"], i["itok_B_0_2"], i["itok_B_0_8"]]),
        "c0_wT": T(i["L0_cond_weight"]), "c0_bias": i["L0_cond_bias"],
        "a0_wqkv": i["L0_attn_wqkv"], "a0_wo": i["L0_attn_wo"],
        **{f"c2_{n}": i[f"L0_cond2_{n}"] for n in ("Wi0", "Wi1", "Wo", "sWi0", "sWi1", "sWo", "g0", "g1")},
        "m_rwT": i["L0_ffn_router_weight"].T, "m_rb": i["L0_ffn_router_bias"],
        "m_guT": T(i["L0_ffn_gate_up_proj"]), "m_dnT": T(i["L0_ffn_down_proj"]),
        "m_gub": i["L0_ffn_gate_up_proj_bias"].reshape(EM, 2 * JT, P).transpose(2, 0, 1),
        "m_db": i["L0_ffn_down_proj_bias"],
        "l_wiT": i["L1_cond_wi"].T, "l_woT": i["L1_cond_wo"].T,
        "l_cia": i["L1_cond_common_wi_a"], "l_cibT": i["L1_cond_common_wi_b"].T,
        "l_coa": i["L1_cond_common_wo_a"], "l_cobT": i["L1_cond_common_wo_b"].T,
        "l_eiaT": i["L1_cond_experts_wi_a"].reshape(EL * RL, D).T,
        "l_eibT": T(i["L1_cond_experts_wi_b"]).reshape(EL * RL, FF),
        "l_eoaT": i["L1_cond_experts_wo_a"].reshape(EL * RL, FF).T,
        "l_eobT": T(i["L1_cond_experts_wo_b"]).reshape(EL * RL, D),
        "n_waT": i["L1_attn_W_attn"].T, "n_wpT": i["L1_attn_W_proj"].T,
        "n_bat": cols(i["L1_attn_b_attn"][:2 * D]), "n_bv": i["L1_attn_b_attn"][2 * D:], "n_bp": cols(i["L1_attn_b_proj"]),
        "f_w1": i["L1_cond2_W1"].transpose(1, 0, 2).reshape(D, LANG * A2), "f_b1": cols(i["L1_cond2_b1"].reshape(-1)),
        "f_w2": i["L1_cond2_W2"].reshape(LANG * A2, D),
        "f_tab": np.stack([i["L1_cond2_b2"], i["L1_cond2_gamma"], i["L1_cond2_beta"]], 1),
        "f_wT": i["L1_ffn_W"].T, "f_vrT": i["L1_ffn_V_r"].T, "f_cT": i["L1_ffn_C"].T, "f_b": cols(i["L1_ffn_b"]),
    }


def kernel(**inputs):
    import concourse.bacc as bacc
    from concourse.bass_utils import run_bass_kernel_spmd

    arrays = {n: np.ascontiguousarray(a) for n, a in {**layouts({k: np.asarray(v) for k, v in inputs.items()}),
                                                      **constants()}.items()}
    nc = bacc.Bacc("TRN2", target_bir_lowering=False, num_devices=1)
    io = {n: nc.dram_tensor(f"in_{n}", a.shape, mybir.dt.from_np(a.dtype), kind="ExternalInput").ap()
          for n, a in arrays.items()}
    out = nc.dram_tensor("outT", (D, N), F32, kind="ExternalOutput").ap()
    build_program(nc, io, out)
    r = run_bass_kernel_spmd(nc, [{f"in_{n}": a for n, a in arrays.items()}], core_ids=[0])
    return np.ascontiguousarray(r.results[0]["outT"].T).reshape(B, S, D)
```
